# Optimizing a Trainium2 kernel written in Bass

```python
import numpy as np
import jax
import jax.numpy as jnp

def _softmax(x, axis=-1):
    return jax.nn.softmax(x, axis=axis)

def _gelu(x):
    return jax.nn.gelu(x, approximate=True)

def _silu(x):
    return jax.nn.silu(x)

def _sigmoid(x):
    return jax.nn.sigmoid(x)

def _layernorm(x, axis=-1, eps=1e-05):
    m = jnp.mean(x, axis=axis, keepdims=True)
    v = jnp.var(x, axis=axis, keepdims=True)
    return (x - m) / jnp.sqrt(v + eps)

def _scatter_add(tgt, idx, src, axis=0):
    return tgt.at[idx].add(src)

def _segment_sum(src, seg, n):
    return jax.ops.segment_sum(src, seg, n)
kernel_name = 'mk_decoder_postln_d2_seqx_r8_4c7071'

def setup_inputs(seed: int=0):
    np.random.seed(seed)
    _w = jnp.asarray

    def _rec_inputs():
        import jax
        import jax.numpy as jnp
        _rk = jax.random.key(seed)
        x = -0.0005207 + 1.001 * jax.random.normal(jax.random.fold_in(_rk, 1), (8, 256, 128), jnp.float32)
        _lenS = 256 - jax.random.randint(jax.random.fold_in(_rk, 7), (8,), 0, max(1, 256 // 4) + 1, jnp.int32)
        _lenS2 = 512 - jax.random.randint(jax.random.fold_in(_rk, 8), (8,), 0, max(1, 512 // 4) + 1, jnp.int32)
        _ctx_1024P = jax.random.normal(jax.random.fold_in(_rk, 11), (8, 16, 128), jnp.float32)
        _ctx_1024c = jax.random.dirichlet(jax.random.fold_in(_rk, 511), 0.3 * jnp.ones((16,), jnp.float32), (8, 512))
        _ctx_1024t = jnp.einsum('bsk,bkd->bsd', _ctx_1024c, _ctx_1024P)
        _ctx_1024t = _ctx_1024t * jax.lax.rsqrt(jnp.mean(jnp.square(_ctx_1024t)) + 1e-12) * 0.953939
        ctx_1024 = -1.52775e-05 + 0.999936 * (_ctx_1024t + 0.3 * jax.random.normal(jax.random.fold_in(_rk, 611), (8, 512, 128), jnp.float32))
        _validS = jnp.arange(256)[None, :] < _lenS[:, None]
        _validS2 = jnp.arange(512)[None, :] < _lenS2[:, None]
        _causal = jnp.tril(jnp.ones((256, 256), dtype=bool))
        mask_BxS2_ff1 = jnp.where(jnp.ones((8, 512), dtype=bool), 1.0, 0.0).astype(jnp.float32)
        return (x, ctx_1024, mask_BxS2_ff1)
    x, ctx_1024, mask_BxS2_ff1 = _rec_inputs()

    def _L0_attn_setup():
        import jax, jax.numpy as jnp
        import numpy as np
        N_HEADS = 16
        LOCAL_WINDOW = 64
        MAX_REL_DIST = 128
        NEG_INF = jnp.float32(-1e+30)
        key = jax.random.key(seed)
        ks = jax.random.split(key, 5)
        B, T, C = (2, 256, 128)
        x = jax.random.normal(ks[0], (B, T, C), dtype=jnp.float32)
        w_qkv = jax.random.normal(ks[1], (3 * C, C), dtype=jnp.float32) * 0.02
        w_proj = jax.random.normal(ks[2], (C, C), dtype=jnp.float32) * 0.02
        b_proj = jax.random.normal(ks[3], (C,), dtype=jnp.float32) * 0.02
        rel_bias = jax.random.normal(ks[4], (2 * MAX_REL_DIST + 1, N_HEADS), dtype=jnp.float32) * 0.02
        return {'x': x, 'w_qkv': w_qkv, 'w_proj': w_proj, 'b_proj': b_proj, 'rel_bias': rel_bias}
    _L0_attn_all = _L0_attn_setup()
    _L0_attn_in = {k: v for k, v in _L0_attn_all.items() if k in ('w_qkv', 'w_proj', 'b_proj', 'rel_bias')}
    del _L0_attn_all

    def _L0_xattn_setup():
        import jax, jax.numpy as jnp
        import numpy as np
        DIM = 128
        HEADS = 16
        DHEAD = 64
        INNER = HEADS * DHEAD
        EPS = 1e-05

        def layer_norm(x, g, b):
            mu = jnp.mean(x, axis=-1, keepdims=True)
            var = jnp.mean(jnp.square(x - mu), axis=-1, keepdims=True)
            return (x - mu) * jax.lax.rsqrt(var + EPS) * g + b

        def apply_rope(x, cos, sin):
            d2 = x.shape[-1] // 2
            x1, x2 = (x[..., :d2], x[..., d2:])
            return jnp.concatenate([x1 * cos - x2 * sin, x2 * cos + x1 * sin], axis=-1)
        key = jax.random.key(seed)
        ks = jax.random.split(key, 10)
        B, N, S = (8, 32, 512)
        latents = jax.random.normal(ks[0], (B, N, DIM), dtype=jnp.float32)
        context = jax.random.normal(ks[1], (B, S, DIM), dtype=jnp.float32)
        cos = jax.random.uniform(ks[2], (S, DHEAD // 2), dtype=jnp.float32)
        sin = jax.random.uniform(ks[3], (S, DHEAD // 2), dtype=jnp.float32)
        init = lambda k, shp, fan_in: jax.random.normal(k, shp, dtype=jnp.float32) / np.sqrt(fan_in)
        return {'latents': latents, 'context': context, 'cos': cos, 'sin': sin, 'ln_lat_g': jnp.ones((DIM,), jnp.float32), 'ln_lat_b': jnp.zeros((DIM,), jnp.float32), 'ln_ctx_g': jnp.ones((DIM,), jnp.float32), 'ln_ctx_b': jnp.zeros((DIM,), jnp.float32), 'Wq': init(ks[4], (DIM, INNER), DIM), 'Wkv': init(ks[5], (DIM, 2 * INNER), DIM), 'Wo': init(ks[6], (INNER, DIM), INNER), 'bo': jnp.zeros((DIM,), jnp.float32)}
    _L0_xattn_all = _L0_xattn_setup()
    _L0_xattn_in = {k: v for k, v in _L0_xattn_all.items() if k in ('cos', 'sin', 'ln_lat_g', 'ln_lat_b', 'ln_ctx_g', 'ln_ctx_b', 'Wq', 'Wkv', 'Wo', 'bo')}
    del _L0_xattn_all

    def _L0_ffn_setup():
        import jax, jax.numpy as jnp
        import numpy as np
        LN_EPS = 0.001
        EPS = 1e-05
        QB = 128.0

        def ste_round(x):
            return x + jax.lax.stop_gradient(jnp.round(x) - x)
        key = jax.random.key(seed)
        k1, k2 = jax.random.split(key)
        x = jax.random.normal(k1, (4, 1024, 128), dtype=jnp.float32)
        weight = jax.random.normal(k2, (128, 128), dtype=jnp.float32) * 0.02
        ln_gamma = jnp.ones((128,), dtype=jnp.float32)
        ln_beta = jnp.zeros((128,), dtype=jnp.float32)
        return {'x': x, 'weight': weight, 'ln_gamma': ln_gamma, 'ln_beta': ln_beta}
    _L0_ffn_all = _L0_ffn_setup()
    _L0_ffn_in = {k: v for k, v in _L0_ffn_all.items() if k in ('weight', 'ln_gamma', 'ln_beta')}
    del _L0_ffn_all

    def _L1_attn_setup():
        import jax, jax.numpy as jnp
        import numpy as np
        D_MODEL = 128
        D_STATE = 128
        BATCH = 8
        SEQ = 512
        key = jax.random.key(seed)
        ks = jax.random.split(key, 10)
        s = 0.1
        return {'x': jax.random.normal(ks[0], (BATCH, SEQ, D_MODEL), dtype=jnp.float32), 'Wi': jax.random.normal(ks[1], (D_STATE, D_MODEL), dtype=jnp.float32) * 0.02, 'bi': jnp.zeros((D_STATE,), dtype=jnp.float32), 'Ws': jax.random.normal(ks[2], (D_STATE, D_MODEL), dtype=jnp.float32) * 0.02, 'bs': jnp.zeros((D_STATE,), dtype=jnp.float32), 'Wo': jax.random.normal(ks[3], (D_MODEL, D_STATE), dtype=jnp.float32) * 0.02, 'bo': jnp.zeros((D_MODEL,), dtype=jnp.float32), 'A': jax.random.normal(ks[4], (D_STATE, D_STATE), dtype=jnp.float32) * s, 'B': jax.random.normal(ks[5], (D_STATE, D_STATE), dtype=jnp.float32) * s, 'C': jax.random.normal(ks[6], (D_STATE, D_STATE), dtype=jnp.float32) * s}
    _L1_attn_all = _L1_attn_setup()
    _L1_attn_in = {k: v for k, v in _L1_attn_all.items() if k in ('Wi', 'bi', 'Ws', 'bs', 'Wo', 'bo', 'A', 'B', 'C')}
    del _L1_attn_all

    def _L1_xattn_setup():
        import jax, jax.numpy as jnp
        import numpy as np
        D_MODEL = 128
        HEADS = 16
        DEPTH = D_MODEL // HEADS
        B, S = (4, 512)
        EPS_K = 1e-06
        EPS_LN = 1e-06

        def _layernorm(x, g, b):
            m = jnp.mean(x, axis=-1, keepdims=True)
            var = jnp.var(x, axis=-1, keepdims=True)
            return (x - m) * jax.lax.rsqrt(var + EPS_LN) * g + b

        def _split_heads(x):
            bsz, sl, _ = x.shape
            return x.reshape(bsz, sl, HEADS, DEPTH).transpose(0, 2, 1, 3)
        key = jax.random.key(seed)
        ks = jax.random.split(key, 8)
        lecun = 1.0 / np.sqrt(D_MODEL)
        glorot = np.sqrt(2.0 / (D_MODEL + D_MODEL))
        return {'q': jax.random.normal(ks[0], (B, S, D_MODEL), jnp.float32), 'k': jax.random.normal(ks[1], (B, S, D_MODEL), jnp.float32), 'v': jax.random.normal(ks[2], (B, S, D_MODEL), jnp.float32), 'mask': jnp.ones((B, S), jnp.float32), 'wq': jax.random.normal(ks[3], (D_MODEL, D_MODEL), jnp.float32) * lecun, 'wk': jax.random.normal(ks[4], (D_MODEL, D_MODEL), jnp.float32) * lecun, 'wv': jax.random.normal(ks[5], (D_MODEL, D_MODEL), jnp.float32) * lecun, 'ln_gamma': jnp.ones((D_MODEL,), jnp.float32), 'ln_beta': jnp.zeros((D_MODEL,), jnp.float32), 'dense_w': jax.random.normal(ks[6], (D_MODEL, D_MODEL), jnp.float32) * glorot, 'dense_b': jnp.zeros((D_MODEL,), jnp.float32)}
    _L1_xattn_all = _L1_xattn_setup()
    _L1_xattn_in = {k: v for k, v in _L1_xattn_all.items() if k in ('wq', 'wk', 'wv', 'ln_gamma', 'ln_beta', 'dense_w', 'dense_b')}
    del _L1_xattn_all

    def _L1_ffn_setup():
        import jax, jax.numpy as jnp
        import numpy as np
        FP8_E4M3_MAX = 448.0

        def fake_quant_fp8(t):
            amax = jnp.max(jnp.abs(t))
            scale = FP8_E4M3_MAX / jnp.maximum(amax, 1e-12)
            q = (t * scale).astype(jnp.float8_e4m3fn).astype(jnp.float32)
            return q / scale
        key = jax.random.key(seed)
        k1, k2, k3 = jax.random.split(key, 3)
        d_in, d_out = (128, 128)
        x = jax.random.normal(k1, (4, 1024, d_in), dtype=jnp.float32)
        weight = jax.random.normal(k2, (d_out, d_in), dtype=jnp.float32) * (1.0 / np.sqrt(d_in))
        bias = jax.random.normal(k3, (d_out,), dtype=jnp.float32) * 0.01
        return {'x': x, 'weight': weight, 'bias': bias}
    _L1_ffn_all = _L1_ffn_setup()
    _L1_ffn_in = {k: v for k, v in _L1_ffn_all.items() if k in ('weight', 'bias')}
    del _L1_ffn_all
    return {'x': x, 'ctx_1024': ctx_1024, 'mask_BxS2_ff1': mask_BxS2_ff1, 'L0_attn_w_qkv': _L0_attn_in['w_qkv'], 'L0_attn_w_proj': _L0_attn_in['w_proj'], 'L0_attn_b_proj': _L0_attn_in['b_proj'], 'L0_attn_rel_bias': _L0_attn_in['rel_bias'], 'L0_xattn_cos': _L0_xattn_in['cos'], 'L0_xattn_sin': _L0_xattn_in['sin'], 'L0_xattn_ln_lat_g': _L0_xattn_in['ln_lat_g'], 'L0_xattn_ln_lat_b': _L0_xattn_in['ln_lat_b'], 'L0_xattn_ln_ctx_g': _L0_xattn_in['ln_ctx_g'], 'L0_xattn_ln_ctx_b': _L0_xattn_in['ln_ctx_b'], 'L0_xattn_Wq': _L0_xattn_in['Wq'], 'L0_xattn_Wkv': _L0_xattn_in['Wkv'], 'L0_xattn_Wo': _L0_xattn_in['Wo'], 'L0_xattn_bo': _L0_xattn_in['bo'], 'L0_ffn_weight': _L0_ffn_in['weight'], 'L0_ffn_ln_gamma': _L0_ffn_in['ln_gamma'], 'L0_ffn_ln_beta': _L0_ffn_in['ln_beta'], 'L1_attn_Wi': _L1_attn_in['Wi'], 'L1_attn_bi': _L1_attn_in['bi'], 'L1_attn_Ws': _L1_attn_in['Ws'], 'L1_attn_bs': _L1_attn_in['bs'], 'L1_attn_Wo': _L1_attn_in['Wo'], 'L1_attn_bo': _L1_attn_in['bo'], 'L1_attn_A': _L1_attn_in['A'], 'L1_attn_B': _L1_attn_in['B'], 'L1_attn_C': _L1_attn_in['C'], 'L1_xattn_wq': _L1_xattn_in['wq'], 'L1_xattn_wk': _L1_xattn_in['wk'], 'L1_xattn_wv': _L1_xattn_in['wv'], 'L1_xattn_ln_gamma': _L1_xattn_in['ln_gamma'], 'L1_xattn_ln_beta': _L1_xattn_in['ln_beta'], 'L1_xattn_dense_w': _L1_xattn_in['dense_w'], 'L1_xattn_dense_b': _L1_xattn_in['dense_b'], 'L1_ffn_weight': _L1_ffn_in['weight'], 'L1_ffn_bias': _L1_ffn_in['bias']}

def reference(x, ctx_1024, mask_BxS2_ff1, L0_attn_w_qkv, L0_attn_w_proj, L0_attn_b_proj, L0_attn_rel_bias, L0_xattn_cos, L0_xattn_sin, L0_xattn_ln_lat_g, L0_xattn_ln_lat_b, L0_xattn_ln_ctx_g, L0_xattn_ln_ctx_b, L0_xattn_Wq, L0_xattn_Wkv, L0_xattn_Wo, L0_xattn_bo, L0_ffn_weight, L0_ffn_ln_gamma, L0_ffn_ln_beta, L1_attn_Wi, L1_attn_bi, L1_attn_Ws, L1_attn_bs, L1_attn_Wo, L1_attn_bo, L1_attn_A, L1_attn_B, L1_attn_C, L1_xattn_wq, L1_xattn_wk, L1_xattn_wv, L1_xattn_ln_gamma, L1_xattn_ln_beta, L1_xattn_dense_w, L1_xattn_dense_b, L1_ffn_weight, L1_ffn_bias):
    import jax
    import jax.numpy as jnp

    def _L0_attn_ref(x, w_qkv, w_proj, b_proj, rel_bias):
        import jax, jax.numpy as jnp
        import numpy as np
        N_HEADS = 16
        LOCAL_WINDOW = 64
        MAX_REL_DIST = 128
        NEG_INF = jnp.float32(-1e+30)
        B, T, C = x.shape
        H = N_HEADS
        hd = C // H
        scale = hd ** (-0.5)
        qkv = (x @ w_qkv.T).reshape(B, T, 3, H, hd).transpose(2, 0, 3, 1, 4)
        q, k, v = (qkv[0], qkv[1], qkv[2])
        attn = jnp.einsum('bhqd,bhkd->bhqk', q, k) * scale
        i = jnp.arange(T)[:, None]
        j = jnp.arange(T)[None, :]
        mask = (i >= j) & (jnp.abs(i - j) <= LOCAL_WINDOW)
        attn = jnp.where(mask[None, None], attn, NEG_INF)
        rel = jnp.clip(i - j, -MAX_REL_DIST, MAX_REL_DIST) + MAX_REL_DIST
        bias = rel_bias[rel].transpose(2, 0, 1)
        attn = attn + bias[None]
        attn = jax.nn.softmax(attn, axis=-1)
        y = jnp.einsum('bhqk,bhkd->bhqd', attn, v)
        y = y.transpose(0, 2, 1, 3).reshape(B, T, C)
        y = y @ w_proj.T + b_proj
        return y

    def _L0_xattn_ref(latents, context, cos, sin, ln_lat_g, ln_lat_b, ln_ctx_g, ln_ctx_b, Wq, Wkv, Wo, bo):
        import jax, jax.numpy as jnp
        import numpy as np
        DIM = 128
        HEADS = 16
        DHEAD = 64
        INNER = HEADS * DHEAD
        EPS = 1e-05

        def layer_norm(x, g, b):
            mu = jnp.mean(x, axis=-1, keepdims=True)
            var = jnp.mean(jnp.square(x - mu), axis=-1, keepdims=True)
            return (x - mu) * jax.lax.rsqrt(var + EPS) * g + b

        def apply_rope(x, cos, sin):
            d2 = x.shape[-1] // 2
            x1, x2 = (x[..., :d2], x[..., d2:])
            return jnp.concatenate([x1 * cos - x2 * sin, x2 * cos + x1 * sin], axis=-1)
        b, n, _ = latents.shape
        s = context.shape[1]
        lat = layer_norm(latents, ln_lat_g, ln_lat_b)
        ctx = layer_norm(context, ln_ctx_g, ln_ctx_b)
        q = (lat @ Wq).reshape(b, n, HEADS, DHEAD).transpose(0, 2, 1, 3)
        kv = ctx @ Wkv
        k, v = jnp.split(kv, 2, axis=-1)
        k = k.reshape(b, s, HEADS, DHEAD).transpose(0, 2, 1, 3)
        v = v.reshape(b, s, HEADS, DHEAD).transpose(0, 2, 1, 3)
        k = apply_rope(k, cos[None, None], sin[None, None])
        scale = DHEAD ** (-0.5)
        attn = jnp.einsum('bhnd,bhsd->bhns', q, k) * scale
        attn = jnp.clip(attn, -11.0, 11.0)
        attn = jax.nn.softmax(attn, axis=-1)
        out = jnp.einsum('bhns,bhsd->bhnd', attn, v)
        out = out.transpose(0, 2, 1, 3).reshape(b, n, INNER)
        return out @ Wo + bo

    def _L0_ffn_ref(x, weight, ln_gamma, ln_beta):
        import jax, jax.numpy as jnp
        import numpy as np
        LN_EPS = 0.001
        EPS = 1e-05
        QB = 128.0

        def ste_round(x):
            return x + jax.lax.stop_gradient(jnp.round(x) - x)
        mu = jnp.mean(x, axis=-1, keepdims=True)
        var = jnp.var(x, axis=-1, keepdims=True)
        xn = (x - mu) * jax.lax.rsqrt(var + LN_EPS) * ln_gamma + ln_beta
        beta = jnp.mean(jnp.abs(weight))
        w_q = jnp.clip(ste_round(weight / (beta + EPS)), -1.0, 1.0)
        gamma = jnp.max(jnp.abs(xn))
        xq = jnp.clip(xn * QB / gamma, -QB + EPS, QB - EPS)
        y = jnp.einsum('bsd,du->bsu', xq, w_q)
        return y * (gamma * beta / QB)

    def _L1_attn_ref(x, Wi, bi, Ws, bs, Wo, bo, A, B, C):
        import jax, jax.numpy as jnp
        import numpy as np
        D_MODEL = 128
        D_STATE = 128
        BATCH = 8
        SEQ = 512
        u = jnp.einsum('bsd,nd->bsn', x, Wi) + bi
        sp = jnp.einsum('bsd,nd->bsn', x, Ws) + bs

        def step(state, inp):
            u_t, sp_t = inp
            state = jnp.tanh(state @ A.T + u_t @ B.T) + sp_t
            y_t = state @ C.T
            return (state, y_t)
        state0 = jnp.zeros((x.shape[0], A.shape[0]), dtype=x.dtype)
        _, ys = jax.lax.scan(step, state0, (u.transpose(1, 0, 2), sp.transpose(1, 0, 2)))
        ys = ys.transpose(1, 0, 2)
        out = jnp.einsum('bsn,dn->bsd', ys, Wo) + bo
        return out

    def _L1_xattn_ref(q, k, v, mask, wq, wk, wv, ln_gamma, ln_beta, dense_w, dense_b):
        import jax, jax.numpy as jnp
        import numpy as np
        D_MODEL = 128
        HEADS = 16
        DEPTH = D_MODEL // HEADS
        B, S = (4, 512)
        EPS_K = 1e-06
        EPS_LN = 1e-06

        def _layernorm(x, g, b):
            m = jnp.mean(x, axis=-1, keepdims=True)
            var = jnp.var(x, axis=-1, keepdims=True)
            return (x - m) * jax.lax.rsqrt(var + EPS_LN) * g + b

        def _split_heads(x):
            bsz, sl, _ = x.shape
            return x.reshape(bsz, sl, HEADS, DEPTH).transpose(0, 2, 1, 3)
        bsz = q.shape[0]
        em = mask[:, None, :, None]
        qh = _split_heads(_layernorm(q @ wq, ln_gamma, ln_beta))
        kh = _split_heads(_layernorm(k @ wk, ln_gamma, ln_beta))
        vh = _split_heads(_layernorm(v @ wv, ln_gamma, ln_beta))
        q_prime = jax.nn.relu(qh) + EPS_K
        k_prime = (jax.nn.relu(kh) + EPS_K) * em
        vh = vh * em
        kv = jnp.einsum('bhnd,bhne->bhde', k_prime, vh)
        z = 1.0 / (jnp.einsum('bhnd,bhd->bhn', q_prime, k_prime.sum(axis=-2)) + EPS_K)
        att = jnp.einsum('bhnd,bhde,bhn->bhne', q_prime, kv, z)
        att = att.reshape(bsz, -1, D_MODEL)
        out = att @ dense_w + dense_b
        return _layernorm(out, ln_gamma, ln_beta)

    def _L1_ffn_ref(x, weight, bias):
        import jax, jax.numpy as jnp
        import numpy as np
        FP8_E4M3_MAX = 448.0

        def fake_quant_fp8(t):
            amax = jnp.max(jnp.abs(t))
            scale = FP8_E4M3_MAX / jnp.maximum(amax, 1e-12)
            q = (t * scale).astype(jnp.float8_e4m3fn).astype(jnp.float32)
            return q / scale
        xq = fake_quant_fp8(x)
        wq = fake_quant_fp8(weight)
        return jnp.einsum('bsd,od->bso', xq, wq) + bias
    x = _layernorm(x + _L0_attn_ref(x, L0_attn_w_qkv, L0_attn_w_proj, L0_attn_b_proj, L0_attn_rel_bias), axis=-1)
    x = _layernorm(x + _L0_xattn_ref(x, ctx_1024, L0_xattn_cos, L0_xattn_sin, L0_xattn_ln_lat_g, L0_xattn_ln_lat_b, L0_xattn_ln_ctx_g, L0_xattn_ln_ctx_b, L0_xattn_Wq, L0_xattn_Wkv, L0_xattn_Wo, L0_xattn_bo), axis=-1)
    x = _layernorm(x + _L0_ffn_ref(x, L0_ffn_weight, L0_ffn_ln_gamma, L0_ffn_ln_beta), axis=-1)
    x = _layernorm(x + _L1_attn_ref(x, L1_attn_Wi, L1_attn_bi, L1_attn_Ws, L1_attn_bs, L1_attn_Wo, L1_attn_bo, L1_attn_A, L1_attn_B, L1_attn_C), axis=-1)
    x = _layernorm(x + _L1_xattn_ref(x, ctx_1024, ctx_1024, mask_BxS2_ff1, L1_xattn_wq, L1_xattn_wk, L1_xattn_wv, L1_xattn_ln_gamma, L1_xattn_ln_beta, L1_xattn_dense_w, L1_xattn_dense_b), axis=-1)
    x = _layernorm(x + _L1_ffn_ref(x, L1_ffn_weight, L1_ffn_bias), axis=-1)
    return x

_drawn_inputs = setup_inputs


def setup_inputs(seed=0):
    import zlib

    import numpy as np

    out = dict(_drawn_inputs(seed))
    spreads = {'L0_xattn_ln_lat_g': (1.0, 0.544),
     'L0_xattn_ln_lat_b': (0.0, 0.408),
     'L0_xattn_ln_ctx_g': (1.0, 0.2),
     'L0_xattn_ln_ctx_b': (0.0, 0.1),
     'L0_xattn_bo': (0.0, 0.1),
     'L0_ffn_ln_gamma': (1.0, 0.2),
     'L0_ffn_ln_beta': (0.0, 0.348),
     'L1_attn_bi': (0.0, 0.1),
     'L1_attn_bs': (0.0, 0.1),
     'L1_attn_bo': (0.0, 0.1),
     'L1_xattn_ln_gamma': (1.0, 0.2),
     'L1_xattn_ln_beta': (0.0, 0.1),
     'L1_xattn_dense_b': (0.0, 0.1)}
    factors = {'L0_attn_w_qkv': 4.079,
     'L0_attn_w_proj': 3.986,
     'L0_attn_rel_bias': 8.0,
     'L0_xattn_cos': 3.289,
     'L0_xattn_sin': 3.284,
     'L1_ffn_bias': 8.0}
    for name, (base, spread) in spreads.items():
        noise = np.random.default_rng([zlib.crc32(name.encode()), seed]).standard_normal(out[name].shape)
        drawn = base * np.exp(spread * noise) if base else spread * noise
        out[name] = jnp.asarray(drawn.astype(out[name].dtype))
    for name, factor in factors.items():
        out[name] = (out[name] * factor).astype(out[name].dtype)
    return out
```

```python
from contextlib import ExitStack

import numpy as np

import concourse.bass as bass
from concourse import mybir

F32 = mybir.dt.float32
BF16 = mybir.dt.bfloat16
U32 = mybir.dt.uint32
ALU = mybir.AluOpType
ACT = mybir.ActivationFunctionType
AX_X = mybir.AxisListType.X

B, T, D = 8, 256, 128
S = 512
P = 128
QT = T // P
KB = S // P
NT = B * QT
H = 16
HD = D // H
G = 4
WINDOW = 64
MAX_REL = 128
DH = 64
HALF = DH // 2
PAIRS = H // 2
INNER = H * DH
CLIP = 11.0
MASKED = -1e30
BAND = WINDOW + P
SCRATCH = P - 1 + BAND
QB = 128.0
ROUND = 12582912.0
FP8_MAX = 448.0
FP8_MIN_NORMAL = 2.0 ** -6
FP8_ROUND = 1.5 * 2.0 ** 20
EPS_LN = 1e-5
EPSILONS = (EPS_LN, 1e-6, 1e-3)

ACT_JOBS = 31
DVE_JOBS = 26
NORMS = 6
SCORES = 12
HALVES = 2 * PAIRS
DVE_LINKS = 19
TAIL_A, TAIL_D, TAIL_NORMS = 3, 3, 2
TAIL_DVE_LINKS = 6
TAIL_POOL_LINKS = 2
STEPS = 5
POOL_LINKS = 30
SETUP_A = 1
SETUP_D = 3


def n(b, per, k):
    return b * per + k


class Chain:

    def __init__(self, eng, sem):
        self.eng, self.sem, self.base, self.k = eng, sem, 0, 0

    def start(self, base):
        self.base, self.k = base, 0

    def link(self, instruction):
        self.k += 1
        instruction.then_inc(self.sem, 1)
        self.eng.wait_ge(self.sem, self.base + self.k)


def rows(ap, parts, offset, dims):
    return bass.AP(tensor=ap.tensor, offset=ap.offset + offset, ap=[list(parts)] + [list(d) for d in dims])


def decoder(nc, a, out):
    with ExitStack() as ctx:
        def sb(name, shape, dt=F32):
            return ctx.enter_context(nc.sbuf_tensor(name, shape, dt))

        def sem(name):
            return ctx.enter_context(nc.semaphore(name))

        sc = ctx.enter_context(nc.psum_tensor("score_banks", [P, 4, 512], F32))
        cf = sc[:, :, :].rearrange("p k c -> p (k c)")
        ob = [ctx.enter_context(nc.psum_tensor(f"out_bank{i}", [P, 512], F32)) for i in range(2)]
        bank_a = ctx.enter_context(nc.psum_tensor("bank_a", [P, 512], F32))
        bank_d = ctx.enter_context(nc.psum_tensor("bank_d", [P, 512], F32))

        ident = sb("ident", [P, P])
        ones = sb("ones", [P, P])
        minus_half = sb("minus_half", [P, 8])
        epsilons = sb("epsilons", [P, 3, 8])
        head_mask = sb("head_mask", [P, H])
        quad_mask = sb("quad_mask", [P, G, P])
        bias_mask = sb("bias_mask", [P, H, BAND])
        w_qkv_t = sb("w_qkv_t", [P, 3 * D])
        w_proj_t = sb("w_proj_t", [P, D])
        wq = sb("wq", [P, INNER])
        wkv = sb("wkv", [P, 2 * INNER])
        wk_swap = sb("wk_swap", [P, INNER])
        wo = sb("wo", [P, PAIRS, D])
        cos_t = sb("cos_t", [P, S])
        sin_t = sb("sin_t", [P, S])
        w_l1kv = sb("w_l1kv", [P, 2 * D])
        w_l1q = sb("w_l1q", [P, D])
        w_dense = sb("w_dense", [P, D])
        keep = sb("keep", [P, B, KB])
        cols = sb("cols", [P, 9])
        LAT_G, LAT_B, CTX_G, CTX_B, FFN_G, FFN_B, BO_COL, BS_COL, BI_COL = range(9)
        b_proj = sb("b_proj", [P, D])
        b_wo = sb("b_wo", [P, D])
        l1_g = sb("l1_g", [P, D])
        l1_b = sb("l1_b", [P, D])
        b_dense = sb("b_dense", [P, D])
        b_ffn = sb("b_ffn", [P, D])

        xb = sb("xb", [P, QT, D])
        cb = sb("cb", [P, KB, D])
        x_t = sb("x_t", [P, T])
        q0 = sb("q0", [P, T])
        k0 = sb("k0", [P, T])
        vm = sb("vm", [P, QT, G, P])
        prob1 = sb("prob1", [P, H, T])
        row_max = sb("row_max", [P, QT, H])
        neg_max = sb("neg_max", [P, QT, H])
        row_sum = sb("row_sum", [P, QT, H])
        row_rec = sb("row_rec", [P, QT, H, HD])
        rec_t = sb("rec_t", [P, T])
        xbp = sb("xbp", [P, QT, D])
        x1 = sb("x1", [P, QT, D])
        x1p = sb("x1p", [P, QT, D])
        pt = sb("pt", [P, 4, 512])
        o0 = sb("o0", [P, T])
        ctx_t = sb("ctx_t", [P, S])
        cn = sb("cn", [P, KB, D])
        cn_t = sb("cn_t", [P, S])
        kv1 = sb("kv1", [P, 2 * KB, D])
        k1 = sb("k1", [P, KB, D])
        v1 = sb("v1", [P, KB, D + 1])
        stats = sb("stats", [P, 8, 6])
        mv = sb("mv", [P, 8, 2])
        var_eps = sb("var_eps", [P, 8])
        rstd = sb("rstd", [P, 8])
        y = sb("y", [P, QT, D])
        lat = sb("lat", [P, QT, D])
        lat_t = sb("lat_t", [P, T])
        qm = sb("qm", [P, PAIRS, 2, T])
        k_raw = sb("k_raw", [P, 2, S])
        k_sin = sb("k_sin", [P, 2, S])
        kr = sb("kr", [P, PAIRS, S])
        v = sb("v", [P, KB, INNER])
        prob = sb("prob", [P, 2, KB, 512])
        km = prob[:, :, :, :].rearrange("p i k (a t) -> p (i k a) t", t=T)
        psum = pt[:, 0:2, :]
        o_rec = sb("o_rec", [P, T])
        on = sb("on", [P, PAIRS, T])
        prob0 = on[:, :, :].rearrange("p k (a q) -> p (k a) q", q=P)

        x2 = sb("x2", [P, NT, D])
        f_all = sb("f_all", [P, NT, D])
        kv_sums = sb("kv_sums", [P, B, D + 1])

        mats = wq[:, :].rearrange("p (k d) -> p k d", d=D)
        M_WI, M_WS, M_WO, M_A, M_B, M_C, M_FFN0, M_FFN1 = range(8)
        f_t = v[:, 0:2, :].rearrange("p k c -> p (k c)")
        x3_t = v[:, 2:4, :].rearrange("p k c -> p (k c)")
        hid = kr[:, 0:4, :].rearrange("p k c -> p (k c)")
        x5 = kr[:, 4:8, :].rearrange("p k (t d) -> p (k t) d", d=D)
        tail = wkv[:, :].rearrange("p (k d) -> p k d", d=D)
        a_t, b_t, wo_t, bwi_t, aws_t, g_t, gws_t, w_round, kvm, ksm = (tail[:, k, :] for k in range(10))
        pre_t = wk_swap[:, 0:T]
        x4_t = wk_swap[:, T:2 * T]
        q1_t = wk_swap[:, 2 * T:3 * T]
        att_t = cn_t[:, :]
        den = ctx_t[:, 0:T]
        att = qm[:, 0:4].rearrange("p k a (i d) -> p (k a i) d", d=D)
        mixed = prob[:, 1, :, :].rearrange("p k (t d) -> p (k t) d", d=D)
        x4_all = f_all
        x4 = x1
        out_t = cn[:, :, :]
        q1 = lat
        one_row = sin_t[0:1, :]
        c_rows = rec_t[0:1, 0:2 * D]
        t4 = cn[:, :, :]
        t4b = cb[:, :, :]
        settled = sb("settled", [P, 32])
        small = sb("small", [P, 16])
        F_MAX, F_SUM, F_ALL, BETA, INV_BETA, F_INV, F_SCALE, OUT_BIAS, Q_MAX, Q_SCALE, Q_INV = 0, 4, 5, 6, 7, 8, 9, 10, 11, 13, 15
        diag2 = sb("diag2", [2, 4])
        level = f_all
        q8 = prob[:, 0, 0:2, :].bitcast(BF16).rearrange("p k (t d) -> p (k t) d", d=D)
        w8 = sb("w8", [P, 2, D], BF16)
        q8_t = sb("q8_t", [P, 512], BF16)
        ident16 = sb("ident16", [P, P], BF16)

        mats_in = sem("mats_in")
        ta_full = sem("ta_full")
        ta_free = sem("ta_free")
        td_full = sem("td_full")
        td_free = sem("td_free")
        f_quantized = sem("f_quantized")
        x3_ready = sem("x3_ready")
        prep_ready = sem("prep_ready")
        c_ready = sem("c_ready")
        z_ready = sem("z_ready")
        h_ready = sem("h_ready")
        x4_ready = sem("x4_ready")
        q1_ready = sem("q1_ready")
        kvm_ready = sem("kvm_ready")
        att_ready = sem("att_ready")
        att_out = sem("att_out")
        mixed_in = sem("mixed_in")
        red_ready = sem("red_ready")
        ident16_ready = sem("ident16_ready")
        q8_ready = sem("q8_ready")
        x5b_ready = sem("x5b_ready")
        out_ready = sem("out_ready")
        consts_made = sem("consts_made")
        weights_in = sem("weights_in")
        scratch_out = sem("scratch_out")
        bias_in = sem("bias_in")
        x_in = sem("x_in")
        ctx_in = sem("ctx_in")
        a_full = sem("a_full")
        a_free = sem("a_free")
        d_full = sem("d_full")
        d_free = sem("d_free")
        var_ready = sem("var_ready")
        rstd_ready = sem("rstd_ready")
        dve_chain = sem("dve_chain")
        pool_chain = sem("pool_chain")
        swap_ready = sem("swap_ready")
        trig_ready = sem("trig_ready")
        km_ready = sem("km_ready")
        cn_ready = sem("cn_ready")
        scores_full = sem("scores_full")
        scores_free = sem("scores_free")
        neg_ready = sem("neg_ready")
        exp0_done = sem("exp0_done")
        rec0_ready = sem("rec0_ready")
        o0_full = sem("o0_full")
        o0_ready = sem("o0_ready")
        lat_ready = sem("lat_ready")
        kr_ready = sem("kr_ready")
        half_full = sem("half_full")
        exp_done = sem("exp_done")
        clamped = sem("clamped")
        psum_ready = sem("psum_ready")
        o_full = sem("o_full")
        on_ready = sem("on_ready")
        xbp_ready = sem("xbp_ready")
        x1_ready = sem("x1_ready")
        x1p_ready = sem("x1p_ready")
        km_half_ready = sem("km_half_ready")
        k1_ready = sem("k1_ready")
        x2_ready = sem("x2_ready")
        out_done = sem("out_done")

        scratch = nc.dram_tensor("bias_scratch", [H, SCRATCH], F32).ap()

        att_dram = nc.dram_tensor("att_scratch", [B, T, D], F32).ap()

        rel = prob0[0:WINDOW + 1, 0, 0:H]
        rel_row = prob1[0:H, 8:10, :].rearrange("p a b -> p (a b)")[:, 0:SCRATCH]
        w_nat = prob1[:, 2:4, :].rearrange("p a (b c) -> p (a b) c", c=P)
        trig_nat = prob1[:, 6, :].rearrange("p (t k d) -> p t k d", t=2, k=KB)
        trig_rep = km[:, 0:4, :].rearrange("p (t a) (b r d) -> p t (a b) r d", t=2, b=2, r=4)

        block = ctx.enter_context(nc.Block())

        SETUP_LOADS = 28

        @block.sync
        def _(sp):
            loads = [0]

            def load(dst, src, slow=False):
                loads[0] += 1
                sp.dma_start(dst, src, allow_slow_non_contiguous=slow).then_inc(weights_in, 16)

            def col(name, k):
                load(cols[:, k:k + 1], a[name].rearrange("(p o) -> p o", o=1), slow=True)

            def row(name, dst):
                load(dst[:, :], rows(a[name], (0, P), 0, [(1, D)]))

            load(rel, a["L0_attn_rel_bias"][MAX_REL:MAX_REL + WINDOW + 1, :])
            load(w_nat[:, 0:3, :], a["L0_attn_w_qkv"].rearrange("(k p) c -> p k c", p=P))
            load(w_nat[:, 3, :], a["L0_attn_w_proj"])
            load(trig_nat[:, 0], a["L0_xattn_cos"].rearrange("(k p) d -> p k d", p=P))
            load(trig_nat[:, 1], a["L0_xattn_sin"].rearrange("(k p) d -> p k d", p=P))
            sp.dma_start(xb[:, :, :], a["x"][0].rearrange("(k p) d -> p k d", p=P)).then_inc(x_in, 16)
            sp.dma_start(cb[:, :, :], a["ctx_1024"][0].rearrange("(k p) d -> p k d", p=P)).then_inc(ctx_in, 16)
            load(w_l1kv[:, 0:D], a["L1_xattn_wk"])
            load(w_l1kv[:, D:2 * D], a["L1_xattn_wv"])
            load(wkv[:, :], a["L0_xattn_Wkv"])
            load(wq[:, :], a["L0_xattn_Wq"])
            load(wo[:, :, :], a["L0_xattn_Wo"].rearrange("(k p) d -> p k d", p=P))
            load(w_l1q[:, :], a["L1_xattn_wq"])
            load(w_dense[:, :], a["L1_xattn_dense_w"])
            load(keep[:, :, :], a["mask_BxS2_ff1"].rearrange("b (k p) -> p b k", p=P), slow=True)
            col("L0_xattn_ln_lat_g", LAT_G)
            col("L0_xattn_ln_lat_b", LAT_B)
            col("L0_xattn_ln_ctx_g", CTX_G)
            col("L0_xattn_ln_ctx_b", CTX_B)
            col("L0_ffn_ln_gamma", FFN_G)
            col("L0_ffn_ln_beta", FFN_B)
            col("L1_attn_bo", BO_COL)
            col("L1_attn_bs", BS_COL)
            col("L1_attn_bi", BI_COL)
            row("L0_attn_b_proj", b_proj)
            row("L0_xattn_bo", b_wo)
            row("L1_xattn_ln_gamma", l1_g)
            row("L1_xattn_ln_beta", l1_b)
            row("L1_xattn_dense_b", b_dense)
            row("L1_ffn_bias", b_ffn)
            assert loads[0] == SETUP_LOADS, loads
            sp.wait_ge(d_free, 2)
            sp.dma_start(scratch, rel_row).then_inc(scratch_out, 16)
            sp.wait_ge(scratch_out, 16)
            sp.dma_start(bias_mask[:, :, :], rows(scratch, (1, P), 0, [(SCRATCH, H), (1, BAND)])).then_inc(bias_in, 16)
            with sp.Fori(1, B) as b:
                sp.wait_ge(d_free, n(b - 1, DVE_JOBS, SETUP_D + 1))
                sp.dma_start(cb[:, :, :], a["ctx_1024"][b].rearrange("(k p) d -> p k d", p=P)).then_inc(ctx_in, 16)
                sp.wait_ge(d_free, n(b - 1, DVE_JOBS, SETUP_D + 20))
                sp.dma_start(xb[:, :, :], a["x"][b].rearrange("(k p) d -> p k d", p=P)).then_inc(x_in, 16)
            sp.wait_ge(d_full, SETUP_D + B * DVE_JOBS)
            for k, name in ((M_WI, "L1_attn_Wi"), (M_WS, "L1_attn_Ws"), (M_WO, "L1_attn_Wo"), (M_A, "L1_attn_A"),
                            (M_B, "L1_attn_B"), (M_C, "L1_attn_C"), (M_FFN0, "L0_ffn_weight"),
                            (M_FFN1, "L1_ffn_weight")):
                sp.dma_start(mats[:, k, :], a[name]).then_inc(mats_in, 16)
            per = P // H
            for b in range(B):
                sp.wait_ge(att_ready, b + 1)
                sp.dma_start(att_dram[b].rearrange("(q p) d -> p q d", p=P), att[:, b * QT:(b + 1) * QT, :]
                             ).then_inc(att_out, 16)
                sp.wait_ge(att_out, 16 * (b + 1))
                for q in range(QT):
                    for h in range(per):
                        sp.dma_start(mixed[H * h:H * (h + 1), b * QT + q, :].rearrange("m (i e) -> m i e", e=HD),
                                     rows(att_dram, (H * D, H), b * T * D + (q * per + h) * HD, [(D, H), (1, HD)])
                                     ).then_inc(mixed_in, 16)
            out_v = out.rearrange("b (q p) d -> p (b q) d", p=P)
            for k in range(4):
                sp.wait_ge(out_ready, k + 1)
                sp.dma_start(out_v[:, 4 * k:4 * k + 4, :], f_all[:, 4 * k:4 * k + 4, :]).then_inc(out_done, 16)
            sp.wait_ge(out_done, 64)

        @block.gpsimd
        def _(pool):
            chain = Chain(pool, pool_chain)
            link = chain.link
            g = nc.gpsimd
            g.memset(ones[:, :], 1.0)
            g.memset(minus_half[:, :], -0.5)
            for k, eps in enumerate(EPSILONS):
                g.memset(epsilons[:, k, :], eps)
            g.memset(ident[:, :], 0.0)
            g.memset(head_mask[:, :], 1.0)
            g.memset(quad_mask[:, :, :], 0.0)
            g.memset(qm[:, :, :, :], 0.0)
            link(g.memset(v1[:, :, D:D + 1], 1.0))
            g.affine_select(out=ident[:, :], in_=ident[:, :], compare_op=ALU.not_equal, fill=1.0, base=0,
                            pattern=[[-1, P]], channel_multiplier=1)
            for j in range(G):
                g.memset(quad_mask[:, j, :].rearrange("p (g j d) -> p g j d", g=G, j=G)[:, :, j, :], 1.0)
            link(g.affine_select(out=head_mask[:, :], in_=head_mask[:, :], compare_op=ALU.is_ge, fill=0.0, base=0,
                                 pattern=[[-HD, H]], channel_multiplier=1))
            g.affine_select(out=head_mask[:, :], in_=head_mask[:, :], compare_op=ALU.is_ge, fill=0.0, base=HD - 1,
                            pattern=[[HD, H]], channel_multiplier=-1).then_inc(consts_made, 1)
            pool.wait_ge(weights_in, 16 * SETUP_LOADS)
            half = wkv[:, 0:INNER].rearrange("c (h t d) -> c h t d", t=2, d=HALF)
            swap = wk_swap[:, :].rearrange("c (h t d) -> c h t d", t=2, d=HALF)
            g.tensor_scalar(swap[:, :, 0, :], half[:, :, 1, :], -1.0, None, ALU.mult)
            g.tensor_copy(swap[:, :, 1, :], half[:, :, 0, :]).then_inc(swap_ready, 1)

            def rstd_of(b, k, count, eps):
                pool.wait_ge(var_ready, n(b, NORMS, k + 1))
                link(g.tensor_tensor(var_eps[:, 0:count], mv[:, 0:count, 1],
                                     epsilons[:, EPSILONS.index(eps), 0:count], ALU.add))
                g.tensor_tensor(rstd[:, 0:count], var_eps[:, 0:count], minus_half[:, 0:count],
                                ALU.pow).then_inc(rstd_ready, 1)

            first = chain.k
            with pool.Fori(0, B) as b:
                chain.start(first + b * POOL_LINKS)
                rstd_of(b, 0, KB, EPS_LN)
                pool.wait_ge(x_in, n(b, 16, 16))
                g.tensor_tensor(xbp[:, :, :], xb[:, :, :], b_proj[:, :].unsqueeze(1).broadcast_to([P, QT, D]),
                                ALU.add).then_inc(xbp_ready, 1)
                pool.wait_ge(a_free, n(b, ACT_JOBS, SETUP_A + 2))
                g.tensor_tensor(km[:, H // 2:H, :], k0[:, :].unsqueeze(1).broadcast_to([P, H // 2, T]),
                                head_mask[:, H // 2:H].unsqueeze(2).broadcast_to([P, H // 2, T]),
                                ALU.mult).then_inc(km_half_ready, 1)
                for p in range(PAIRS):
                    pool.wait_ge(a_free, n(b, ACT_JOBS, SETUP_A + 12 + p))
                    link(g.tensor_tensor(k_raw[:, p % 2, :], k_raw[:, p % 2, :], cos_t[:, :], ALU.mult))
                    pool.wait_ge(d_free, n(b, DVE_JOBS, SETUP_D + 6 + p))
                    g.tensor_tensor(kr[:, p, :], k_raw[:, p % 2, :], k_sin[:, p % 2, :], ALU.add).then_inc(kr_ready, 1)
                rstd_of(b, 1, QT, EPS_LN)
                rstd_of(b, 2, QT, EPS_LN)
                pool.wait_ge(x1_ready, n(b, 1, 1))
                g.tensor_tensor(x1p[:, :, :], x1[:, :, :], b_wo[:, :].unsqueeze(1).broadcast_to([P, QT, D]),
                                ALU.add).then_inc(x1p_ready, 1)
                rstd_of(b, 3, 2 * KB, 1e-6)
                for p in range(PAIRS):
                    pool.wait_ge(clamped, n(b, HALVES, 2 * p + 2))
                    if p >= 2:
                        pool.wait_ge(o_full, n(b, PAIRS, p - 1))
                    pp = prob[:, p % 2]
                    link(g.tensor_tensor(psum[:, p % 2, :], pp[:, 0, :], pp[:, 1, :], ALU.add))
                    link(g.tensor_tensor(psum[:, p % 2, :], psum[:, p % 2, :], pp[:, 2, :], ALU.add))
                    g.tensor_tensor(psum[:, p % 2, :], psum[:, p % 2, :], pp[:, 3, :],
                                    ALU.add).then_inc(psum_ready, 1)
                rstd_of(b, 4, QT, EPS_LN)
                rstd_of(b, 5, QT, 1e-3)
                assert chain.k == POOL_LINKS, chain.k
            base = first + B * POOL_LINKS
            chain.start(base)
            g.tensor_copy(ident16[:, :], ident[:, :]).then_inc(ident16_ready, 1)
            pool.wait_ge(d_full, SETUP_D + B * DVE_JOBS)
            g.memset(one_row, 1.0).then_inc(ident16_ready, 1)
            for k in range(4):
                rstd_of(B, k, 4, EPS_LN)
            base += chain.k
            with pool.Fori(0, B) as b:
                chain.start(base + b * TAIL_POOL_LINKS)
                late = B * NORMS + 4
                for k, eps in enumerate((EPS_LN, 1e-6)):
                    rstd_of(0, late + b * TAIL_NORMS + k, QT, eps)
                assert chain.k == TAIL_POOL_LINKS, chain.k
            chain.start(base + B * TAIL_POOL_LINKS)
            late = B * NORMS + 4 + B * TAIL_NORMS
            for k in range(4):
                rstd_of(0, late + 2 * k, 4, 1e-6)
                rstd_of(0, late + 2 * k + 1, 4, EPS_LN)
            late += 8
            pool.wait_ge(x2_ready, B + 4)
            g.tensor_tensor(x2[:, :, :], x5[:, :, :], b_ffn[:, :].unsqueeze(1).broadcast_to([P, NT, D]),
                            ALU.add).then_inc(x5b_ready, 1)
            for k in range(4):
                rstd_of(0, late + k, 4, EPS_LN)

        @block.scalar
        def _(act):
            s = nc.scalar

            def evacuate(b, job, dst, src=None, **kw):
                act.wait_ge(a_full, n(b, ACT_JOBS, SETUP_A + job + 1))
                src = bank_a[:, :] if src is None else src
                s.activation(dst, src, ACT.Identity, **kw).then_inc(a_free, 1)

            act.wait_ge(weights_in, 16 * SETUP_LOADS)
            act.wait_ge(a_full, 1)
            s.copy(sin_t[:, :], bank_a[:, :]).then_inc(a_free, 1)
            with act.Fori(0, B) as b:
                evacuate(b, 0, x_t[:, :], bank_a[:, 0:T])
                evacuate(b, 1, k0[:, :], bank_a[:, 0:T])
                evacuate(b, 2, cn_t[:, :], scale=cols[:, CTX_G:CTX_G + 1], bias=cols[:, CTX_B:CTX_B + 1])

                def exps(lo, hi):
                    for e in range(lo, hi):
                        qt, h = divmod(e, H)
                        if h == 0:
                            act.wait_ge(neg_ready, n(b, QT, qt + 1))
                        pr = prob0[:, h, :] if qt == 0 else prob1[:, h, WINDOW:T]
                        i = s.activation(pr, pr, ACT.Exp, bias=neg_max[:, qt, h:h + 1],
                                         accum_out=row_sum[:, qt, h:h + 1])
                        if h == H - 1:
                            i.then_inc(exp0_done, 1)

                for j in range(8):
                    evacuate(b, 3 + j, v[:, j // 2, 512 * (j % 2):512 * (j % 2) + 512])
                    if j >= 4:
                        exps(2 * (j - 4), 2 * (j - 3))
                for p in range(PAIRS):
                    if p >= 2:
                        act.wait_ge(kr_ready, n(b, PAIRS, p - 1))
                    evacuate(b, 11 + p, k_raw[:, p % 2, :])
                    exps(8 + 3 * p, 8 + 3 * p + 3)
                for j in range(0, 12, 2):
                    evacuate(b, 19 + j // 2, pt[:, j % 4, :])
                evacuate(b, 25, rec_t[:, :], bank_a[:, 0:T])
                evacuate(b, 26, lat_t[:, :], bank_a[:, 0:T], scale=cols[:, LAT_G:LAT_G + 1],
                         bias=cols[:, LAT_B:LAT_B + 1])
                for p in range(0, PAIRS, 2):
                    act.wait_ge(a_full, n(b, ACT_JOBS, SETUP_A + 28 + p // 2))
                    s.activation(qm[0:DH, p, 0, :], bank_a[0:DH, 0:T], ACT.Identity)
                    s.activation(qm[DH:P, p, 1, :], bank_a[DH:P, 0:T], ACT.Identity).then_inc(a_free, 1)
                for p in range(PAIRS):
                    for hf in range(2):
                        act.wait_ge(half_full, n(b, HALVES, 2 * p + hf + 1))
                        if p >= 2 and hf == 0:
                            act.wait_ge(o_full, n(b, PAIRS, p - 1))
                        s.activation(prob[:, p % 2, 2 * hf:2 * hf + 2, :], sc[:, 2 * hf:2 * hf + 2, :], ACT.Exp,
                                     scale=DH ** -0.5).then_inc(exp_done, 1)

            def late(job, dst, src, **kw):
                act.wait_ge(ta_full, job)
                s.activation(dst, src, ACT.Identity, **kw).then_inc(ta_free, 1)

            late(1, tail[:, 0:3, :].rearrange("p k d -> p (k d)"), bank_a[:, 0:3 * D])
            for k in range(4):
                late(2 + k, f_t[:, 512 * k:512 * k + 512], bank_a[:, :], scale=cols[:, FFN_G:FFN_G + 1],
                     bias=cols[:, FFN_B:FFN_B + 1])
            for k in range(4):
                late(6 + k, x3_t.rearrange("p (t b) -> p b t", b=B)[:, 2 * k:2 * k + 2, :],
                     bank_a[:, :].rearrange("p (b t) -> p b t", b=2))
            act.wait_ge(c_ready, 1)
            s.activation(hid[:, 0:B], cf[:, 0:B], ACT.Tanh).then_inc(h_ready, 1)
            with act.Fori(0, (T - 1) // STEPS) as part:
                t0 = part * STEPS + 1
                for i in range(STEPS):
                    act.wait_ge(z_ready, t0 + i)
                    s.activation(hid[:, bass.ds((t0 + i) * B, B)], cf[:, bass.ds((t0 + i) * B, B)],
                                 ACT.Tanh).then_inc(h_ready, 1)
            with act.Fori(0, B) as b:
                job = 10 + b * TAIL_A
                late(job, pre_t, bank_a[:, 0:T], bias=small[:, OUT_BIAS:OUT_BIAS + 1])
                late(job + 1, x4_t, bank_a[:, 0:T])
                late(job + 2, q1_t, bank_a[:, 0:T])
            job = 10 + B * TAIL_A
            for k in range(4):
                late(job + k, att_t, bank_a[:, :])
            job += 4
            for k in range(4):
                act.wait_ge(ta_full, job + k)
                s.activation(q8_t[:, :], bank_a[:, 0:256].bitcast(BF16), ACT.Identity).then_inc(ta_free, 1)

        @block.vector
        def _(dve):
            chain = Chain(dve, dve_chain)
            link = chain.link
            w = nc.vector

            w.memset(settled[:, :], 0.0)
            dve.wait_ge(weights_in, 16 * SETUP_LOADS)
            for t in range(2):
                w.tensor_copy(trig_rep[:, t], trig_nat[:, t].unsqueeze(2).broadcast_to([P, KB, 4, HALF]))
            w.memset(rel_row, MASKED).then_inc(trig_ready, 1)
            dve.wait_ge(trig_ready, 1)
            dve.wait_ge(d_full, 1)
            w.tensor_copy(w_qkv_t[:, :], bank_d[:, 0:3 * D])
            w.tensor_copy(w_proj_t[:, :], bank_d[:, 3 * D:4 * D]).then_inc(d_free, 1)
            dve.wait_ge(d_full, 2)
            w.tensor_copy(rel_row[:, P - 1:P + WINDOW], bank_d[0:H, 0:WINDOW + 1]).then_inc(d_free, 1)
            dve.wait_ge(d_full, 3)
            w.tensor_copy(cos_t[:, :], bank_d[:, :]).then_inc(d_free, 1)
            dve.wait_ge(bias_in, 16)
            w.memset(prob1[:, :, 0:WINDOW], 0.0)
            first = chain.k

            def band_of(h, count):
                band = bias_mask[:, h, 0:count]
                return bass.AP(tensor=band.tensor, offset=band.offset + count - 1, ap=[list(band.ap[0]), [-1, count]])

            cells = [0]

            def settle():
                cells[0] = cells[0] % 31 + 1
                w.tensor_copy(settled[:, cells[0]:cells[0] + 1], settled[:, 0:1])

            def statistics(b, k, tiles):
                settle()
                for i, tile in enumerate(tiles):
                    last = w.bn_stats(stats[:, i, :], tile)
                link(last)
                settle()
                for i in range(len(tiles)):
                    last = w.bn_aggr(mv[:, i, :], stats[:, i, :])
                last.then_inc(var_ready, 1)
                dve.wait_ge(rstd_ready, n(b, NORMS, k + 1))

            def normalize(dsts, tiles):
                for i, (dst, tile) in enumerate(zip(dsts, tiles)):
                    last = w.tensor_scalar(dst, tile, mv[:, i, 0:1], rstd[:, i:i + 1], ALU.subtract, ALU.mult)
                return last

            def bank_ready(b, job):
                dve.wait_ge(d_full, n(b, DVE_JOBS, SETUP_D + job + 1))

            def tiles_of(t, count):
                return [t[:, i, :] for i in range(count)]

            with dve.Fori(0, B) as b:
                chain.start(first + b * DVE_LINKS)
                dve.wait_ge(ctx_in, n(b, 16, 16))
                statistics(b, 0, tiles_of(cb, KB))
                normalize(tiles_of(cn, KB), tiles_of(cb, KB)).then_inc(cn_ready, 1)
                bank_ready(b, 0)
                w.tensor_copy(ctx_t[:, :], bank_d[:, :]).then_inc(d_free, 1)
                bank_ready(b, 1)
                w.tensor_scalar(q0[:, :], bank_d[:, 0:T], HD ** -0.5, None, ALU.mult).then_inc(d_free, 1)
                dve.wait_ge(a_free, n(b, ACT_JOBS, SETUP_A + 2))
                w.tensor_tensor(km[:, 0:H // 2, :], k0[:, :].unsqueeze(1).broadcast_to([P, H // 2, T]),
                                head_mask[:, 0:H // 2].unsqueeze(2).broadcast_to([P, H // 2, T]),
                                ALU.mult).then_inc(km_ready, 1)
                bank_ready(b, 2)
                for t in range(QT):
                    last = w.tensor_tensor(vm[:, t], bank_d[:, t * D:(t + 1) * D].unsqueeze(1).broadcast_to([P, G, D]),
                                           quad_mask[:, :, :], ALU.mult)
                last.then_inc(d_free, 1)
                for j in range(2):
                    bank_ready(b, 3 + j)
                    w.tensor_copy(kv1[:, 4 * j:4 * j + 4, :],
                                  bank_d[:, :].rearrange("p (k d) -> p k d", d=D)).then_inc(d_free, 1)
                for g in range(SCORES):
                    dve.wait_ge(scores_full, n(b, SCORES, g + 1))
                    settle()
                    if g < 4:
                        for h in range(4):
                            hh = 4 * g + h
                            last = w.tensor_tensor_reduce(prob0[:, hh, :], sc[:, g, h * P:(h + 1) * P],
                                                          band_of(hh, P), 1.0, 0.0, ALU.add, ALU.max,
                                                          row_max[:, 0, hh:hh + 1])
                    else:
                        for h in range(2):
                            hh = 2 * (g - 4) + h
                            last = w.tensor_tensor_reduce(prob1[:, hh, WINDOW:T], sc[:, g % 4, h * BAND:(h + 1) * BAND],
                                                          band_of(hh, BAND), 1.0, 0.0, ALU.add, ALU.max,
                                                          row_max[:, 1, hh:hh + 1])
                    last.then_inc(scores_free, 1)
                    if g in (3, SCORES - 1):
                        qt = 0 if g == 3 else 1
                        dve.wait_ge(scores_free, n(b, SCORES, g + 1))
                        w.tensor_scalar(neg_max[:, qt, :], row_max[:, qt, :], -1.0, None,
                                        ALU.mult).then_inc(neg_ready, 1)
                for p in range(PAIRS):
                    bank_ready(b, 5 + p)
                    if p >= 2:
                        dve.wait_ge(kr_ready, n(b, PAIRS, p - 1))
                    w.tensor_tensor(k_sin[:, p % 2, :], bank_d[:, :], sin_t[:, :], ALU.mult).then_inc(d_free, 1)
                for qt in range(QT):
                    dve.wait_ge(exp0_done, n(b, QT, qt + 1))
                    w.reciprocal(row_rec[:, qt], row_sum[:, qt, :].unsqueeze(2).broadcast_to([P, H, HD])
                                 ).then_inc(rec0_ready, 1)
                for j in range(1, 12, 2):
                    bank_ready(b, 13 + j // 2)
                    w.tensor_copy(pt[:, j % 4, :], bank_d[:, :]).then_inc(d_free, 1)
                dve.wait_ge(o0_full, n(b, 1, 1))
                dve.wait_ge(a_free, n(b, ACT_JOBS, SETUP_A + 26))
                for qt in range(QT):
                    last = w.tensor_tensor(o0[:, qt * P:(qt + 1) * P], ob[qt][:, 0:P], rec_t[:, qt * P:(qt + 1) * P],
                                           ALU.mult)
                last.then_inc(o0_ready, 1)
                bank_ready(b, 19)
                dve.wait_ge(xbp_ready, n(b, 1, 1))
                w.tensor_tensor(y[:, :, :], bank_d[:, 0:QT * D].rearrange("p (q d) -> p q d", q=QT), xbp[:, :, :],
                                ALU.add).then_inc(d_free, 1)
                dve.wait_ge(d_free, n(b, DVE_JOBS, SETUP_D + 20))
                statistics(b, 1, tiles_of(y, QT))
                normalize(tiles_of(x1, QT), tiles_of(y, QT)).then_inc(x1_ready, 1)
                dve.wait_ge(x1_ready, n(b, 1, 1))
                statistics(b, 2, tiles_of(x1, QT))
                normalize(tiles_of(lat, QT), tiles_of(x1, QT)).then_inc(lat_ready, 1)
                for p in range(1, PAIRS, 2):
                    bank_ready(b, 20 + p // 2)
                    w.tensor_copy(qm[0:DH, p, 0, :], bank_d[0:DH, 0:T])
                    w.tensor_copy(qm[DH:P, p, 1, :], bank_d[DH:P, 0:T]).then_inc(d_free, 1)
                statistics(b, 3, tiles_of(kv1, 2 * KB))
                link(normalize(tiles_of(kv1, 2 * KB), tiles_of(kv1, 2 * KB)))
                link(w.tensor_tensor(kv1[:, :, :], kv1[:, :, :], l1_g[:, :].unsqueeze(1).broadcast_to([P, 2 * KB, D]),
                                     ALU.mult))
                link(w.tensor_tensor(kv1[:, :, :], kv1[:, :, :], l1_b[:, :].unsqueeze(1).broadcast_to([P, 2 * KB, D]),
                                     ALU.add))
                kv1_v = kv1[:, :, :].rearrange("p (k t) d -> p k t d", t=2)
                keep_b = keep[:, b, :].unsqueeze(2).broadcast_to([P, KB, D])
                link(w.tensor_scalar(k1[:, :, :], kv1_v[:, :, 0, :], 0.0, 1e-6, ALU.max, ALU.add))
                w.tensor_tensor(v1[:, :, 0:D], kv1_v[:, :, 1, :], keep_b, ALU.mult)
                w.tensor_tensor(k1[:, :, :], k1[:, :, :], keep_b, ALU.mult).then_inc(k1_ready, 1)

                def attended(p):
                    dve.wait_ge(o_full, n(b, PAIRS, p + 1))
                    if p >= 1:
                        dve.wait_ge(on_ready, n(b, PAIRS, p))
                    link(w.reciprocal(o_rec[:, :], ob[p % 2][:, T:2 * T]))
                    w.tensor_tensor(on[:, p, :], ob[p % 2][:, 0:T], o_rec[:, :], ALU.mult).then_inc(on_ready, 1)

                for p in range(PAIRS):
                    for hf in range(2):
                        dve.wait_ge(exp_done, n(b, HALVES, 2 * p + hf + 1))
                        pr = prob[:, p % 2, 2 * hf:2 * hf + 2, :]
                        w.tensor_scalar(pr, pr, float(np.exp(-CLIP)), float(np.exp(CLIP)), ALU.max,
                                        ALU.min).then_inc(clamped, 1)
                    if p >= 1:
                        attended(p - 1)
                    if p == 4:
                        bank_ready(b, 24)
                        w.tensor_copy(kv_sums[:, b, :], bank_d[:, 0:D + 1]).then_inc(d_free, 1)
                attended(PAIRS - 1)
                bank_ready(b, 25)
                dve.wait_ge(x1p_ready, n(b, 1, 1))
                w.tensor_tensor(y[:, :, :], bank_d[:, 0:QT * D].rearrange("p (q d) -> p q d", q=QT), x1p[:, :, :],
                                ALU.add).then_inc(d_free, 1)
                dve.wait_ge(d_free, n(b, DVE_JOBS, SETUP_D + 26))
                statistics(b, 4, tiles_of(y, QT))
                link(normalize(tiles_of(x1, QT), tiles_of(y, QT)))
                w.tensor_copy(x2[:, bass.ds(b * QT, QT), :], x1[:, :, :])
                statistics(b, 5, tiles_of(x1, QT))
                normalize([f_all[:, b * QT + i, :] for i in range(QT)], tiles_of(x1, QT)).then_inc(x2_ready, 1)
                assert chain.k == DVE_LINKS, chain.k
            base = first + B * DVE_LINKS
            chain.start(base)

            def cell(k, m=1):
                return small[:, k:k + m]

            dve.wait_ge(mats_in, 16 * 8)
            w.tensor_reduce(cell(F_SUM), mats[:, M_FFN0, :], AX_X, ALU.add,
                            apply_absolute_value=True).then_inc(red_ready, 1)
            dve.wait_ge(td_full, 1)
            w.tensor_scalar(cell(BETA), bank_d[:, 0:1], 1.0 / (D * D), None, ALU.mult).then_inc(td_free, 1)
            dve.wait_ge(td_free, 1)
            link(w.tensor_scalar(cell(INV_BETA), cell(BETA), 1e-5, None, ALU.add))
            link(w.reciprocal(cell(INV_BETA), cell(INV_BETA)))
            link(w.tensor_scalar(w_round, mats[:, M_FFN0, :], cell(INV_BETA), ROUND, ALU.mult, ALU.add))
            link(w.tensor_scalar(w_round, w_round, ROUND, None, ALU.subtract))
            w.tensor_scalar(w_round, w_round, -1.0, 1.0, ALU.max, ALU.min).then_inc(prep_ready, 1)
            dve.wait_ge(td_full, 2)
            w.tensor_copy(tail[:, 3:6, :].rearrange("p k d -> p (k d)"), bank_d[:, 0:3 * D])
            w.tensor_copy(c_rows[:, 0:D], bank_d[0:1, 3 * D:4 * D]).then_inc(td_free, 1)
            dve.wait_ge(td_full, 3)
            w.tensor_tensor(gws_t, bank_d[:, 0:D], ident[:, :], ALU.add)
            w.tensor_copy(c_rows[:, D:2 * D], bank_d[0:1, D:2 * D])
            w.tensor_tensor(cell(OUT_BIAS), bank_d[:, 2 * D:2 * D + 1], cols[:, BO_COL:BO_COL + 1],
                            ALU.add).then_inc(td_free, 1)
            for k in range(4):
                dve.wait_ge(ta_free, 2 + k)
                last = w.tensor_reduce(cell(F_MAX + k), f_t[:, 512 * k:512 * k + 512], AX_X, ALU.max,
                                       apply_absolute_value=True)
            link(last)
            w.tensor_reduce(cell(Q_MAX), cell(F_MAX, 4), AX_X, ALU.max).then_inc(red_ready, 1)
            dve.wait_ge(td_full, 4)
            w.tensor_reduce(diag2[0:1, 0:1], bank_d[0:1, 0:P], AX_X, ALU.max).then_inc(td_free, 1)
            dve.wait_ge(td_full, 5)
            w.tensor_copy(cell(F_ALL), bank_d[:, 0:1]).then_inc(td_free, 1)
            dve.wait_ge(td_free, 5)
            w.tensor_scalar(cell(F_SCALE), cell(F_ALL), cell(BETA), 1.0 / QB, ALU.mult, ALU.mult)
            link(w.reciprocal(cell(F_INV), cell(F_ALL)))
            for k in range(4):
                part = f_t[:, 512 * k:512 * k + 512]
                link(w.tensor_scalar(part, part, QB, cell(F_INV), ALU.mult, ALU.mult))
                limit = float(np.float32(QB - 1e-5))
                w.tensor_scalar(part, part, -limit, limit, ALU.max, ALU.min).then_inc(f_quantized, 1)
            for k in range(4):
                dve.wait_ge(td_full, 6 + k)
                w.scalar_tensor_tensor(out=t4, in0=bank_d[:, :].rearrange("p (t d) -> p t d", d=D),
                                       scalar=cell(F_SCALE), in1=x2[:, 4 * k:4 * k + 4, :], op0=ALU.mult,
                                       op1=ALU.add).then_inc(td_free, 1)
                dve.wait_ge(td_free, 6 + k)
                statistics(B, k, tiles_of(t4, 4))
                if k >= 1:
                    dve.wait_ge(ta_full, 5 + k)
                normalize(tiles_of(t4b, 4), tiles_of(t4, 4)).then_inc(x3_ready, 1)
                dve.wait_ge(x3_ready, k + 1)
            base += chain.k

            def affine(t, count):
                for row, op in ((l1_g, ALU.mult), (l1_b, ALU.add)):
                    link(w.tensor_tensor(t, t, row[:, :].unsqueeze(1).broadcast_to([P, count, D]), op))

            with dve.Fori(0, B) as b:
                chain.start(base + b * TAIL_DVE_LINKS)
                late = B * NORMS + 4 + b * TAIL_NORMS
                job = 10 + b * TAIL_D
                hm = head_mask[:, :].unsqueeze(2).broadcast_to([P, H, HD])
                w.tensor_scalar(ksm.rearrange("p (h d) -> p h d", d=HD), hm, kv_sums[:, b, D:D + 1], None, ALU.mult)
                w.tensor_tensor(kvm.rearrange("p (h d) -> p h d", d=HD),
                                kv_sums[:, b, 0:D].rearrange("p (h d) -> p h d", d=HD), hm,
                                ALU.mult).then_inc(kvm_ready, 1)
                dve.wait_ge(td_full, job)
                pre = [bank_d[:, i * P:(i + 1) * P] for i in range(QT)]
                statistics(0, late, pre)
                normalize(tiles_of(x4, QT), pre).then_inc(td_free, 1)
                dve.wait_ge(td_full, job + 1)
                statistics(0, late + 1, pre)
                normalize(tiles_of(q1, QT), pre).then_inc(td_free, 1)
                dve.wait_ge(td_free, job + 1)

                affine(q1[:, :, :], QT)
                w.tensor_scalar(q1[:, :, :], q1[:, :, :], 0.0, 1e-6, ALU.max, ALU.add).then_inc(q1_ready, 1)
                dve.wait_ge(td_full, job + 2)
                link(w.tensor_scalar(den, bank_d[:, T:2 * T], 1e-6, None, ALU.add))
                link(w.reciprocal(den, den))
                w.tensor_tensor(att[:, bass.ds(b * QT, QT), :].rearrange("p q d -> p (q d)"), bank_d[:, 0:T], den,
                                ALU.mult).then_inc(att_ready, 1)
                dve.wait_ge(att_ready, b + 1)
                w.tensor_copy(x4_all[:, bass.ds(b * QT, QT), :], x4[:, :, :]).then_inc(td_free, 1)
                assert chain.k == TAIL_DVE_LINKS, chain.k
            chain.start(base + B * TAIL_DVE_LINKS)
            job = 10 + B * TAIL_D
            late = B * NORMS + 4 + B * TAIL_NORMS
            for k in range(4):
                dve.wait_ge(td_full, job + k)
                w.tensor_tensor(out_t, bank_d[:, :].rearrange("p (t d) -> p t d", d=D),
                                b_dense[:, :].unsqueeze(1).broadcast_to([P, 4, D]), ALU.add).then_inc(td_free, 1)
                dve.wait_ge(td_free, job + k)
                statistics(0, late + 2 * k, tiles_of(out_t, 4))
                link(normalize(tiles_of(out_t, 4), tiles_of(out_t, 4)))
                affine(out_t, 4)
                link(w.tensor_tensor(out_t, out_t, x4_all[:, 4 * k:4 * k + 4, :], ALU.add))
                statistics(0, late + 2 * k + 1, tiles_of(out_t, 4))
                normalize([x5[:, 4 * k + i, :] for i in range(4)], tiles_of(out_t, 4)).then_inc(x2_ready, 1)
                dve.wait_ge(x2_ready, B + k + 1)
            job += 4
            late += 8
            w.tensor_reduce(cell(Q_MAX + 1), mats[:, M_FFN1, :], AX_X, ALU.max, apply_absolute_value=True)
            w.tensor_reduce(cell(Q_MAX), x5[:, :, :], mybir.AxisListType.XY, ALU.max,
                            apply_absolute_value=True).then_inc(red_ready, 1)
            dve.wait_ge(td_full, job)
            w.tensor_reduce(diag2[0:2, 2:3], bank_d[0:2, 0:P], AX_X, ALU.max).then_inc(td_free, 1)
            dve.wait_ge(td_free, job)
            w.tensor_scalar(diag2[0:2, 0:2], ident[0:2, 0:2], diag2[0:2, 2:3], None, ALU.mult).then_inc(red_ready, 1)
            dve.wait_ge(td_full, job + 1)
            w.tensor_scalar(cell(Q_SCALE, 2), bank_d[:, 0:2], 1e-12, None, ALU.max).then_inc(td_free, 1)
            dve.wait_ge(td_free, job + 1)
            link(w.reciprocal(cell(Q_SCALE, 2), cell(Q_SCALE, 2)))
            link(w.tensor_scalar(cell(Q_SCALE, 2), cell(Q_SCALE, 2), FP8_MAX, None, ALU.mult))
            link(w.tensor_tensor(cell(Q_INV), cell(Q_SCALE), cell(Q_SCALE + 1), ALU.mult))
            link(w.reciprocal(cell(Q_INV), cell(Q_INV)))

            def round8(dst, src, lev, scale):
                link(w.tensor_scalar(src, src, scale, None, ALU.mult))
                link(w.tensor_scalar(lev.bitcast(U32), src.bitcast(U32), 0x7F800000, None, ALU.bitwise_and))
                link(w.tensor_scalar(lev, lev, FP8_MIN_NORMAL, FP8_ROUND, ALU.max, ALU.mult))
                link(w.tensor_tensor(src, src, lev, ALU.add))
                return w.tensor_tensor(dst, src, lev, ALU.subtract)

            round8(w8[:, 0, :], mats[:, M_FFN1, :], w_round, cell(Q_SCALE + 1)).then_inc(q8_ready, 1)
            dve.wait_ge(x5b_ready, 1)
            for k in range(4):
                part = x5[:, 4 * k:4 * k + 4, :]
                round8(q8[:, 4 * k:4 * k + 4, :], part, level[:, 4 * k:4 * k + 4, :],
                       cell(Q_SCALE)).then_inc(q8_ready, 1)
            dve.wait_ge(td_full, job + 2)
            w.tensor_copy(w8[:, 1, :], bank_d[:, 0:64].bitcast(BF16)).then_inc(td_free, 1)
            dve.wait_ge(q8_ready, 5)
            for k in range(4):
                dve.wait_ge(td_full, job + 3 + k)
                res = x2[:, 4 * k:4 * k + 4, :]
                w.scalar_tensor_tensor(out=res, in0=bank_d[:, :].rearrange("p (t d) -> p t d", d=D),
                                       scalar=cell(Q_INV), in1=res, op0=ALU.mult, op1=ALU.add).then_inc(td_free, 1)
                dve.wait_ge(td_free, job + 3 + k)
                statistics(0, late + k, tiles_of(res, 4))
                normalize(tiles_of(f_all[:, 4 * k:4 * k + 4, :], 4), tiles_of(res, 4)).then_inc(out_ready, 1)
                dve.wait_ge(out_ready, k + 1)

        @block.tensor
        def _(pe):
            mm = nc.tensor.matmul

            def turn(out_ap, in_ap):
                return nc.tensor.transpose(out_ap, in_ap, ident[0:in_ap.shape[0], 0:in_ap.shape[0]])

            pe.wait_ge(weights_in, 16 * SETUP_LOADS)
            pe.wait_ge(consts_made, 1)
            for k in range(4):
                last = turn(bank_d[:, k * P:(k + 1) * P], w_nat[:, k, :])
            last.then_inc(d_full, 1)
            pe.wait_ge(d_free, 1)
            pe.wait_ge(trig_ready, 1)
            pe.wait_ge(swap_ready, 1)
            turn(bank_d[0:H, 0:WINDOW + 1], rel).then_inc(d_full, 1)
            pe.wait_ge(d_free, 2)
            for t, bank in ((0, bank_d), (1, bank_a)):
                for k in range(KB):
                    last = turn(bank[:, k * P:(k + 1) * P], trig_rep[:, t, k].rearrange("p r d -> p (r d)"))
                last.then_inc(d_full if t == 0 else a_full, 1)

            with pe.Fori(0, B) as b:
                def a_job(job):
                    pe.wait_ge(a_free, n(b, ACT_JOBS, SETUP_A + job))

                def d_job(job):
                    pe.wait_ge(d_free, n(b, DVE_JOBS, SETUP_D + job))

                pe.wait_ge(x_in, n(b, 16, 16))
                a_job(0)
                for t in range(QT):
                    last = turn(bank_a[:, t * P:(t + 1) * P], xb[:, t, :])
                last.then_inc(a_full, 1)
                pe.wait_ge(ctx_in, n(b, 16, 16))
                d_job(0)
                for k in range(KB):
                    last = turn(bank_d[:, k * P:(k + 1) * P], cb[:, k, :])
                last.then_inc(d_full, 1)
                a_job(1)
                mm(bank_a[:, 0:T], w_qkv_t[:, D:2 * D], x_t[:, :], start=True, stop=True).then_inc(a_full, 1)
                d_job(1)
                mm(bank_d[:, 0:T], w_qkv_t[:, 0:D], x_t[:, :], start=True, stop=True).then_inc(d_full, 1)
                d_job(2)
                for t in range(QT):
                    last = mm(bank_d[:, t * D:(t + 1) * D], x_t[:, t * P:(t + 1) * P], w_qkv_t[:, 2 * D:3 * D],
                              start=True, stop=True, skip_group_check=True)
                last.then_inc(d_full, 1)
                for j in range(2):
                    d_job(3 + j)
                    for k in range(2):
                        kb = 2 * j + k
                        last = mm(bank_d[:, 2 * k * D:2 * (k + 1) * D], ctx_t[:, kb * P:(kb + 1) * P], w_l1kv[:, :],
                                  start=True, stop=True, skip_group_check=True)
                    last.then_inc(d_full, 1)
                a_job(2)
                pe.wait_ge(cn_ready, n(b, 1, 1))
                for k in range(KB):
                    last = turn(bank_a[:, k * P:(k + 1) * P], cn[:, k, :])
                last.then_inc(a_full, 1)

                def values(j):
                    a_job(3 + j)
                    kb, half = divmod(j, 2)
                    mm(bank_a[:, :], cn_t[:, kb * P:(kb + 1) * P], wkv[:, INNER + 512 * half:INNER + 512 * half + 512],
                       start=True, stop=True).then_inc(a_full, 1)

                for j in range(4):
                    values(j)
                pe.wait_ge(km_ready, n(b, 1, 1))
                pe.wait_ge(km_half_ready, n(b, 1, 1))
                for g in range(SCORES):
                    if g >= 4:
                        pe.wait_ge(scores_free, n(b, SCORES, g - 3))
                    if g < 4:
                        last = mm(sc[:, g, 0:4 * P], q0[:, 0:P], km[:, 4 * g:4 * g + 4, 0:P], start=True, stop=True)
                    else:
                        h = 2 * (g - 4)
                        last = mm(sc[:, g % 4, 0:2 * BAND], q0[:, P:T], km[:, h:h + 2, T - BAND:T], start=True,
                                  stop=True)
                    last.then_inc(scores_full, 1)
                for j in range(4, 8):
                    values(j)
                for p in range(PAIRS):
                    a_job(11 + p)
                    mm(bank_a[:, :], wkv[:, p * P:(p + 1) * P], cn_t[:, :], start=True, stop=True).then_inc(a_full, 1)
                    d_job(5 + p)
                    mm(bank_d[:, :], wk_swap[:, p * P:(p + 1) * P], cn_t[:, :], start=True,
                       stop=True).then_inc(d_full, 1)

                jobs = [[(0, j, 0, g) for g in range(G)] for j in range(G)]
                jobs += [[(1, j, kt, 2 * m + g) for kt in range(QT) for g in range(2)] for j in range(G)
                         for m in range(2)]

                def turn_probs(j):
                    bank, full = (bank_a, a_full) if j % 2 == 0 else (bank_d, d_full)
                    if j % 2 == 0:
                        a_job(19 + j // 2)
                    else:
                        d_job(13 + j // 2)
                    for i, (qt, hq, kt, g) in enumerate(jobs[j]):
                        h = 4 * g + hq
                        src = prob0[:, h, :] if qt == 0 else prob1[:, h, kt * P:(kt + 1) * P]
                        last = turn(bank[:, i * P:(i + 1) * P], src)
                    last.then_inc(full, 1)

                def weigh_values(j):
                    if j % 2 == 0:
                        a_job(20 + j // 2)
                    else:
                        d_job(14 + j // 2)
                    for i, (qt, hq, kt, g) in enumerate(jobs[j]):
                        last = mm(ob[qt][32 * g:32 * g + 32, 0:P], vm[:, kt, hq, 32 * g:32 * g + 32],
                                  pt[:, j % 4, i * P:(i + 1) * P], start=(hq == 0 and kt == 0),
                                  stop=(hq == G - 1 and (qt == 0 or kt == QT - 1)), skip_group_check=True)
                    return last

                pe.wait_ge(exp0_done, n(b, QT, QT))
                for j in range(12):
                    turn_probs(j)
                    if j >= 2:
                        weigh_values(j - 2)
                weigh_values(10)
                a_job(25)
                pe.wait_ge(rec0_ready, n(b, QT, QT))
                for qt in range(QT):
                    last = turn(bank_a[:, qt * P:(qt + 1) * P], row_rec[:, qt].rearrange("p h d -> p (h d)"))
                last.then_inc(a_full, 1)
                weigh_values(11).then_inc(o0_full, 1)
                pe.wait_ge(o0_ready, n(b, 1, 1))
                d_job(19)
                for qt in range(QT):
                    last = mm(bank_d[:, qt * D:(qt + 1) * D], o0[:, qt * P:(qt + 1) * P], w_proj_t[:, :], start=True,
                              stop=True, skip_group_check=True)
                last.then_inc(d_full, 1)
                a_job(26)
                pe.wait_ge(lat_ready, n(b, 1, 1))
                for qt in range(QT):
                    last = turn(bank_a[:, qt * P:(qt + 1) * P], lat[:, qt, :])
                last.then_inc(a_full, 1)
                pe.wait_ge(a_free, n(b, ACT_JOBS, SETUP_A + 27))
                for p in range(PAIRS):
                    bank, full = (bank_a, a_full) if p % 2 == 0 else (bank_d, d_full)
                    if p % 2 == 0:
                        a_job(27 + p // 2)
                    else:
                        d_job(20 + p // 2)
                    mm(bank[:, 0:T], wq[:, p * P:(p + 1) * P], lat_t[:, :], start=True, stop=True).then_inc(full, 1)
                pe.wait_ge(a_free, n(b, ACT_JOBS, SETUP_A + 31))
                pe.wait_ge(d_free, n(b, DVE_JOBS, SETUP_D + 24))
                pe.wait_ge(kr_ready, n(b, PAIRS, PAIRS))

                def pair_scores(p):
                    for hf in range(2):
                        if p >= 1:
                            pe.wait_ge(exp_done, n(b, HALVES, 2 * p + hf - 1))
                        for k in range(2):
                            kb = 2 * hf + k
                            last = mm(sc[:, kb, :], kr[:, p, kb * P:(kb + 1) * P], qm[:, p], start=True, stop=True)
                        last.then_inc(half_full, 1)

                def pair_values(p):
                    pe.wait_ge(clamped, n(b, HALVES, 2 * p + 2))
                    if p >= 2:
                        pe.wait_ge(on_ready, n(b, PAIRS, p - 1))
                    o = ob[p % 2]
                    for kb in range(KB):
                        for h in range(2):
                            mm(o[DH * h:DH * (h + 1), 0:T], v[:, kb, P * p + DH * h:P * p + DH * (h + 1)],
                               prob[:, p % 2, kb, T * h:T * (h + 1)], start=(kb == 0), stop=(kb == KB - 1),
                               skip_group_check=True)
                    pe.wait_ge(psum_ready, n(b, PAIRS, p + 1))
                    for h in range(2):
                        last = mm(o[DH * h:DH * (h + 1), T:2 * T], ones[:, 0:DH], psum[:, p % 2, T * h:T * (h + 1)],
                                  start=True, stop=True, skip_group_check=True)
                    last.then_inc(o_full, 1)

                for p in range(PAIRS):
                    pair_scores(p)
                    if p >= 1:
                        pair_values(p - 1)
                    if p == 3:
                        d_job(24)
                        pe.wait_ge(k1_ready, n(b, 1, 1))
                        for kb in range(KB):
                            last = mm(bank_d[:, 0:D + 1], k1[:, kb, :], v1[:, kb, :], start=(kb == 0),
                                      stop=(kb == KB - 1))
                        last.then_inc(d_full, 1)
                pair_values(PAIRS - 1)
                d_job(25)
                pe.wait_ge(on_ready, n(b, PAIRS, PAIRS))
                for qt in range(QT):
                    for p in range(PAIRS):
                        last = mm(bank_d[:, qt * D:(qt + 1) * D], on[:, p, qt * P:(qt + 1) * P], wo[:, p, :],
                                  start=(p == 0), stop=(p == PAIRS - 1), skip_group_check=True)
                last.then_inc(d_full, 1)

            pe.wait_ge(a_free, SETUP_A + B * ACT_JOBS)
            pe.wait_ge(mats_in, 16 * 8)
            for k, m in enumerate((M_A, M_B, M_WO)):
                last = turn(bank_a[:, k * P:(k + 1) * P], mats[:, m, :])
            last.then_inc(ta_full, 1)
            pe.wait_ge(d_free, SETUP_D + B * DVE_JOBS)
            pe.wait_ge(red_ready, 1)
            mm(bank_d[:, 0:1], ones[:, :], small[:, F_SUM:F_SUM + 1], start=True, stop=True).then_inc(td_full, 1)
            pe.wait_ge(x2_ready, B)
            for k in range(4):
                pe.wait_ge(ta_free, 1 + k)
                for i in range(4):
                    last = turn(bank_a[:, i * P:(i + 1) * P], f_all[:, 4 * k + i, :])
                last.then_inc(ta_full, 1)
            pe.wait_ge(td_free, 1)
            mm(bank_d[:, 0:D], mats[:, M_WI, :], b_t, start=True, stop=True, skip_group_check=True)
            mm(bank_d[:, D:2 * D], mats[:, M_WS, :], a_t, start=True, stop=True, skip_group_check=True)
            mm(bank_d[:, 2 * D:3 * D], mats[:, M_C, :], wo_t, start=True, stop=True, skip_group_check=True)
            mm(bank_d[0:1, 3 * D:4 * D], cols[:, BI_COL:BI_COL + 1], b_t, start=True, stop=True,
               skip_group_check=True).then_inc(td_full, 1)
            pe.wait_ge(td_free, 2)
            mm(bank_d[:, 0:D], mats[:, M_WS, :], g_t, start=True, stop=True, skip_group_check=True)
            mm(bank_d[0:1, D:2 * D], cols[:, BI_COL:BI_COL + 1], b_t, start=True, stop=False, skip_group_check=True)
            mm(bank_d[0:1, D:2 * D], cols[:, BS_COL:BS_COL + 1], a_t, start=False, stop=True, skip_group_check=True)
            mm(bank_d[:, 2 * D:2 * D + 1], g_t, cols[:, BS_COL:BS_COL + 1], start=True, stop=True,
               skip_group_check=True).then_inc(td_full, 1)
            pe.wait_ge(td_free, 3)
            pe.wait_ge(red_ready, 2)
            turn(bank_d[0:1, 0:P], small[:, Q_MAX:Q_MAX + 1]).then_inc(td_full, 1)
            pe.wait_ge(td_free, 4)
            mm(bank_d[:, 0:1], ones[0:1, :], diag2[0:1, 0:1], start=True, stop=True).then_inc(td_full, 1)

            def turn_x3(k):
                pe.wait_ge(x3_ready, k + 1)
                pe.wait_ge(ta_free, 5 + k)
                for i in range(4):
                    last = turn(bank_a[:, i * P:(i + 1) * P], t4b[:, i, :])
                last.then_inc(ta_full, 1)

            pe.wait_ge(prep_ready, 1)
            for k in range(4):
                pe.wait_ge(td_free, 5 + k)
                pe.wait_ge(f_quantized, k + 1)
                for i in range(4):
                    t = 4 * k + i
                    last = mm(bank_d[:, i * D:(i + 1) * D], f_t[:, t * P:(t + 1) * P], w_round, start=True, stop=True,
                              skip_group_check=True)
                last.then_inc(td_full, 1)
                if k >= 1:
                    turn_x3(k - 1)
            turn_x3(3)
            pe.wait_ge(ta_free, 9)
            pe.wait_ge(ident16_ready, 2)
            for k in range(4):
                mm(sc[:, k, :], bwi_t, x3_t[:, 512 * k:512 * k + 512], start=True, stop=False, skip_group_check=True)
                lo = B if k == 0 else 0
                mm(sc[:, k, lo:512], aws_t, x3_t[:, 512 * k + lo - B:512 * k + 512 - B], start=False, stop=False,
                   skip_group_check=True)
                last = mm(sc[:, k, lo:512], c_rows[:, D:2 * D], one_row[:, lo:512], start=False, stop=True,
                          skip_group_check=True)
                if k == 0:
                    last = mm(sc[:, 0, 0:B], c_rows[:, 0:D], one_row[:, 0:B], start=False, stop=True,
                              skip_group_check=True)
            last.then_inc(c_ready, 1)
            with pe.Fori(0, (T - 1) // STEPS) as part:
                t0 = part * STEPS + 1
                for i in range(STEPS):
                    pe.wait_ge(h_ready, t0 + i)
                    mm(cf[:, bass.ds((t0 + i) * B, B)], a_t, hid[:, bass.ds((t0 + i - 1) * B, B)], start=False,
                       stop=True, skip_group_check=True).then_inc(z_ready, 1)
            pe.wait_ge(h_ready, T)
            hid_b = hid.rearrange("p (t b) -> p b t", b=B)
            x3_b = x3_t.rearrange("p (t b) -> p b t", b=B)
            with pe.Fori(0, B) as b:
                ja = 9 + b * TAIL_A
                jd = 9 + b * TAIL_D
                pe.wait_ge(ta_free, ja)
                mm(bank_a[:, 0:T], g_t, hid_b[:, b, :], start=True, stop=False)
                mm(bank_a[:, 0:T], gws_t, x3_b[:, b, :], start=False, stop=True).then_inc(ta_full, 1)
                pe.wait_ge(ta_free, ja + 1)
                pe.wait_ge(td_free, jd)
                for i in range(QT):
                    last = turn(bank_d[:, i * P:(i + 1) * P], pre_t[:, i * P:(i + 1) * P])
                last.then_inc(td_full, 1)
                pe.wait_ge(td_free, jd + 1)
                for i in range(QT):
                    last = turn(bank_a[:, i * P:(i + 1) * P], x4[:, i, :])
                last.then_inc(ta_full, 1)
                pe.wait_ge(ta_free, ja + 2)
                for i in range(QT):
                    last = mm(bank_d[:, i * P:(i + 1) * P], x4_t[:, i * P:(i + 1) * P], w_l1q[:, :], start=True,
                              stop=True, skip_group_check=True)
                last.then_inc(td_full, 1)
                pe.wait_ge(q1_ready, b + 1)
                for i in range(QT):
                    last = turn(bank_a[:, i * P:(i + 1) * P], q1[:, i, :])
                last.then_inc(ta_full, 1)
                pe.wait_ge(ta_free, ja + 3)
                pe.wait_ge(td_free, jd + 2)
                pe.wait_ge(kvm_ready, b + 1)
                for i in range(QT):
                    tok = q1_t[:, i * P:(i + 1) * P]
                    mm(bank_d[:, i * P:(i + 1) * P], tok, kvm, start=True, stop=True, skip_group_check=True)
                    last = mm(bank_d[:, T + i * P:T + (i + 1) * P], tok, ksm, start=True, stop=True,
                              skip_group_check=True)
                last.then_inc(td_full, 1)
            ja = 9 + B * TAIL_A
            jd = 9 + B * TAIL_D
            pe.wait_ge(mixed_in, 16 * B * H)
            for k in range(4):
                pe.wait_ge(ta_free, ja + k)
                for i in range(4):
                    last = turn(bank_a[:, i * P:(i + 1) * P], mixed[:, 4 * k + i, :])
                last.then_inc(ta_full, 1)
                pe.wait_ge(ta_free, ja + k + 1)
                pe.wait_ge(td_free, jd + k)
                for i in range(4):
                    last = mm(bank_d[:, i * P:(i + 1) * P], att_t[:, i * P:(i + 1) * P], w_dense[:, :], start=True,
                              stop=True, skip_group_check=True)
                last.then_inc(td_full, 1)
            ja += 4
            jd += 4
            pe.wait_ge(td_free, jd)
            pe.wait_ge(red_ready, 3)
            turn(bank_d[0:2, 0:P], small[:, Q_MAX:Q_MAX + 2]).then_inc(td_full, 1)
            pe.wait_ge(td_free, jd + 1)
            pe.wait_ge(red_ready, 4)
            mm(bank_d[:, 0:2], ones[0:2, :], diag2[0:2, 0:2], start=True, stop=True).then_inc(td_full, 1)
            pe.wait_ge(q8_ready, 1)
            pe.wait_ge(td_free, jd + 2)
            nc.tensor.transpose(bank_d[:, 0:64].bitcast(BF16), w8[:, 0, :], ident16[:, :]).then_inc(td_full, 1)
            for k in range(4):
                pe.wait_ge(q8_ready, 2 + k)
                pe.wait_ge(ta_free, ja + k)
                for i in range(4):
                    last = nc.tensor.transpose(bank_a[:, 64 * i:64 * i + 64].bitcast(BF16), q8[:, 4 * k + i, :],
                                               ident16[:, :])
                last.then_inc(ta_full, 1)
                pe.wait_ge(ta_free, ja + k + 1)
                pe.wait_ge(td_free, jd + 3 + k)
                for i in range(4):
                    last = mm(bank_d[:, i * P:(i + 1) * P], q8_t[:, i * P:(i + 1) * P], w8[:, 1, :], start=True,
                              stop=True, skip_group_check=True)
                last.then_inc(td_full, 1)


_INS = [
    "x", "ctx_1024", "mask_BxS2_ff1", "L0_attn_w_qkv", "L0_attn_w_proj", "L0_attn_b_proj", "L0_attn_rel_bias",
    "L0_xattn_cos", "L0_xattn_sin", "L0_xattn_ln_lat_g", "L0_xattn_ln_lat_b", "L0_xattn_ln_ctx_g",
    "L0_xattn_ln_ctx_b", "L0_xattn_Wq", "L0_xattn_Wkv", "L0_xattn_Wo", "L0_xattn_bo", "L0_ffn_weight",
    "L0_ffn_ln_gamma", "L0_ffn_ln_beta", "L1_attn_Wi", "L1_attn_bi", "L1_attn_Ws", "L1_attn_bs", "L1_attn_Wo",
    "L1_attn_bo", "L1_attn_A", "L1_attn_B", "L1_attn_C", "L1_xattn_wq", "L1_xattn_wk", "L1_xattn_wv",
    "L1_xattn_ln_gamma", "L1_xattn_ln_beta", "L1_xattn_dense_w", "L1_xattn_dense_b", "L1_ffn_weight", "L1_ffn_bias",
]


def kernel(**inputs):
    import numpy as _np
    import concourse.bacc as _bacc
    from concourse import mybir as _mybir
    from concourse.bass_utils import run_bass_kernel_spmd as _run

    nc = _bacc.Bacc("TRN2", target_bir_lowering=False, num_devices=1)
    arrays, args = {}, {}
    for name in _INS:
        arr = _np.ascontiguousarray(inputs[name])
        arrays[f"in_{name}_dram"] = arr
        args[name] = nc.dram_tensor(f"in_{name}_dram", arr.shape, _mybir.dt.from_np(arr.dtype),
                                    kind="ExternalInput").ap()
    out = nc.dram_tensor("out_0_dram", (B, T, D), F32, kind="ExternalOutput").ap()
    decoder(nc, args, out)
    r = _run(nc, [arrays], core_ids=[0])
    return r.results[0]["out_0_dram"]
```

```python
from contextlib import ExitStack

import numpy as np

import concourse.bass as bass
from concourse import mybir

F32 = mybir.dt.float32
F32R = mybir.dt.float32r
BF16 = mybir.dt.bfloat16
U32 = mybir.dt.uint32
ALU = mybir.AluOpType
ACT = mybir.ActivationFunctionType
AX_X = mybir.AxisListType.X

B, T, D = 8, 256, 128
S = 512
P = 128
QT = T // P
KB = S // P
NT = B * QT
H = 16
HD = D // H
G = 4
WINDOW = 64
MAX_REL = 128
DH = 64
HALF = DH // 2
PAIRS = H // 2
INNER = H * DH
CLIP = 11.0
MASKED = -1e30
BAND = WINDOW + P
SCRATCH = P - 1 + BAND
QB = 128.0
ROUND = 12582912.0
FP8_MAX = 448.0
FP8_MIN_NORMAL = 2.0 ** -6
FP8_ROUND = 1.5 * 2.0 ** 20
EPS_LN = 1e-5
EPSILONS = (EPS_LN, 1e-6, 1e-3)

PER_PAIR = 6
SLOTS = PER_PAIR * PAIRS
S_X, S_K, S_Q, S_CTX, S_V, S_KV_A, S_KV_B = range(7)
S_SCORE = range(10, 22)
S_MASKED = (2, 4, 14, 17)
S_EXP = list(range(17, 23)) + list(range(24, 30))
S_NORM, S_SCALE, S_SHIFT, S_RELU = (9, 15), 17, 19, 23
S_TURN, S_SUMS, S_REC, S_CN, S_PROJ, S_KV, S_LAT = 24, 30, 37, 36, 39, 41, 42
TURNS = 12
SCORES = 12
A_X, A_K, A_CTX, A_KV, A_TURN, A_CN, A_REC, A_LAT = 0, 1, 2, 3, 5, 17, 18, 19
ACT_JOBS = 20
D_SCORE, D_PROJ, D_KV = 2, 14, 15
DVE_JOBS = 16
SETUP_A = 1
SETUP_D = 3
PREP = []
for _p in range(8):
    VALUES = [(_p, "values 0"), (_p, "values 1")] if _p % 2 == 1 else []
    PREP += (VALUES + [(_p, "queries"), (_p, "keys")] if _p < 7 else
             [(_p, "keys")] + VALUES + [(_p, "queries")])
PREP_JOBS = len(PREP)
FIRST_PREP = 5
SELF_NORMS, NORMS = 5, 6
UNITS = KB * PAIRS
HALVES = 2 * PAIRS
SELF_DVE_LINKS, DVE_LINKS = 10, 20
SELF_POOL_LINKS, POOL_LINKS = 5, 30
TAIL_A, TAIL_D, TAIL_NORMS = 3, 3, 2
TAIL_DVE_LINKS = 6
TAIL_POOL_LINKS = 2
STEPS = 5


def n(b, per, k):
    return b * per + k


class Chain:

    def __init__(self, eng, sem):
        self.eng, self.sem, self.base, self.k = eng, sem, 0, 0

    def start(self, base):
        self.base, self.k = base, 0

    def link(self, instruction):
        self.k += 1
        instruction.then_inc(self.sem, 1)
        self.eng.wait_ge(self.sem, self.base + self.k)


def rows(ap, parts, offset, dims):
    return bass.AP(tensor=ap.tensor, offset=ap.offset + offset, ap=[list(parts)] + [list(d) for d in dims])


def decoder(nc, a, out):
    with ExitStack() as ctx:
        def sb(name, shape, dt=F32):
            return ctx.enter_context(nc.sbuf_tensor(name, shape, dt))

        def sem(name):
            return ctx.enter_context(nc.semaphore(name))

        sc = ctx.enter_context(nc.psum_tensor("score_banks", [P, 4, 512], F32))
        o0_bank = sc[:, 2, :]
        bank_p = sc[:, 3, :]
        cf = sc[:, :, :].rearrange("p k c -> p (k c)")
        ob = ctx.enter_context(nc.psum_tensor("out_bank", [P, 512], F32))
        bank_a = ctx.enter_context(nc.psum_tensor("bank_a", [P, 512], F32))
        bank_d, bank_d2 = (ctx.enter_context(nc.psum_tensor(f"bank_d{i}", [P, 512], F32)) for i in range(2))

        def pair_bank(p):
            return ob if p < PAIRS - 1 else o0_bank

        def d_bank(job):
            return (bank_d, bank_d2)[(SETUP_D + job) % 2]


        ident = sb("ident", [P, P])
        ones = sb("ones", [P, P])
        minus_half = sb("minus_half", [P, 8])
        epsilons = sb("epsilons", [P, 3, 8])
        head_mask = sb("head_mask", [P, H])
        mask_jg = sb("mask_jg", [P, H])
        quad_mask = sb("quad_mask", [P, G, P])
        bias_mask = sb("bias_mask", [P, H, BAND])
        w_qkv_t = sb("w_qkv_t", [P, 3 * D])
        w_proj_t = sb("w_proj_t", [P, D])
        wq_s = sb("wq_s", [P, 2, INNER], F32R)
        wk_s = sb("wk_s", [P, 2, INNER], F32R)
        wv_s = sb("wv_s", [P, 2, INNER], F32R)
        pair_mask = sb("pair_mask", [P, 2])
        wo = sb("wo", [P, PAIRS, D])
        cos_t = sb("cos_t", [P, S])
        sin_t = sb("sin_t", [P, S])
        w_l1kv = sb("w_l1kv", [P, 2 * D])
        w_l1q = sb("w_l1q", [P, D])
        w_dense = sb("w_dense", [P, D])
        keep = sb("keep", [P, B + 1, KB])
        cols = sb("cols", [P, 9])
        LAT_G, LAT_B, CTX_G, CTX_B, FFN_G, FFN_B, BO_COL, BS_COL, BI_COL = range(9)
        b_proj = sb("b_proj", [P, D])
        b_wo = sb("b_wo", [P, D])
        l1_g = sb("l1_g", [P, D])
        l1_b = sb("l1_b", [P, D])
        b_dense = sb("b_dense", [P, D])
        b_ffn = sb("b_ffn", [P, D])

        xb = sb("xb", [P, QT, D])
        cb = sb("cb", [P, KB, D])
        x_t = sb("x_t", [P, T])
        q0 = sb("q0", [P, T])
        k0 = sb("k0", [P, T])
        km = sb("km", [P, 2, G, T])
        vm = sb("vm", [P, QT, G, P])
        prob0 = sb("prob0", [P, H, P])
        prob1 = sb("prob1", [P, H, T])
        row_max = sb("row_max", [P, QT, G, G])
        neg_max = sb("neg_max", [P, QT, G, G])
        row_sum = sb("row_sum", [P, QT, G, G])
        row_rec = sb("row_rec", [P, QT, H, HD])
        rec_t = sb("rec_t", [P, T])
        xbp = sb("xbp", [P, QT, D])
        x1 = sb("x1", [P, QT, D])
        pt = sb("pt", [P, 4, 512])
        o0 = sb("o0", [P, T])
        ctx_t = sb("ctx_t", [P, S])
        cn = sb("cn", [P, KB, D])
        cn_raw = ctx_t
        cn_s = sb("cn_s", [P, 2, S], F32R)
        kv1 = sb("kv1", [P, 2 * KB, D])
        k1 = sb("k1", [P, KB, D])
        v1 = sb("v1", [P, KB, D + 1])
        stats = sb("stats", [P, 8, 6])
        mv = sb("mv", [P, 8, 2])
        var_eps = sb("var_eps", [P, 8])
        rstd = sb("rstd", [P, 8])
        y = sb("y", [P, QT, D])
        lat = sb("lat", [P, QT, D])
        lat_raw = x_t
        lat_s = sb("lat_s", [P, 2, T], F32R)
        k_raw = sb("k_raw", [P, S])
        k_sin = sb("k_sin", [P, S])
        kr_s = sb("kr_s", [P, 2, 2, S], F32R)
        q_raw = sb("q_raw", [P, T])
        qm_s = sb("qm_s", [P, 2, 2, 2, T], F32R)
        v = sb("v", [P, 2, KB, 2 * P])
        prob = sb("prob", [P, 2, KB, 512])
        psum = sb("psum", [P, 2, 512])
        o_rec = sb("o_rec", [P, T])
        on = sb("on", [P, PAIRS, T])

        x2 = sb("x2", [P, NT + QT, D])
        kv_sums = sb("kv_sums", [P, B + 1, D + 1])

        mats = km[:, :, :, :].rearrange("p j g t -> p (j g t)").rearrange("p (k d) -> p k d", d=D)
        M_WI, M_WS, M_WO, M_A, M_B, M_C, M_FFN0, M_FFN1 = range(8)
        f_t = prob[:, 0, :, :].rearrange("p k c -> p (k c)")
        x3_t = prob[:, 1, :, :].rearrange("p k c -> p (k c)")
        hid = prob1[:, 0:8, :].rearrange("p k c -> p (k c)")
        x5 = prob1[:, 8:16, :].rearrange("p k (t d) -> p (k t) d", d=D)
        tail = pt[:, :, :].rearrange("p k (t d) -> p (k t) d", d=D)
        a_t, b_t, wo_t, bwi_t, aws_t, g_t, gws_t, w_round, kvm, ksm = (tail[:, k, :] for k in range(10))
        pre_t = psum[:, 0, 0:T]
        x4_t = psum[:, 0, T:2 * T]
        q1_t = psum[:, 1, 0:T]
        att_t = cn_raw[:, :]
        den = o_rec[:, :]
        att = on[:, :, :].rearrange("p k (i d) -> p (k i) d", d=D)
        mixed = prob0[:, :, :]
        f_all = v[:, :, :, :].rearrange('p g k c -> p (g k c)').rearrange('p (t d) -> p t d', d=D)
        x4_all = f_all
        x4 = x1
        out_t = cn[:, :, :]
        q1 = lat
        one_row = sin_t[0:1, :]
        c_rows = rec_t[0:1, 0:2 * D]
        t4 = cn[:, :, :]
        t4b = cb[:, :, :]
        settled = sb("settled", [P, 32])
        small = sb("small", [P, 16])
        F_MAX, F_SUM, F_ALL, BETA, INV_BETA, F_INV, F_SCALE, OUT_BIAS, Q_MAX, Q_SCALE, Q_INV = 0, 4, 5, 6, 7, 8, 9, 10, 11, 13, 15
        diag2 = sb("diag2", [2, 4])
        level = f_all
        q8 = prob[:, 0, 0:2, :].bitcast(BF16).rearrange("p k (t d) -> p (k t) d", d=D)
        w8 = sb("w8", [P, 2, D], BF16)
        q8_t = sb("q8_t", [P, 512], BF16)
        ident16 = sb("ident16", [P, P], BF16)

        mats_in = sem("mats_in")
        ta_full = sem("ta_full")
        ta_free = sem("ta_free")
        td_full = sem("td_full")
        td_free = sem("td_free")
        f_quantized = sem("f_quantized")
        x3_ready = sem("x3_ready")
        prep_ready = sem("prep_ready")
        c_ready = sem("c_ready")
        z_ready = sem("z_ready")
        h_ready = sem("h_ready")
        x4_ready = sem("x4_ready")
        q1_ready = sem("q1_ready")
        kvm_ready = sem("kvm_ready")
        att_ready = sem("att_ready")
        att_out = sem("att_out")
        mixed_in = sem("mixed_in")
        red_ready = sem("red_ready")
        ident16_ready = sem("ident16_ready")
        q8_ready = sem("q8_ready")
        x5b_ready = sem("x5b_ready")
        out_ready = sem("out_ready")
        consts_made = sem("consts_made")
        mask_ready = sem("mask_ready")
        weights_in = sem("weights_in")
        scratch_out = sem("scratch_out")
        bias_in = sem("bias_in")
        x_in = sem("x_in")
        ctx_in = sem("ctx_in")
        a_full = sem("a_full")
        a_free = sem("a_free")
        d_full = sem("d_full")
        d_free = sem("d_free")
        var_ready = sem("var_ready")
        rstd_ready = sem("rstd_ready")
        dve_chain = sem("dve_chain")
        pool_chain = sem("pool_chain")
        swap_ready = sem("swap_ready")
        trig_ready = sem("trig_ready")
        km_ready = sem("km_ready")
        cn_ready = sem("cn_ready")
        cn_split = sem("cn_split")
        lat_split = sem("lat_split")
        p_full = sem("p_full")
        y_full = sem("y_full")
        y_free = sem("y_free")
        p_free = sem("p_free")
        weights_high = sem("weights_high")
        weights_split = sem("weights_split")
        ksin_ready = sem("ksin_ready")
        ksum_ready = sem("ksum_ready")
        kr_high = sem("kr_high")
        q_split = sem("q_split")
        neg_ready = sem("neg_ready")
        exp0_done = sem("exp0_done")
        rec0_ready = sem("rec0_ready")
        o0_full = sem("o0_full")
        o0_ready = sem("o0_ready")
        lat_ready = sem("lat_ready")
        kr_ready = sem("kr_ready")
        unit_full = sem("unit_full")
        exp_done = sem("exp_done")
        clamped = sem("clamped")
        psum_ready = sem("psum_ready")
        o_full = sem("o_full")
        on_ready = sem("on_ready")
        xbp_ready = sem("xbp_ready")
        x1_ready = sem("x1_ready")
        x1p_ready = sem("x1p_ready")
        k1_ready = sem("k1_ready")
        x2_ready = sem("x2_ready")
        f_ready = sem("f_ready")
        out_done = sem("out_done")

        scratch = nc.dram_tensor("bias_scratch", [H, SCRATCH], F32).ap()

        att_dram = nc.dram_tensor("att_scratch", [B, T, D], F32).ap()

        rel = prob0[0:WINDOW + 1, 0, 0:H]
        rel_row = prob1[0:H, 8:10, :].rearrange("p a b -> p (a b)")[:, 0:SCRATCH]
        w_nat = prob1[:, 2:4, :].rearrange("p a (b c) -> p (a b) c", c=P)
        trig_nat = prob1[:, 6, :].rearrange("p (t k d) -> p t k d", t=2, k=KB)
        trig_rep = km[:, :, 0:2, :].rearrange("p t a (b r d) -> p t (a b) r d", b=2, r=4)
        wkv_nat = prob[:, 0, :, :].rearrange("p k c -> p (k c)")
        wq_nat = prob[:, 1, 0:2, :].rearrange("p k c -> p (k c)")

        block = ctx.enter_context(nc.Block())

        SETUP_LOADS = 29

        @block.sync
        def _(sp):
            loads = [0]

            def load(dst, src, slow=False):
                loads[0] += 1
                sp.dma_start(dst, src, allow_slow_non_contiguous=slow).then_inc(weights_in, 16)

            def col(name, k):
                load(cols[:, k:k + 1], a[name].rearrange("(p o) -> p o", o=1), slow=True)

            def row(name, dst):
                load(dst[:, :], rows(a[name], (0, P), 0, [(1, D)]))

            load(rel, a["L0_attn_rel_bias"][MAX_REL:MAX_REL + WINDOW + 1, :])
            load(w_nat[:, 0:3, :], a["L0_attn_w_qkv"].rearrange("(k p) c -> p k c", p=P))
            load(w_nat[:, 3, :], a["L0_attn_w_proj"])
            load(trig_nat[:, 0], a["L0_xattn_cos"].rearrange("(k p) d -> p k d", p=P))
            load(trig_nat[:, 1], a["L0_xattn_sin"].rearrange("(k p) d -> p k d", p=P))
            sp.dma_start(xb[:, :, :], a["x"][0].rearrange("(k p) d -> p k d", p=P)).then_inc(x_in, 16)
            sp.dma_start(cb[:, :, :], a["ctx_1024"][0].rearrange("(k p) d -> p k d", p=P)).then_inc(ctx_in, 16)
            load(w_l1kv[:, 0:D], a["L1_xattn_wk"])
            load(w_l1kv[:, D:2 * D], a["L1_xattn_wv"])
            load(wkv_nat, a["L0_xattn_Wkv"])
            load(wq_nat, a["L0_xattn_Wq"])
            load(wo[:, :, :], a["L0_xattn_Wo"].rearrange("(k p) d -> p k d", p=P))
            load(w_l1q[:, :], a["L1_xattn_wq"])
            load(w_dense[:, :], a["L1_xattn_dense_w"])
            load(keep[:, 0:B, :], a["mask_BxS2_ff1"].rearrange("b (k p) -> p b k", p=P), slow=True)
            load(keep[:, B, :], a["mask_BxS2_ff1"][0].rearrange("(k p) -> p k", p=P), slow=True)
            col("L0_xattn_ln_lat_g", LAT_G)
            col("L0_xattn_ln_lat_b", LAT_B)
            col("L0_xattn_ln_ctx_g", CTX_G)
            col("L0_xattn_ln_ctx_b", CTX_B)
            col("L0_ffn_ln_gamma", FFN_G)
            col("L0_ffn_ln_beta", FFN_B)
            col("L1_attn_bo", BO_COL)
            col("L1_attn_bs", BS_COL)
            col("L1_attn_bi", BI_COL)
            row("L0_attn_b_proj", b_proj)
            row("L0_xattn_bo", b_wo)
            row("L1_xattn_ln_gamma", l1_g)
            row("L1_xattn_ln_beta", l1_b)
            row("L1_xattn_dense_b", b_dense)
            row("L1_ffn_bias", b_ffn)
            assert loads[0] == SETUP_LOADS, loads
            sp.wait_ge(d_free, 2)
            sp.dma_start(scratch, rel_row).then_inc(scratch_out, 16)
            sp.wait_ge(scratch_out, 16)
            sp.dma_start(bias_mask[:, :, :], rows(scratch, (1, P), 0, [(SCRATCH, H), (1, BAND)])).then_inc(bias_in, 16)
            def load_next(b, src):
                sp.wait_ge(a_free, n(b, ACT_JOBS, SETUP_A + A_X + 1))
                sp.wait_ge(xbp_ready, n(b, 1, 1))
                sp.dma_start(xb[:, :, :], a["x"][src].rearrange("(k p) d -> p k d", p=P)).then_inc(x_in, 16)
                sp.wait_ge(a_free, n(b, ACT_JOBS, SETUP_A + A_CTX + 1))
                sp.wait_ge(cn_ready, n(b, 1, 1))
                sp.dma_start(cb[:, :, :], a["ctx_1024"][src].rearrange("(k p) d -> p k d", p=P)).then_inc(ctx_in, 16)

            with sp.Fori(1, B) as b:
                load_next(b - 1, b)
            load_next(B - 1, 0)
            sp.wait_ge(y_full, B)
            for k, name in ((M_WI, "L1_attn_Wi"), (M_WS, "L1_attn_Ws"), (M_WO, "L1_attn_Wo"), (M_A, "L1_attn_A"),
                            (M_B, "L1_attn_B"), (M_C, "L1_attn_C"), (M_FFN0, "L0_ffn_weight"),
                            (M_FFN1, "L1_ffn_weight")):
                sp.dma_start(mats[:, k, :], a[name]).then_inc(mats_in, 16)
            per = P // H
            for b in range(B):
                sp.wait_ge(att_ready, b + 1)
                sp.dma_start(att_dram[b].rearrange("(q p) d -> p q d", p=P), att[:, b * QT:(b + 1) * QT, :]
                             ).then_inc(att_out, 16)
                sp.wait_ge(att_out, 16 * (b + 1))
                for q in range(QT):
                    for h in range(per):
                        sp.dma_start(mixed[H * h:H * (h + 1), b * QT + q, :].rearrange("m (i e) -> m i e", e=HD),
                                     rows(att_dram, (H * D, H), b * T * D + (q * per + h) * HD, [(D, H), (1, HD)])
                                     ).then_inc(mixed_in, 16)
            out_v = out.rearrange("b (q p) d -> p (b q) d", p=P)
            for k in range(4):
                sp.wait_ge(out_ready, k + 1)
                sp.dma_start(out_v[:, 4 * k:4 * k + 4, :], f_all[:, 4 * k:4 * k + 4, :]).then_inc(out_done, 16)
            sp.wait_ge(out_done, 64)

        @block.gpsimd
        def _(pool):
            chain = Chain(pool, pool_chain)
            link = chain.link
            g = nc.gpsimd
            g.memset(ones[:, :], 1.0)
            g.memset(minus_half[:, :], -0.5)
            for k, eps in enumerate(EPSILONS):
                g.memset(epsilons[:, k, :], eps)
            g.memset(ident[:, :], 0.0)
            g.memset(head_mask[:, :], 1.0)
            g.memset(quad_mask[:, :, :], 0.0)
            link(g.memset(v1[:, :, D:D + 1], 1.0))
            g.affine_select(out=ident[:, :], in_=ident[:, :], compare_op=ALU.not_equal, fill=1.0, base=0,
                            pattern=[[-1, P]], channel_multiplier=1)
            for j in range(G):
                g.memset(quad_mask[:, j, :].rearrange("p (g j d) -> p g j d", g=G, j=G)[:, :, j, :], 1.0)
            link(g.affine_select(out=head_mask[:, :], in_=head_mask[:, :], compare_op=ALU.is_ge, fill=0.0, base=0,
                                 pattern=[[-HD, H]], channel_multiplier=1))
            g.affine_select(out=head_mask[:, :], in_=head_mask[:, :], compare_op=ALU.is_ge, fill=0.0, base=HD - 1,
                            pattern=[[HD, H]], channel_multiplier=-1).then_inc(consts_made, 1)
            pool.wait_ge(consts_made, 1)
            g.tensor_copy(mask_jg[:, :].rearrange("p (j g) -> p g j", g=G),
                          head_mask[:, :].rearrange("p (g j) -> p g j", j=G)).then_inc(mask_ready, 1)
            pool.wait_ge(mask_ready, 1)
            def rstd_of(before, k, count, eps):
                pool.wait_ge(var_ready, before + k + 1)
                link(g.tensor_tensor(var_eps[:, 0:count], mv[:, 0:count, 1],
                                     epsilons[:, EPSILONS.index(eps), 0:count], ALU.add))
                g.tensor_tensor(rstd[:, 0:count], var_eps[:, 0:count], minus_half[:, 0:count],
                                ALU.pow).then_inc(rstd_ready, 1)

            def self_attention(b, slot, norms, after=True):
                if slot == S_X:
                    pool.wait_ge(x_in, n(b, 16, 16))
                    if after:
                        pool.wait_ge(x1_ready, b)
                    g.tensor_tensor(xbp[:, :, :], xb[:, :, :], b_proj[:, :].unsqueeze(1).broadcast_to([P, QT, D]),
                                    ALU.add).then_inc(xbp_ready, 1)
                if slot == S_CTX:
                    rstd_of(norms, 0, KB, EPS_LN)
                if slot in S_NORM:
                    rstd_of(norms, 1 + S_NORM.index(slot), KB, 1e-6)
                if slot == S_PROJ:
                    rstd_of(norms, 3, QT, EPS_LN)
                    rstd_of(norms, 4, QT, EPS_LN)
                    pool.wait_ge(x1_ready, n(b, 1, 1))
                    x2_b = x2[:, bass.ds(b * QT, QT), :]
                    g.tensor_tensor(x2_b, x1[:, :, :], b_wo[:, :].unsqueeze(1).broadcast_to([P, QT, D]),
                                    ALU.add).then_inc(x1p_ready, 1)

            def rotate(prep):
                pool.wait_ge(ksin_ready, prep)
                link(g.tensor_tensor(k_raw[:, :], k_raw[:, :], cos_t[:, :], ALU.mult))
                g.tensor_tensor(k_raw[:, :], k_raw[:, :], k_sin[:, :], ALU.add).then_inc(ksum_ready, 1)

            pool.wait_ge(weights_in, 16 * SETUP_LOADS)
            first = chain.k
            chain.start(first)
            for slot in range(SLOTS):
                self_attention(0, slot, 0, after=False)
            assert chain.k == SELF_POOL_LINKS, chain.k
            chain.start(first + SELF_POOL_LINKS)
            rotate(1)
            rotate(2)
            first += SELF_POOL_LINKS + 2
            with pool.Fori(0, B) as b:
                chain.start(first + b * POOL_LINKS)
                norms = n(b, NORMS, SELF_NORMS)
                for p in range(PAIRS):
                    for i in range(4):
                        self_attention(b + 1, PER_PAIR * p + i, norms)
                    pool.wait_ge(clamped, n(b, HALVES, 2 * p + 1))
                    if p >= 2:
                        pool.wait_ge(o_full, n(b, PAIRS, p - 1))
                    pp = prob[:, p % 2]
                    link(g.tensor_tensor(psum[:, p % 2, :], pp[:, 0, :], pp[:, 1, :], ALU.add))
                    pool.wait_ge(clamped, n(b, HALVES, 2 * p + 2))
                    link(g.tensor_tensor(psum[:, p % 2, :], psum[:, p % 2, :], pp[:, 2, :], ALU.add))
                    g.tensor_tensor(psum[:, p % 2, :], psum[:, p % 2, :], pp[:, 3, :],
                                    ALU.add).then_inc(psum_ready, 1)
                    rotate(n(b, PAIRS, p + 3))
                    for i in range(4, PER_PAIR):
                        self_attention(b + 1, PER_PAIR * p + i, norms)
                rstd_of(norms, 5, QT, EPS_LN)
                assert chain.k == POOL_LINKS, chain.k
            base = first + B * POOL_LINKS
            chain.start(base)
            g.tensor_copy(ident16[:, :], ident[:, :]).then_inc(ident16_ready, 1)
            pool.wait_ge(y_full, B)
            g.memset(one_row, 1.0).then_inc(ident16_ready, 1)
            norms = SELF_NORMS + B * NORMS
            for k in range(4):
                rstd_of(norms, k, 4, 1e-3)
            for k in range(4):
                rstd_of(norms + 4, k, 4, EPS_LN)
            base += chain.k
            with pool.Fori(0, B) as b:
                chain.start(base + b * TAIL_POOL_LINKS)
                late = norms + 8
                for k, eps in enumerate((EPS_LN, 1e-6)):
                    rstd_of(n(b, TAIL_NORMS, late), k, QT, eps)
                assert chain.k == TAIL_POOL_LINKS, chain.k
            chain.start(base + B * TAIL_POOL_LINKS)
            late = SELF_NORMS + B * NORMS + 8 + B * TAIL_NORMS
            for k in range(4):
                rstd_of(0, late + 2 * k, 4, 1e-6)
                rstd_of(0, late + 2 * k + 1, 4, EPS_LN)
            late += 8
            pool.wait_ge(x2_ready, B + 4)
            g.tensor_tensor(x2[:, 0:NT, :], x5[:, :, :], b_ffn[:, :].unsqueeze(1).broadcast_to([P, NT, D]),
                            ALU.add).then_inc(x5b_ready, 1)
            for k in range(4):
                rstd_of(0, late + k, 4, EPS_LN)

        @block.scalar
        def _(act):
            s = nc.scalar

            act.wait_ge(weights_in, 16 * SETUP_LOADS)
            act.wait_ge(mask_ready, 1)
            act.wait_ge(a_full, 1)
            s.activation(sin_t[0:DH, :], bank_a[0:DH, :], ACT.Identity)
            s.activation(sin_t[DH:P, :], bank_a[DH:P, :], ACT.Identity, scale=-1.0).then_inc(a_free, 1)
            natural = "c (p h t d) -> c p t h d"
            for wide, nat in ((wk_s, wkv_nat[:, 0:INNER]), (wq_s, wq_nat)):
                for t in range(2):
                    s.activation(wide[:, 0, :].rearrange("c (p t h d) -> c p t h d", t=2, h=2, d=HALF)[:, :, t],
                                 nat.rearrange(natural, h=2, t=2, d=HALF)[:, :, t], ACT.Identity)
            s.activation(wv_s[:, 0, :], wkv_nat[:, INNER:2 * INNER], ACT.Identity).then_inc(weights_high, 1)

            def evacuate(b, job, dst, src, free=True, **kw):
                act.wait_ge(a_full, n(b, ACT_JOBS, SETUP_A + job + 1))
                i = s.activation(dst, src, ACT.Identity, **kw)
                if free:
                    i.then_inc(a_free, 1)

            def self_attention(b, slot):
                if slot == S_X:
                    evacuate(b, A_X, x_t[:, :], bank_a[:, 0:T])
                if slot == S_CTX:
                    evacuate(b, A_CTX, ctx_t[:, :], bank_a[:, :])
                if slot == S_K:
                    evacuate(b, A_K, k0[:, :], bank_a[:, 0:T])
                if slot in (S_KV_A, S_KV_B):
                    k = slot - S_KV_A
                    evacuate(b, A_KV + k, kv1[:, 4 * k:4 * k + 4, :].rearrange("p k d -> p (k d)"), bank_a[:, :])
                if slot in S_MASKED:
                    j = S_MASKED.index(slot)
                    if j == 0:
                        act.wait_ge(a_free, n(b, ACT_JOBS, SETUP_A + A_K + 1))
                    if j >= 2:
                        act.wait_ge(d_full, n(b, DVE_JOBS, SETUP_D + D_SCORE + 3 * (j - 1)))
                    for g in range(G):
                        last = s.activation(km[:, j % 2, g, :], k0[:, :], ACT.Identity,
                                            scale=mask_jg[:, G * j + g:G * j + g + 1])
                    last.then_inc(km_ready, 1)
                if slot in S_EXP:
                    half, i = divmod(S_EXP.index(slot), 6)
                    heads = [(qt, j, g) for qt in range(QT) for j in (2 * half, 2 * half + 1) for g in range(G)]
                    if i == 0:
                        act.wait_ge(neg_ready, n(b, 2, half + 1))
                    for qt, j, g in heads[i * 16 // 6:(i + 1) * 16 // 6]:
                        h = 4 * g + j
                        pr = prob0[:, h, :] if qt == 0 else prob1[:, h, WINDOW:T]
                        last = s.activation(pr, pr, ACT.Exp, bias=neg_max[:, qt, j, g:g + 1],
                                            accum_out=row_sum[:, qt, j, g:g + 1])
                    if i == 5:
                        last.then_inc(exp0_done, 1)
                at = slot - S_TURN
                if 0 <= at < TURNS:
                    evacuate(b, A_TURN + at, pt[:, at % 4, :], bank_a[:, :])
                if slot == S_REC:
                    evacuate(b, A_REC, rec_t[:, :], bank_a[:, 0:T])
                if slot == S_LAT:
                    by_feature = dict(scale=cols[:, LAT_G:LAT_G + 1], bias=cols[:, LAT_B:LAT_B + 1])
                    evacuate(b, A_LAT, lat_raw[:, :], bank_a[:, 0:T], free=False, **by_feature)
                    s.activation(lat_s[:, 0, :], bank_a[:, 0:T], ACT.Identity, **by_feature).then_inc(a_free, 1)
                if slot == S_CN:
                    by_feature = dict(scale=cols[:, CTX_G:CTX_G + 1], bias=cols[:, CTX_B:CTX_B + 1])
                    evacuate(b, A_CN, cn_raw[:, :], bank_a[:, :], free=False, **by_feature)
                    s.activation(cn_s[:, 0, :], bank_a[:, :], ACT.Identity, **by_feature).then_inc(a_free, 1)

            def keys(job, prep, after=True):
                act.wait_ge(p_full, job)
                if after:
                    act.wait_ge(kr_ready, prep - 1)
                s.activation(k_raw[:, :], bank_p, ACT.Identity).then_inc(p_free, 1)

            def keys_high(prep, buf):
                act.wait_ge(ksum_ready, prep)
                s.activation(kr_s[:, buf, 0, :], k_raw[:, :], ACT.Identity).then_inc(kr_high, 1)

            def values(job, group, half):
                act.wait_ge(p_full, job)
                s.activation(v[:, group % 2, 2 * half:2 * half + 2, :],
                             bank_p.rearrange("p (k c) -> p k c", k=2), ACT.Identity).then_inc(p_free, 1)

            def queries(job, prep, buf, after=True):
                act.wait_ge(p_full, job)
                if after:
                    act.wait_ge(q_split, prep - 1)
                s.activation(q_raw[:, :], bank_p[:, 0:T], ACT.Identity)
                for h in range(2):
                    last = s.activation(qm_s[:, buf, 0, h, :], bank_p[:, 0:T], ACT.Identity,
                                        scale=pair_mask[:, h:h + 1])
                last.then_inc(p_free, 1)

            for slot in range(SLOTS):
                self_attention(0, slot)
            keys(1, 1, after=False)
            for half in range(2):
                values(2 + half, 0, half)
            queries(4, 1, 0, after=False)
            keys_high(1, 0)
            keys(5, 2)
            with act.Fori(0, B) as b:
                for p in range(PAIRS):
                    def exps(kb):
                        act.wait_ge(unit_full, n(b, UNITS, KB * p + kb + 1))
                        if p >= 2 and kb == 0:
                            act.wait_ge(o_full, n(b, PAIRS, p - 1))
                        s.activation(prob[:, p % 2, kb, :], sc[:, kb % 2, :], ACT.Exp,
                                     scale=DH ** -0.5).then_inc(exp_done, 1)

                    def slots(lo, hi):
                        for i in range(lo, hi):
                            self_attention(b + 1, PER_PAIR * p + i)

                    def prep(make, kind, *args):
                        make(n(b, PREP_JOBS, FIRST_PREP + PREP.index((p, kind)) + 1), *args)

                    def next_values(half):
                        if p % 2 == 1:
                            prep(values, f"values {half}", (p + 1) // 2, half)

                    last_pair = p == PAIRS - 1
                    exps(0)
                    slots(0, 1)
                    exps(1)
                    slots(1, 2)
                    if not last_pair:
                        next_values(0)
                    exps(2)
                    if not last_pair:
                        next_values(1)
                    slots(2, 3)
                    if not last_pair:
                        prep(queries, "queries", n(b, PAIRS, p + 2), (p + 1) % 2)
                    keys_high(n(b, PAIRS, p + 2), (p + 1) % 2)
                    slots(3, 4)
                    prep(keys, "keys", n(b, PAIRS, p + 3))
                    exps(3)
                    slots(4, 6)
                for half in range(2):
                    next_values(half)
                prep(queries, "queries", n(b, PAIRS, PAIRS + 1), 0)

            def late(job, dst, src, **kw):
                act.wait_ge(ta_full, job)
                s.activation(dst, src, ACT.Identity, **kw).then_inc(ta_free, 1)

            late(1, tail[:, 0:3, :].rearrange("p k d -> p (k d)"), bank_a[:, 0:3 * D])
            for k in range(4):
                late(2 + k, f_t[:, 512 * k:512 * k + 512], bank_a[:, :], scale=cols[:, FFN_G:FFN_G + 1],
                     bias=cols[:, FFN_B:FFN_B + 1])
            for k in range(4):
                late(6 + k, x3_t.rearrange("p (t b) -> p b t", b=B)[:, 2 * k:2 * k + 2, :],
                     bank_a[:, :].rearrange("p (b t) -> p b t", b=2))
            act.wait_ge(c_ready, 1)
            s.activation(hid[:, 0:B], cf[:, 0:B], ACT.Tanh).then_inc(h_ready, 1)
            with act.Fori(0, (T - 1) // STEPS) as part:
                t0 = part * STEPS + 1
                for i in range(STEPS):
                    act.wait_ge(z_ready, t0 + i)
                    s.activation(hid[:, bass.ds((t0 + i) * B, B)], cf[:, bass.ds((t0 + i) * B, B)],
                                 ACT.Tanh).then_inc(h_ready, 1)
            with act.Fori(0, B) as b:
                job = 10 + b * TAIL_A
                late(job, pre_t, bank_a[:, 0:T], bias=small[:, OUT_BIAS:OUT_BIAS + 1])
                late(job + 1, x4_t, bank_a[:, 0:T])
                late(job + 2, q1_t, bank_a[:, 0:T])
            job = 10 + B * TAIL_A
            for k in range(4):
                late(job + k, att_t, bank_a[:, :])
            job += 4
            for k in range(4):
                act.wait_ge(ta_full, job + k)
                s.activation(q8_t[:, :], bank_a[:, 0:256].bitcast(BF16), ACT.Identity).then_inc(ta_free, 1)

        @block.vector
        def _(dve):
            chain = Chain(dve, dve_chain)
            link = chain.link
            w = nc.vector

            w.memset(settled[:, :], 0.0).then_inc(y_free, 1)
            for block_row in range(4):
                for h in range(2):
                    lo = HALF * block_row
                    w.memset(pair_mask[lo:lo + HALF, h:h + 1], 1.0 if block_row % 2 == h else 0.0)
            dve.wait_ge(weights_in, 16 * SETUP_LOADS)
            for t in range(2):
                w.tensor_copy(trig_rep[:, t], trig_nat[:, t].unsqueeze(2).broadcast_to([P, KB, 4, HALF]))
            w.memset(rel_row, MASKED).then_inc(trig_ready, 1)
            dve.wait_ge(trig_ready, 1)
            dve.wait_ge(d_full, 1)
            w.tensor_copy(w_qkv_t[:, :], bank_d[:, 0:3 * D])
            w.tensor_copy(w_proj_t[:, :], bank_d[:, 3 * D:4 * D]).then_inc(d_free, 1)
            dve.wait_ge(d_full, 2)
            w.tensor_copy(rel_row[:, P - 1:P + WINDOW], bank_d[0:H, 0:WINDOW + 1]).then_inc(d_free, 1)
            dve.wait_ge(d_full, 3)
            w.tensor_copy(cos_t[:, :], bank_d[:, :]).then_inc(d_free, 1)
            dve.wait_ge(bias_in, 16)
            w.memset(prob1[:, :, 0:WINDOW], 0.0)
            first = chain.k
            dve.wait_ge(weights_high, 1)
            natural = "c (p h t d) -> c p t h d"
            for wide, nat in ((wk_s, wkv_nat[:, 0:INNER]), (wq_s, wq_nat)):
                for t in range(2):
                    view = [wide[:, k, :].rearrange("c (p t h d) -> c p t h d", t=2, h=2, d=HALF)[:, :, t]
                            for k in range(2)]
                    w.tensor_tensor(view[1], nat.rearrange(natural, h=2, t=2, d=HALF)[:, :, t],
                                    view[0].bitcast(F32), ALU.subtract)
            w.tensor_tensor(wv_s[:, 1, :], wkv_nat[:, INNER:2 * INNER], wv_s[:, 0, :].bitcast(F32),
                            ALU.subtract).then_inc(weights_split, 1)

            def band_of(h, count):
                band = bias_mask[:, h, 0:count]
                return bass.AP(tensor=band.tensor, offset=band.offset + count - 1, ap=[list(band.ap[0]), [-1, count]])

            cells = [0]

            def settle():
                cells[0] = cells[0] % 31 + 1
                w.tensor_copy(settled[:, cells[0]:cells[0] + 1], settled[:, 0:1])

            def statistics(before, k, tiles):
                settle()
                for i, tile in enumerate(tiles):
                    last = w.bn_stats(stats[:, i, :], tile)
                link(last)
                settle()
                for i in range(len(tiles)):
                    last = w.bn_aggr(mv[:, i, :], stats[:, i, :])
                last.then_inc(var_ready, 1)
                dve.wait_ge(rstd_ready, before + k + 1)

            def normalize(dsts, tiles):
                for i, (dst, tile) in enumerate(zip(dsts, tiles)):
                    last = w.tensor_scalar(dst, tile, mv[:, i, 0:1], rstd[:, i:i + 1], ALU.subtract, ALU.mult)
                return last

            def bank_ready(b, job):
                dve.wait_ge(d_full, n(b, DVE_JOBS, SETUP_D + job + 1))

            def tiles_of(t, count):
                return [t[:, i, :] for i in range(count)]

            def self_attention(b, slot, norms):
                if slot == S_CTX:
                    dve.wait_ge(ctx_in, n(b, 16, 16))
                    statistics(norms, 0, tiles_of(cb, KB))
                    normalize(tiles_of(cn, KB), tiles_of(cb, KB)).then_inc(cn_ready, 1)
                if slot == S_Q:
                    bank_ready(b, 0)
                    w.tensor_scalar(q0[:, :], d_bank(0)[:, 0:T], HD ** -0.5, None, ALU.mult).then_inc(d_free, 1)
                if slot == S_V:
                    bank_ready(b, 1)
                    for t in range(QT):
                        last = w.tensor_tensor(vm[:, t],
                                               d_bank(1)[:, t * D:(t + 1) * D].unsqueeze(1).broadcast_to([P, G, D]),
                                               quad_mask[:, :, :], ALU.mult)
                    last.then_inc(d_free, 1)
                if slot in S_SCORE:
                    at = S_SCORE.index(slot)
                    j, i = divmod(at, 3)
                    bank_ready(b, D_SCORE + at)
                    settle()
                    if i == 0:
                        for g in range(G):
                            h = 4 * g + j
                            last = w.tensor_tensor_reduce(prob0[:, h, :], d_bank(D_SCORE + at)[:, g * P:(g + 1) * P],
                                                          band_of(h, P), 1.0, 0.0, ALU.add, ALU.max,
                                                          row_max[:, 0, j, g:g + 1])
                    else:
                        for k in range(2):
                            g = 2 * (i - 1) + k
                            h = 4 * g + j
                            last = w.tensor_tensor_reduce(prob1[:, h, WINDOW:T],
                                                          d_bank(D_SCORE + at)[:, k * BAND:(k + 1) * BAND],
                                                          band_of(h, BAND), 1.0, 0.0, ALU.add, ALU.max,
                                                          row_max[:, 1, j, g:g + 1])
                    last.then_inc(d_free, 1)
                    if at % 6 == 5:
                        half = at // 6
                        dve.wait_ge(d_free, n(b, DVE_JOBS, SETUP_D + D_SCORE + at + 1))
                        w.tensor_scalar(neg_max[:, :, 2 * half:2 * half + 2, :], row_max[:, :, 2 * half:2 * half + 2, :],
                                        -1.0, None, ALU.mult).then_inc(neg_ready, 1)
                if slot in S_NORM:
                    k = S_NORM.index(slot)
                    tiles = tiles_of(kv1[:, KB * k:KB * (k + 1), :], KB)
                    dve.wait_ge(a_free, n(b, ACT_JOBS, SETUP_A + A_KV + k + 1))
                    statistics(norms, 1 + k, tiles)
                    link(normalize(tiles, tiles))
                if slot in (S_SCALE, S_SHIFT):
                    row, op = (l1_g, ALU.mult) if slot == S_SCALE else (l1_b, ALU.add)
                    link(w.tensor_tensor(kv1[:, :, :], kv1[:, :, :],
                                         row[:, :].unsqueeze(1).broadcast_to([P, 2 * KB, D]), op))
                if slot == S_RELU:
                    kv1_v = kv1[:, :, :].rearrange("p (k t) d -> p k t d", t=2)
                    keep_b = keep[:, b, :].unsqueeze(2).broadcast_to([P, KB, D])
                    link(w.tensor_scalar(k1[:, :, :], kv1_v[:, :, 0, :], 0.0, 1e-6, ALU.max, ALU.add))
                    w.tensor_tensor(v1[:, :, 0:D], kv1_v[:, :, 1, :], keep_b, ALU.mult)
                    w.tensor_tensor(k1[:, :, :], k1[:, :, :], keep_b, ALU.mult).then_inc(k1_ready, 1)
                if slot == S_SUMS:
                    dve.wait_ge(exp0_done, n(b, 2, 2))
                    for qt in range(QT):
                        last = w.reciprocal(row_rec[:, qt].rearrange("p (g j) d -> p j g d", j=G),
                                            row_sum[:, qt].unsqueeze(3).broadcast_to([P, G, G, HD]))
                    last.then_inc(rec0_ready, 1)
                if slot == S_PROJ:
                    dve.wait_ge(o0_full, n(b, 1, 1))
                    dve.wait_ge(a_free, n(b, ACT_JOBS, SETUP_A + A_REC + 1))
                    w.tensor_tensor(o0[:, :], o0_bank[:, 0:T], rec_t[:, :], ALU.mult).then_inc(o0_ready, 1)
                    bank_ready(b, D_PROJ)
                    dve.wait_ge(xbp_ready, n(b, 1, 1))
                    w.tensor_tensor(y[:, :, :], d_bank(D_PROJ)[:, 0:QT * D].rearrange("p (q d) -> p q d", q=QT), xbp[:, :, :],
                                    ALU.add).then_inc(d_free, 1)
                    dve.wait_ge(d_free, n(b, DVE_JOBS, SETUP_D + D_PROJ + 1))
                    statistics(norms, 3, tiles_of(y, QT))
                    normalize(tiles_of(x1, QT), tiles_of(y, QT)).then_inc(x1_ready, 1)
                    dve.wait_ge(x1_ready, n(b, 1, 1))
                    statistics(norms, 4, tiles_of(x1, QT))
                    normalize(tiles_of(lat, QT), tiles_of(x1, QT)).then_inc(lat_ready, 1)
                if slot == S_KV:
                    bank_ready(b, D_KV)
                    settle()
                    w.tensor_copy(kv_sums[:, b, :], d_bank(D_KV)[:, 0:D + 1]).then_inc(d_free, 1)
                if slot == S_LAT:
                    dve.wait_ge(a_free, n(b, ACT_JOBS, SETUP_A + A_LAT + 1))
                    w.tensor_tensor(lat_s[:, 1, :], lat_raw[:, :], lat_s[:, 0, :].bitcast(F32),
                                    ALU.subtract).then_inc(lat_split, 1)
                if slot == S_CN:
                    dve.wait_ge(a_free, n(b, ACT_JOBS, SETUP_A + A_CN + 1))
                    w.tensor_tensor(cn_s[:, 1, :], cn_raw[:, :], cn_s[:, 0, :].bitcast(F32),
                                    ALU.subtract).then_inc(cn_split, 1)

            def keys_sin(job, prep):
                dve.wait_ge(p_free, job)
                w.tensor_tensor(k_sin[0:DH, :], k_raw[DH:P, :], sin_t[DH:P, :], ALU.mult)
                w.tensor_tensor(k_sin[DH:P, :], k_raw[0:DH, :], sin_t[0:DH, :], ALU.mult).then_inc(ksin_ready, 1)

            def keys_low(prep, buf):
                dve.wait_ge(kr_high, prep)
                w.tensor_tensor(kr_s[:, buf, 1, :], k_raw[:, :], kr_s[:, buf, 0, :].bitcast(F32),
                                ALU.subtract).then_inc(kr_ready, 1)

            def queries_low(job, buf):
                dve.wait_ge(p_free, job)
                for h in range(2):
                    last = w.scalar_tensor_tensor(out=qm_s[:, buf, 1, h, :], in0=q_raw[:, :],
                                                  scalar=pair_mask[:, h:h + 1],
                                                  in1=qm_s[:, buf, 0, h, :].bitcast(F32), op0=ALU.mult,
                                                  op1=ALU.subtract)
                last.then_inc(q_split, 1)

            for slot in range(SLOTS):
                self_attention(0, slot, 0)
            assert chain.k - first == SELF_DVE_LINKS, chain.k - first
            keys_sin(1, 1)
            queries_low(4, 0)
            keys_low(1, 0)
            keys_sin(5, 2)
            first = chain.k
            with dve.Fori(0, B) as b:
                chain.start(first + b * DVE_LINKS)
                norms = n(b, NORMS, SELF_NORMS)

                def attended(p):
                    bank = pair_bank(p)
                    dve.wait_ge(o_full, n(b, PAIRS, p + 1))
                    if p >= 1:
                        dve.wait_ge(on_ready, n(b, PAIRS, p))
                    link(w.reciprocal(o_rec[:, :], bank[:, T:2 * T]))
                    w.tensor_tensor(on[:, p, :], bank[:, 0:T], o_rec[:, :], ALU.mult).then_inc(on_ready, 1)

                for p in range(PAIRS):
                    def clamp(hf):
                        dve.wait_ge(exp_done, n(b, UNITS, KB * p + 2 * hf + 2))
                        pr = prob[:, p % 2, 2 * hf:2 * hf + 2, :]
                        w.tensor_scalar(pr, pr, float(np.exp(-CLIP)), float(np.exp(CLIP)), ALU.max,
                                        ALU.min).then_inc(clamped, 1)

                    def slots(lo, hi):
                        for i in range(lo, hi):
                            self_attention(b + 1, PER_PAIR * p + i, norms)

                    def prep(make, kind, *args):
                        make(n(b, PREP_JOBS, FIRST_PREP + PREP.index((p, kind)) + 1), *args)

                    slots(0, 1)
                    clamp(0)
                    slots(1, 3)
                    if p < PAIRS - 1:
                        prep(queries_low, "queries", (p + 1) % 2)
                    keys_low(n(b, PAIRS, p + 2), (p + 1) % 2)
                    slots(3, 4)
                    clamp(1)
                    slots(4, 5)
                    prep(keys_sin, "keys", n(b, PAIRS, p + 3))
                    slots(5, 6)
                    if p >= 1:
                        attended(p - 1)
                attended(PAIRS - 1)
                prep(queries_low, "queries", 0)
                x2_b = x2[:, bass.ds(b * QT, QT), :]
                dve.wait_ge(x1p_ready, n(b, 1, 1))
                dve.wait_ge(y_full, n(b, 1, 1))
                w.tensor_tensor(y[:, :, :], ob[:, 0:QT * D].rearrange("p (q d) -> p q d", q=QT), x2_b,
                                ALU.add).then_inc(y_free, 1)
                dve.wait_ge(y_free, n(b, 1, 2))
                statistics(norms, 5, tiles_of(y, QT))
                dve.wait_ge(x1p_ready, n(b, 1, 2))
                link(normalize(tiles_of(x1, QT), tiles_of(y, QT)))
                settle()
                w.tensor_copy(x2_b, x1[:, :, :]).then_inc(x2_ready, 1)
                assert chain.k == DVE_LINKS, chain.k
            base = first + B * DVE_LINKS
            chain.start(base)

            def cell(k, m=1):
                return small[:, k:k + m]

            dve.wait_ge(y_full, B)
            dve.wait_ge(x2_ready, B)
            for k in range(4):
                tiles = tiles_of(x2[:, 4 * k:4 * k + 4, :], 4)
                statistics(SELF_NORMS + B * NORMS, k, tiles)
                normalize(tiles_of(f_all[:, 4 * k:4 * k + 4, :], 4), tiles).then_inc(f_ready, 1)
                dve.wait_ge(f_ready, k + 1)
            dve.wait_ge(mats_in, 16 * 8)
            w.tensor_reduce(cell(F_SUM), mats[:, M_FFN0, :], AX_X, ALU.add,
                            apply_absolute_value=True).then_inc(red_ready, 1)
            dve.wait_ge(td_full, 1)
            w.tensor_scalar(cell(BETA), bank_d[:, 0:1], 1.0 / (D * D), None, ALU.mult).then_inc(td_free, 1)
            dve.wait_ge(td_free, 1)
            link(w.tensor_scalar(cell(INV_BETA), cell(BETA), 1e-5, None, ALU.add))
            link(w.reciprocal(cell(INV_BETA), cell(INV_BETA)))
            link(w.tensor_scalar(w_round, mats[:, M_FFN0, :], cell(INV_BETA), ROUND, ALU.mult, ALU.add))
            link(w.tensor_scalar(w_round, w_round, ROUND, None, ALU.subtract))
            w.tensor_scalar(w_round, w_round, -1.0, 1.0, ALU.max, ALU.min).then_inc(prep_ready, 1)
            dve.wait_ge(td_full, 2)
            w.tensor_copy(tail[:, 3:6, :].rearrange("p k d -> p (k d)"), bank_d[:, 0:3 * D])
            w.tensor_copy(c_rows[:, 0:D], bank_d[0:1, 3 * D:4 * D]).then_inc(td_free, 1)
            dve.wait_ge(td_full, 3)
            w.tensor_tensor(gws_t, bank_d[:, 0:D], ident[:, :], ALU.add)
            w.tensor_copy(c_rows[:, D:2 * D], bank_d[0:1, D:2 * D])
            w.tensor_tensor(cell(OUT_BIAS), bank_d[:, 2 * D:2 * D + 1], cols[:, BO_COL:BO_COL + 1],
                            ALU.add).then_inc(td_free, 1)
            for k in range(4):
                dve.wait_ge(ta_free, 2 + k)
                last = w.tensor_reduce(cell(F_MAX + k), f_t[:, 512 * k:512 * k + 512], AX_X, ALU.max,
                                       apply_absolute_value=True)
            link(last)
            w.tensor_reduce(cell(Q_MAX), cell(F_MAX, 4), AX_X, ALU.max).then_inc(red_ready, 1)
            dve.wait_ge(td_full, 4)
            w.tensor_reduce(diag2[0:1, 0:1], bank_d[0:1, 0:P], AX_X, ALU.max).then_inc(td_free, 1)
            dve.wait_ge(td_full, 5)
            w.tensor_copy(cell(F_ALL), bank_d[:, 0:1]).then_inc(td_free, 1)
            dve.wait_ge(td_free, 5)
            w.tensor_scalar(cell(F_SCALE), cell(F_ALL), cell(BETA), 1.0 / QB, ALU.mult, ALU.mult)
            link(w.reciprocal(cell(F_INV), cell(F_ALL)))
            for k in range(4):
                part = f_t[:, 512 * k:512 * k + 512]
                link(w.tensor_scalar(part, part, QB, cell(F_INV), ALU.mult, ALU.mult))
                limit = float(np.float32(QB - 1e-5))
                w.tensor_scalar(part, part, -limit, limit, ALU.max, ALU.min).then_inc(f_quantized, 1)
            for k in range(4):
                dve.wait_ge(td_full, 6 + k)
                w.scalar_tensor_tensor(out=t4, in0=bank_d[:, :].rearrange("p (t d) -> p t d", d=D),
                                       scalar=cell(F_SCALE), in1=x2[:, 4 * k:4 * k + 4, :], op0=ALU.mult,
                                       op1=ALU.add).then_inc(td_free, 1)
                dve.wait_ge(td_free, 6 + k)
                statistics(SELF_NORMS + B * NORMS + 4, k, tiles_of(t4, 4))
                if k >= 1:
                    dve.wait_ge(ta_full, 5 + k)
                normalize(tiles_of(t4b, 4), tiles_of(t4, 4)).then_inc(x3_ready, 1)
                dve.wait_ge(x3_ready, k + 1)
            base += chain.k

            def affine(t, count):
                for row, op in ((l1_g, ALU.mult), (l1_b, ALU.add)):
                    link(w.tensor_tensor(t, t, row[:, :].unsqueeze(1).broadcast_to([P, count, D]), op))

            with dve.Fori(0, B) as b:
                chain.start(base + b * TAIL_DVE_LINKS)
                late = n(b, TAIL_NORMS, SELF_NORMS + B * NORMS + 8)
                job = 10 + b * TAIL_D
                hm = head_mask[:, :].unsqueeze(2).broadcast_to([P, H, HD])
                w.tensor_scalar(ksm.rearrange("p (h d) -> p h d", d=HD), hm, kv_sums[:, b, D:D + 1], None, ALU.mult)
                w.tensor_tensor(kvm.rearrange("p (h d) -> p h d", d=HD),
                                kv_sums[:, b, 0:D].rearrange("p (h d) -> p h d", d=HD), hm,
                                ALU.mult).then_inc(kvm_ready, 1)
                dve.wait_ge(td_full, job)
                pre = [bank_d[:, i * P:(i + 1) * P] for i in range(QT)]
                statistics(late, 0, pre)
                normalize(tiles_of(x4, QT), pre).then_inc(td_free, 1)
                dve.wait_ge(td_full, job + 1)
                statistics(late, 1, pre)
                normalize(tiles_of(q1, QT), pre).then_inc(td_free, 1)
                dve.wait_ge(td_free, job + 1)

                affine(q1[:, :, :], QT)
                w.tensor_scalar(q1[:, :, :], q1[:, :, :], 0.0, 1e-6, ALU.max, ALU.add).then_inc(q1_ready, 1)
                dve.wait_ge(td_full, job + 2)
                link(w.tensor_scalar(den, bank_d[:, T:2 * T], 1e-6, None, ALU.add))
                link(w.reciprocal(den, den))
                w.tensor_tensor(att[:, bass.ds(b * QT, QT), :].rearrange("p q d -> p (q d)"), bank_d[:, 0:T], den,
                                ALU.mult).then_inc(att_ready, 1)
                dve.wait_ge(att_ready, b + 1)
                w.tensor_copy(x4_all[:, bass.ds(b * QT, QT), :], x4[:, :, :]).then_inc(td_free, 1)
                assert chain.k == TAIL_DVE_LINKS, chain.k
            chain.start(base + B * TAIL_DVE_LINKS)
            job = 10 + B * TAIL_D
            late = SELF_NORMS + B * NORMS + 8 + B * TAIL_NORMS
            for k in range(4):
                dve.wait_ge(td_full, job + k)
                w.tensor_tensor(out_t, bank_d[:, :].rearrange("p (t d) -> p t d", d=D),
                                b_dense[:, :].unsqueeze(1).broadcast_to([P, 4, D]), ALU.add).then_inc(td_free, 1)
                dve.wait_ge(td_free, job + k)
                statistics(0, late + 2 * k, tiles_of(out_t, 4))
                link(normalize(tiles_of(out_t, 4), tiles_of(out_t, 4)))
                affine(out_t, 4)
                link(w.tensor_tensor(out_t, out_t, x4_all[:, 4 * k:4 * k + 4, :], ALU.add))
                statistics(0, late + 2 * k + 1, tiles_of(out_t, 4))
                normalize([x5[:, 4 * k + i, :] for i in range(4)], tiles_of(out_t, 4)).then_inc(x2_ready, 1)
                dve.wait_ge(x2_ready, B + k + 1)
            job += 4
            late += 8
            w.tensor_reduce(cell(Q_MAX + 1), mats[:, M_FFN1, :], AX_X, ALU.max, apply_absolute_value=True)
            w.tensor_reduce(cell(Q_MAX), x5[:, :, :], mybir.AxisListType.XY, ALU.max,
                            apply_absolute_value=True).then_inc(red_ready, 1)
            dve.wait_ge(td_full, job)
            w.tensor_reduce(diag2[0:2, 2:3], bank_d[0:2, 0:P], AX_X, ALU.max).then_inc(td_free, 1)
            dve.wait_ge(td_free, job)
            w.tensor_scalar(diag2[0:2, 0:2], ident[0:2, 0:2], diag2[0:2, 2:3], None, ALU.mult).then_inc(red_ready, 1)
            dve.wait_ge(td_full, job + 1)
            w.tensor_scalar(cell(Q_SCALE, 2), bank_d[:, 0:2], 1e-12, None, ALU.max).then_inc(td_free, 1)
            dve.wait_ge(td_free, job + 1)
            link(w.reciprocal(cell(Q_SCALE, 2), cell(Q_SCALE, 2)))
            link(w.tensor_scalar(cell(Q_SCALE, 2), cell(Q_SCALE, 2), FP8_MAX, None, ALU.mult))
            link(w.tensor_tensor(cell(Q_INV), cell(Q_SCALE), cell(Q_SCALE + 1), ALU.mult))
            link(w.reciprocal(cell(Q_INV), cell(Q_INV)))

            def round8(dst, src, lev, scale):
                link(w.tensor_scalar(src, src, scale, None, ALU.mult))
                link(w.tensor_scalar(lev.bitcast(U32), src.bitcast(U32), 0x7F800000, None, ALU.bitwise_and))
                link(w.tensor_scalar(lev, lev, FP8_MIN_NORMAL, FP8_ROUND, ALU.max, ALU.mult))
                link(w.tensor_tensor(src, src, lev, ALU.add))
                return w.tensor_tensor(dst, src, lev, ALU.subtract)

            round8(w8[:, 0, :], mats[:, M_FFN1, :], w_round, cell(Q_SCALE + 1)).then_inc(q8_ready, 1)
            dve.wait_ge(x5b_ready, 1)
            for k in range(4):
                part = x5[:, 4 * k:4 * k + 4, :]
                round8(q8[:, 4 * k:4 * k + 4, :], part, level[:, 4 * k:4 * k + 4, :],
                       cell(Q_SCALE)).then_inc(q8_ready, 1)
            dve.wait_ge(td_full, job + 2)
            w.tensor_copy(w8[:, 1, :], bank_d[:, 0:64].bitcast(BF16)).then_inc(td_free, 1)
            dve.wait_ge(q8_ready, 5)
            for k in range(4):
                dve.wait_ge(td_full, job + 3 + k)
                res = x2[:, 4 * k:4 * k + 4, :]
                w.scalar_tensor_tensor(out=res, in0=bank_d[:, :].rearrange("p (t d) -> p t d", d=D),
                                       scalar=cell(Q_INV), in1=res, op0=ALU.mult, op1=ALU.add).then_inc(td_free, 1)
                dve.wait_ge(td_free, job + 3 + k)
                statistics(0, late + k, tiles_of(res, 4))
                normalize(tiles_of(f_all[:, 4 * k:4 * k + 4, :], 4), tiles_of(res, 4)).then_inc(out_ready, 1)
                dve.wait_ge(out_ready, k + 1)

        @block.tensor
        def _(pe):
            mm = nc.tensor.matmul

            def turn(out_ap, in_ap):
                return nc.tensor.transpose(out_ap, in_ap, ident[0:in_ap.shape[0], 0:in_ap.shape[0]])

            pe.wait_ge(weights_in, 16 * SETUP_LOADS)
            pe.wait_ge(consts_made, 1)
            for k in range(4):
                last = turn(bank_d[:, k * P:(k + 1) * P], w_nat[:, k, :])
            last.then_inc(d_full, 1)
            pe.wait_ge(d_free, 1)
            pe.wait_ge(trig_ready, 1)
            turn(bank_d[0:H, 0:WINDOW + 1], rel).then_inc(d_full, 1)
            pe.wait_ge(d_free, 2)
            for t, bank in ((0, bank_d), (1, bank_a)):
                for k in range(KB):
                    last = turn(bank[:, k * P:(k + 1) * P], trig_rep[:, t, k].rearrange("p r d -> p (r d)"))
                last.then_inc(d_full if t == 0 else a_full, 1)

            def split_mm(out_ap, a_high, a_low, b_high, b_low, **kw):
                mm(out_ap, a_high, b_low, start=True, stop=False, **kw)
                mm(out_ap, a_low, b_high, start=False, stop=False, **kw)
                return mm(out_ap, a_high, b_high, start=False, stop=True, **kw)

            jobs = []
            for half in range(2):
                two = (2 * half, 2 * half + 1)
                jobs += [[(0, j, 0, g) for g in range(G)] for j in two]
                jobs += [[(1, j, kt, 2 * m + g) for kt in range(QT) for g in range(2)] for j in two for m in range(2)]

            def self_attention(b, slot):
                def a_job(job):
                    pe.wait_ge(a_free, n(b, ACT_JOBS, SETUP_A + job))

                def d_job(job):
                    pe.wait_ge(d_free, n(b, DVE_JOBS, SETUP_D + job - 1))
                    return d_bank(job)

                def weigh_values(t):
                    a_job(A_TURN + t + 1)
                    for i, (qt, j, kt, g) in enumerate(jobs[t]):
                        last = mm(o0_bank[32 * g:32 * g + 32, qt * P:(qt + 1) * P], vm[:, kt, j, 32 * g:32 * g + 32],
                                  pt[:, t % 4, i * P:(i + 1) * P], start=(j == 0 and kt == 0 and qt == 0),
                                  stop=(j == G - 1 and (qt == 0 or kt == QT - 1)), skip_group_check=True)
                    return last

                if slot == S_X:
                    pe.wait_ge(x_in, n(b, 16, 16))
                    a_job(0)
                    for t in range(QT):
                        last = turn(bank_a[:, t * P:(t + 1) * P], xb[:, t, :])
                    last.then_inc(a_full, 1)
                if slot == S_CTX:
                    pe.wait_ge(ctx_in, n(b, 16, 16))
                    a_job(A_CTX)
                    for k in range(KB):
                        last = turn(bank_a[:, k * P:(k + 1) * P], cb[:, k, :])
                    last.then_inc(a_full, 1)
                if slot == S_K:
                    a_job(A_K)
                    mm(bank_a[:, 0:T], w_qkv_t[:, D:2 * D], x_t[:, :], start=True, stop=True).then_inc(a_full, 1)
                if slot == S_Q:
                    bank = d_job(0)
                    mm(bank[:, 0:T], w_qkv_t[:, 0:D], x_t[:, :], start=True, stop=True).then_inc(d_full, 1)
                if slot == S_V:
                    bank = d_job(1)
                    for t in range(QT):
                        last = mm(bank[:, t * D:(t + 1) * D], x_t[:, t * P:(t + 1) * P], w_qkv_t[:, 2 * D:3 * D],
                                  start=True, stop=True, skip_group_check=True)
                    last.then_inc(d_full, 1)
                if slot in (S_KV_A, S_KV_B):
                    j = slot - S_KV_A
                    a_job(A_KV + j)
                    for k in range(2):
                        kb = 2 * j + k
                        last = mm(bank_a[:, 2 * k * D:2 * (k + 1) * D], ctx_t[:, kb * P:(kb + 1) * P], w_l1kv[:, :],
                                  start=True, stop=True, skip_group_check=True)
                    last.then_inc(a_full, 1)
                if slot in S_SCORE:
                    at = S_SCORE.index(slot)
                    j, i = divmod(at, 3)
                    if i == 0:
                        pe.wait_ge(km_ready, n(b, G, j + 1))
                    bank = d_job(D_SCORE + at)
                    if i == 0:
                        last = mm(bank[:, 0:4 * P], q0[:, 0:P], km[:, j % 2, :, 0:P], start=True, stop=True)
                    else:
                        g = 2 * (i - 1)
                        last = mm(bank[:, 0:2 * BAND], q0[:, P:T], km[:, j % 2, g:g + 2, T - BAND:T],
                                  start=True, stop=True)
                    last.then_inc(d_full, 1)
                at = slot - S_TURN
                if 0 <= at < TURNS:
                    if at % 6 == 0:
                        pe.wait_ge(exp0_done, n(b, 2, at // 6 + 1))
                    a_job(A_TURN + at)
                    for i, (qt, j, kt, g) in enumerate(jobs[at]):
                        h = 4 * g + j
                        src = prob0[:, h, :] if qt == 0 else prob1[:, h, kt * P:(kt + 1) * P]
                        last = turn(bank_a[:, i * P:(i + 1) * P], src)
                    last.then_inc(a_full, 1)
                if 1 <= at <= TURNS:
                    last = weigh_values(at - 1)
                    if at == TURNS:
                        last.then_inc(o0_full, 1)
                if slot == S_REC:
                    pe.wait_ge(rec0_ready, n(b, 1, 1))
                    a_job(A_REC)
                    for qt in range(QT):
                        last = turn(bank_a[:, qt * P:(qt + 1) * P], row_rec[:, qt].rearrange("p h d -> p (h d)"))
                    last.then_inc(a_full, 1)
                if slot == S_PROJ:
                    pe.wait_ge(o0_ready, n(b, 1, 1))
                    bank = d_job(D_PROJ)
                    for qt in range(QT):
                        last = mm(bank[:, qt * D:(qt + 1) * D], o0[:, qt * P:(qt + 1) * P], w_proj_t[:, :],
                                  start=True, stop=True, skip_group_check=True)
                    last.then_inc(d_full, 1)
                if slot == S_KV:
                    bank = d_job(D_KV)
                    pe.wait_ge(k1_ready, n(b, 1, 1))
                    for kb in range(KB):
                        last = mm(bank[:, 0:D + 1], k1[:, kb, :], v1[:, kb, :], start=(kb == 0), stop=(kb == KB - 1))
                    last.then_inc(d_full, 1)
                if slot == S_LAT:
                    a_job(A_LAT)
                    pe.wait_ge(lat_ready, n(b, 1, 1))
                    for qt in range(QT):
                        last = turn(bank_a[:, qt * P:(qt + 1) * P], lat[:, qt, :])
                    last.then_inc(a_full, 1)
                if slot == S_CN:
                    a_job(A_CN)
                    pe.wait_ge(cn_ready, n(b, 1, 1))
                    for k in range(KB):
                        last = turn(bank_a[:, k * P:(k + 1) * P], cn[:, k, :])
                    last.then_inc(a_full, 1)

            def prep_keys(done, p, after=True):
                if after:
                    pe.wait_ge(p_free, done)
                c = slice(p * P, (p + 1) * P)
                split_mm(bank_p, wk_s[:, 0, c], wk_s[:, 1, c], cn_s[:, 0, :], cn_s[:, 1, :]).then_inc(p_full, 1)

            def prep_values(done, group, half):
                pe.wait_ge(p_free, done)
                c = slice(group * 2 * P, (group + 1) * 2 * P)
                for k in range(2):
                    kb = slice((2 * half + k) * P, (2 * half + k + 1) * P)
                    last = split_mm(bank_p[:, k * 2 * P:(k + 1) * 2 * P], cn_s[:, 0, kb], cn_s[:, 1, kb],
                                    wv_s[:, 0, c], wv_s[:, 1, c], skip_group_check=True)
                last.then_inc(p_full, 1)

            def prep_queries(done, p):
                pe.wait_ge(p_free, done)
                c = slice(p * P, (p + 1) * P)
                split_mm(bank_p[:, 0:T], wq_s[:, 0, c], wq_s[:, 1, c], lat_s[:, 0, :],
                         lat_s[:, 1, :]).then_inc(p_full, 1)

            for slot in range(SLOTS):
                self_attention(0, slot)
            pe.wait_ge(weights_split, 1)
            pe.wait_ge(cn_split, 1)
            prep_keys(0, 0, after=False)
            for half in range(2):
                prep_values(1 + half, 0, half)
            pe.wait_ge(lat_split, 1)
            prep_queries(3, 0)
            prep_keys(4, 1)
            with pe.Fori(0, B) as b:
                for p in range(PAIRS):
                    def unit(kb):
                        i = KB * p + kb
                        if kb == 0:
                            pe.wait_ge(kr_ready, n(b, PAIRS, p + 1))
                            pe.wait_ge(q_split, n(b, PAIRS, p + 1))
                        if i >= 2:
                            pe.wait_ge(exp_done, n(b, UNITS, i - 1))
                        c = slice(kb * P, (kb + 1) * P)
                        split_mm(sc[:, kb % 2, :], kr_s[:, p % 2, 0, c], kr_s[:, p % 2, 1, c], qm_s[:, p % 2, 0],
                                 qm_s[:, p % 2, 1]).then_inc(unit_full, 1)

                    def values_of(q, kbs):
                        o = pair_bank(q)
                        if kbs[0] == 0:
                            if q == 0:
                                pe.wait_ge(y_free, n(b, 1, 1))
                            elif q < PAIRS - 1:
                                pe.wait_ge(on_ready, n(b, PAIRS, q))
                        pe.wait_ge(clamped, n(b, HALVES, 2 * q + kbs[-1] // 2 + 1))
                        for kb in kbs:
                            for h in range(2):
                                lo = P * (q % 2) + DH * h
                                mm(o[DH * h:DH * (h + 1), 0:T], v[:, (q // 2) % 2, kb, lo:lo + DH],
                                   prob[:, q % 2, kb, T * h:T * (h + 1)], start=(kb == 0), stop=(kb == KB - 1),
                                   skip_group_check=True)

                    def sum_of(q):
                        pe.wait_ge(psum_ready, n(b, PAIRS, q + 1))
                        for h in range(2):
                            last = mm(pair_bank(q)[DH * h:DH * (h + 1), T:2 * T], ones[:, 0:DH],
                                      psum[:, q % 2, T * h:T * (h + 1)], start=True, stop=True, skip_group_check=True)
                        last.then_inc(o_full, 1)

                    def slots(lo, hi):
                        for i in range(lo, hi):
                            self_attention(b + 1, PER_PAIR * p + i)

                    def prep(make, kind, *args):
                        make(n(b, PREP_JOBS, FIRST_PREP + PREP.index((p, kind))), *args)

                    def next_values(half):
                        if p % 2 == 1:
                            prep(prep_values, f"values {half}", (p + 1) % PAIRS // 2, half)

                    last_pair = p == PAIRS - 1
                    unit(0)
                    slots(0, 1)
                    unit(1)
                    slots(1, 2)
                    if not last_pair:
                        next_values(0)
                    unit(2)
                    if not last_pair:
                        next_values(1)
                    slots(2, 3)
                    if not last_pair:
                        prep(prep_queries, "queries", p + 1)
                    slots(3, 4)
                    if p == PAIRS - 2:
                        pe.wait_ge(cn_split, n(b, 1, 2))
                    prep(prep_keys, "keys", (p + 2) % PAIRS)
                    if p >= 1:
                        values_of(p - 1, (0, 1))
                    unit(3)
                    slots(4, 5)
                    if p >= 1:
                        values_of(p - 1, (2, 3))
                        sum_of(p - 1)
                    slots(5, 6)
                values_of(PAIRS - 1, (0, 1))
                next_values(0)
                values_of(PAIRS - 1, (2, 3))
                next_values(1)
                sum_of(PAIRS - 1)
                pe.wait_ge(lat_split, n(b, 1, 2))
                prep(prep_queries, "queries", 0)
                pe.wait_ge(on_ready, n(b, PAIRS, PAIRS - 1))
                for p in range(PAIRS):
                    if p == PAIRS - 1:
                        pe.wait_ge(on_ready, n(b, PAIRS, PAIRS))
                    for qt in range(QT):
                        last = mm(ob[:, qt * D:(qt + 1) * D], on[:, p, qt * P:(qt + 1) * P], wo[:, p, :],
                                  start=(p == 0 and qt == 0), stop=(p == PAIRS - 1), skip_group_check=True)
                last.then_inc(y_full, 1)

            pe.wait_ge(a_free, SETUP_A + (B + 1) * ACT_JOBS)
            pe.wait_ge(mats_in, 16 * 8)
            for k, m in enumerate((M_A, M_B, M_WO)):
                last = turn(bank_a[:, k * P:(k + 1) * P], mats[:, m, :])
            last.then_inc(ta_full, 1)
            pe.wait_ge(d_free, SETUP_D + (B + 1) * DVE_JOBS)
            pe.wait_ge(p_free, FIRST_PREP + B * PREP_JOBS)
            pe.wait_ge(red_ready, 1)
            mm(bank_d[:, 0:1], ones[:, :], small[:, F_SUM:F_SUM + 1], start=True, stop=True).then_inc(td_full, 1)
            for k in range(4):
                pe.wait_ge(f_ready, k + 1)
                pe.wait_ge(ta_free, 1 + k)
                for i in range(4):
                    last = turn(bank_a[:, i * P:(i + 1) * P], f_all[:, 4 * k + i, :])
                last.then_inc(ta_full, 1)
            pe.wait_ge(td_free, 1)
            mm(bank_d[:, 0:D], mats[:, M_WI, :], b_t, start=True, stop=True, skip_group_check=True)
            mm(bank_d[:, D:2 * D], mats[:, M_WS, :], a_t, start=True, stop=True, skip_group_check=True)
            mm(bank_d[:, 2 * D:3 * D], mats[:, M_C, :], wo_t, start=True, stop=True, skip_group_check=True)
            mm(bank_d[0:1, 3 * D:4 * D], cols[:, BI_COL:BI_COL + 1], b_t, start=True, stop=True,
               skip_group_check=True).then_inc(td_full, 1)
            pe.wait_ge(td_free, 2)
            mm(bank_d[:, 0:D], mats[:, M_WS, :], g_t, start=True, stop=True, skip_group_check=True)
            mm(bank_d[0:1, D:2 * D], cols[:, BI_COL:BI_COL + 1], b_t, start=True, stop=False, skip_group_check=True)
            mm(bank_d[0:1, D:2 * D], cols[:, BS_COL:BS_COL + 1], a_t, start=False, stop=True, skip_group_check=True)
            mm(bank_d[:, 2 * D:2 * D + 1], g_t, cols[:, BS_COL:BS_COL + 1], start=True, stop=True,
               skip_group_check=True).then_inc(td_full, 1)
            pe.wait_ge(td_free, 3)
            pe.wait_ge(red_ready, 2)
            turn(bank_d[0:1, 0:P], small[:, Q_MAX:Q_MAX + 1]).then_inc(td_full, 1)
            pe.wait_ge(td_free, 4)
            mm(bank_d[:, 0:1], ones[0:1, :], diag2[0:1, 0:1], start=True, stop=True).then_inc(td_full, 1)

            def turn_x3(k):
                pe.wait_ge(x3_ready, k + 1)
                pe.wait_ge(ta_free, 5 + k)
                for i in range(4):
                    last = turn(bank_a[:, i * P:(i + 1) * P], t4b[:, i, :])
                last.then_inc(ta_full, 1)

            pe.wait_ge(prep_ready, 1)
            for k in range(4):
                pe.wait_ge(td_free, 5 + k)
                pe.wait_ge(f_quantized, k + 1)
                for i in range(4):
                    t = 4 * k + i
                    last = mm(bank_d[:, i * D:(i + 1) * D], f_t[:, t * P:(t + 1) * P], w_round, start=True, stop=True,
                              skip_group_check=True)
                last.then_inc(td_full, 1)
                if k >= 1:
                    turn_x3(k - 1)
            turn_x3(3)
            pe.wait_ge(ta_free, 9)
            pe.wait_ge(ident16_ready, 2)
            for k in range(4):
                mm(sc[:, k, :], bwi_t, x3_t[:, 512 * k:512 * k + 512], start=True, stop=False, skip_group_check=True)
                lo = B if k == 0 else 0
                mm(sc[:, k, lo:512], aws_t, x3_t[:, 512 * k + lo - B:512 * k + 512 - B], start=False, stop=False,
                   skip_group_check=True)
                last = mm(sc[:, k, lo:512], c_rows[:, D:2 * D], one_row[:, lo:512], start=False, stop=True,
                          skip_group_check=True)
                if k == 0:
                    last = mm(sc[:, 0, 0:B], c_rows[:, 0:D], one_row[:, 0:B], start=False, stop=True,
                              skip_group_check=True)
            last.then_inc(c_ready, 1)
            with pe.Fori(0, (T - 1) // STEPS) as part:
                t0 = part * STEPS + 1
                for i in range(STEPS):
                    pe.wait_ge(h_ready, t0 + i)
                    mm(cf[:, bass.ds((t0 + i) * B, B)], a_t, hid[:, bass.ds((t0 + i - 1) * B, B)], start=False,
                       stop=True, skip_group_check=True).then_inc(z_ready, 1)
            pe.wait_ge(h_ready, T)
            hid_b = hid.rearrange("p (t b) -> p b t", b=B)
            x3_b = x3_t.rearrange("p (t b) -> p b t", b=B)
            with pe.Fori(0, B) as b:
                ja = 9 + b * TAIL_A
                jd = 9 + b * TAIL_D
                pe.wait_ge(ta_free, ja)
                mm(bank_a[:, 0:T], g_t, hid_b[:, b, :], start=True, stop=False)
                mm(bank_a[:, 0:T], gws_t, x3_b[:, b, :], start=False, stop=True).then_inc(ta_full, 1)
                pe.wait_ge(ta_free, ja + 1)
                pe.wait_ge(td_free, jd)
                for i in range(QT):
                    last = turn(bank_d[:, i * P:(i + 1) * P], pre_t[:, i * P:(i + 1) * P])
                last.then_inc(td_full, 1)
                pe.wait_ge(td_free, jd + 1)
                for i in range(QT):
                    last = turn(bank_a[:, i * P:(i + 1) * P], x4[:, i, :])
                last.then_inc(ta_full, 1)
                pe.wait_ge(ta_free, ja + 2)
                for i in range(QT):
                    last = mm(bank_d[:, i * P:(i + 1) * P], x4_t[:, i * P:(i + 1) * P], w_l1q[:, :], start=True,
                              stop=True, skip_group_check=True)
                last.then_inc(td_full, 1)
                pe.wait_ge(q1_ready, b + 1)
                for i in range(QT):
                    last = turn(bank_a[:, i * P:(i + 1) * P], q1[:, i, :])
                last.then_inc(ta_full, 1)
                pe.wait_ge(ta_free, ja + 3)
                pe.wait_ge(td_free, jd + 2)
                pe.wait_ge(kvm_ready, b + 1)
                for i in range(QT):
                    tok = q1_t[:, i * P:(i + 1) * P]
                    mm(bank_d[:, i * P:(i + 1) * P], tok, kvm, start=True, stop=True, skip_group_check=True)
                    last = mm(bank_d[:, T + i * P:T + (i + 1) * P], tok, ksm, start=True, stop=True,
                              skip_group_check=True)
                last.then_inc(td_full, 1)
            ja = 9 + B * TAIL_A
            jd = 9 + B * TAIL_D
            pe.wait_ge(mixed_in, 16 * B * H)
            for k in range(4):
                pe.wait_ge(ta_free, ja + k)
                for i in range(4):
                    last = turn(bank_a[:, i * P:(i + 1) * P], mixed[:, 4 * k + i, :])
                last.then_inc(ta_full, 1)
                pe.wait_ge(ta_free, ja + k + 1)
                pe.wait_ge(td_free, jd + k)
                for i in range(4):
                    last = mm(bank_d[:, i * P:(i + 1) * P], att_t[:, i * P:(i + 1) * P], w_dense[:, :], start=True,
                              stop=True, skip_group_check=True)
                last.then_inc(td_full, 1)
            ja += 4
            jd += 4
            pe.wait_ge(td_free, jd)
            pe.wait_ge(red_ready, 3)
            turn(bank_d[0:2, 0:P], small[:, Q_MAX:Q_MAX + 2]).then_inc(td_full, 1)
            pe.wait_ge(td_free, jd + 1)
            pe.wait_ge(red_ready, 4)
            mm(bank_d[:, 0:2], ones[0:2, :], diag2[0:2, 0:2], start=True, stop=True).then_inc(td_full, 1)
            pe.wait_ge(q8_ready, 1)
            pe.wait_ge(td_free, jd + 2)
            nc.tensor.transpose(bank_d[:, 0:64].bitcast(BF16), w8[:, 0, :], ident16[:, :]).then_inc(td_full, 1)
            for k in range(4):
                pe.wait_ge(q8_ready, 2 + k)
                pe.wait_ge(ta_free, ja + k)
                for i in range(4):
                    last = nc.tensor.transpose(bank_a[:, 64 * i:64 * i + 64].bitcast(BF16), q8[:, 4 * k + i, :],
                                               ident16[:, :])
                last.then_inc(ta_full, 1)
                pe.wait_ge(ta_free, ja + k + 1)
                pe.wait_ge(td_free, jd + 3 + k)
                for i in range(4):
                    last = mm(bank_d[:, i * P:(i + 1) * P], q8_t[:, i * P:(i + 1) * P], w8[:, 1, :], start=True,
                              stop=True, skip_group_check=True)
                last.then_inc(td_full, 1)


_INS = [
    "x", "ctx_1024", "mask_BxS2_ff1", "L0_attn_w_qkv", "L0_attn_w_proj", "L0_attn_b_proj", "L0_attn_rel_bias",
    "L0_xattn_cos", "L0_xattn_sin", "L0_xattn_ln_lat_g", "L0_xattn_ln_lat_b", "L0_xattn_ln_ctx_g",
    "L0_xattn_ln_ctx_b", "L0_xattn_Wq", "L0_xattn_Wkv", "L0_xattn_Wo", "L0_xattn_bo", "L0_ffn_weight",
    "L0_ffn_ln_gamma", "L0_ffn_ln_beta", "L1_attn_Wi", "L1_attn_bi", "L1_attn_Ws", "L1_attn_bs", "L1_attn_Wo",
    "L1_attn_bo", "L1_attn_A", "L1_attn_B", "L1_attn_C", "L1_xattn_wq", "L1_xattn_wk", "L1_xattn_wv",
    "L1_xattn_ln_gamma", "L1_xattn_ln_beta", "L1_xattn_dense_w", "L1_xattn_dense_b", "L1_ffn_weight", "L1_ffn_bias",
]


def kernel(**inputs):
    import numpy as _np
    import concourse.bacc as _bacc
    from concourse import mybir as _mybir
    from concourse.bass_utils import run_bass_kernel_spmd as _run

    nc = _bacc.Bacc("TRN2", target_bir_lowering=False, num_devices=1)
    arrays, args = {}, {}
    for name in _INS:
        arr = _np.ascontiguousarray(inputs[name])
        arrays[f"in_{name}_dram"] = arr
        args[name] = nc.dram_tensor(f"in_{name}_dram", arr.shape, _mybir.dt.from_np(arr.dtype),
                                    kind="ExternalInput").ap()
    out = nc.dram_tensor("out_0_dram", (B, T, D), F32, kind="ExternalOutput").ap()
    decoder(nc, args, out)
    r = _run(nc, [arrays], core_ids=[0])
    return r.results[0]["out_0_dram"]
```

```python
from contextlib import ExitStack

import numpy as np

import concourse.bass as bass
from concourse import mybir

F32 = mybir.dt.float32
F32R = mybir.dt.float32r
BF16 = mybir.dt.bfloat16
U32 = mybir.dt.uint32
ALU = mybir.AluOpType
ACT = mybir.ActivationFunctionType
AX_X = mybir.AxisListType.X

B, T, D = 8, 256, 128
S = 512
P = 128
QT = T // P
KB = S // P
NT = B * QT
H = 16
HD = D // H
G = 4
WINDOW = 64
MAX_REL = 128
DH = 64
HALF = DH // 2
PAIRS = H // 2
INNER = H * DH
CLIP = 11.0
MASKED = -1e30
BAND = WINDOW + P
SCRATCH = P - 1 + BAND
QB = 128.0
ROUND = 12582912.0
FP8_MAX = 448.0
FP8_MIN_NORMAL = 2.0 ** -6
FP8_ROUND = 1.5 * 2.0 ** 20
EPS_LN = 1e-5
EPSILONS = (EPS_LN, 1e-6, 1e-3)

PER_PAIR = 6
SLOTS = PER_PAIR * PAIRS
S_X, S_K, S_Q, S_CTX, S_V, S_KV_A, S_KV_B = range(7)
S_SCORE = range(10, 22)
S_MASKED = (3, 6, 14, 17)
S_EXP = list(range(17, 23)) + list(range(24, 30))
S_NORM, S_AFFINE, S_RELU = (9, 13), (17, 18, 19, 20), 23
S_CTX_NORM, S_KV_NORM = 5, (10, 15)
S_TURN, S_SUMS, S_REC, S_DIVIDE, S_CN, S_PROJ, S_KV, S_LAT = 24, 30, 37, 38, 36, 39, 41, 42
TURNS = 12
A_X, A_K, A_CTX, A_KV, A_TURN, A_CN, A_REC, A_LAT = 0, 1, 2, 3, 5, 17, 18, 19
ACT_JOBS = 20
D_SCORE, D_PROJ, D_KV = 2, 14, 15
DVE_JOBS = 16
SETUP_A = 1
SETUP_D = 3
def prep_jobs():
    jobs = []
    for p in range(PAIRS):
        values = [(p, "values 0"), (p, "values 1")] if p % 2 == 1 else []
        if p < PAIRS - 1:
            jobs += values + [(p, "queries"), (p, "keys")]
        else:
            jobs += [(p, "keys")] + values + [(p, "queries")]
    return jobs


PREP = prep_jobs()
PREP_JOBS = len(PREP)
LAST_PREPS = PREP.index((PAIRS - 2, "keys"))
FIRST_PREP = 5
SELF_NORMS, NORMS = 5, 6
UNITS = KB * PAIRS
HALVES = 2 * PAIRS
SELF_DVE_LINKS, DVE_LINKS, LAST_DVE_LINKS = 6, 16, 10
SELF_POOL_LINKS, POOL_LINKS, LAST_POOL_LINKS = 13, 38, 23
STEPS = 7
Z_STEPS = (T * B - 1024) // P
LATE_STEPS = (T - P) // B
EARLY_A, EARLY_D, EARLY_NORMS = 3, 3, 2
EARLY_DVE_LINKS = 6
EARLY_POOL_LINKS = 2
LATE_GROUPS = 2


def n(b, per, k):
    return b * per + k


class Chain:

    def __init__(self, eng, sem):
        self.eng, self.sem, self.base, self.k = eng, sem, 0, 0

    def start(self, base):
        self.base, self.k = base, 0

    def link(self, instruction):
        self.k += 1
        instruction.then_inc(self.sem, 1)
        self.eng.wait_ge(self.sem, self.base + self.k)


def rows(ap, parts, offset, dims):
    return bass.AP(tensor=ap.tensor, offset=ap.offset + offset, ap=[list(parts)] + [list(d) for d in dims])


def decoder(nc, a, out):
    with ExitStack() as ctx:
        def sb(name, shape, dt=F32):
            return ctx.enter_context(nc.sbuf_tensor(name, shape, dt))

        def sem(name):
            return ctx.enter_context(nc.semaphore(name))

        sc = ctx.enter_context(nc.psum_tensor("score_banks", [P, 4, 512], F32))
        o0_bank = sc[:, 2, :]
        bank_p = sc[:, 3, :]
        cf = sc[:, :, :].rearrange("p k c -> p (k c)")
        ob = ctx.enter_context(nc.psum_tensor("out_bank", [P, 512], F32))
        bank_a = ctx.enter_context(nc.psum_tensor("bank_a", [P, 512], F32))
        bank_d, bank_d2 = (ctx.enter_context(nc.psum_tensor(f"bank_d{i}", [P, 512], F32)) for i in range(2))

        def pair_bank(p):
            return ob if p < PAIRS - 1 else o0_bank

        def d_bank(job):
            return (bank_d, bank_d2)[(SETUP_D + job) % 2]


        ident = sb("ident", [P, P])
        ones = sb("ones", [P, P])
        minus_half = sb("minus_half", [P, 8])
        minus_one = sb("minus_one", [P, 4])
        epsilons = sb("epsilons", [P, 3, 8])
        head_mask = sb("head_mask", [P, H])
        mask_jg = sb("mask_jg", [P, H])
        quad_mask = sb("quad_mask", [P, G, P])
        bias_mask = sb("bias_mask", [P, H, BAND])
        w_qkv_t = sb("w_qkv_t", [P, 3 * D])
        w_proj_t = sb("w_proj_t", [P, D])
        wq_s = sb("wq_s", [P, 2, INNER], F32R)
        wk_s = sb("wk_s", [P, 2, INNER], F32R)
        wv_s = sb("wv_s", [P, 2, INNER], F32R)
        pair_mask = sb("pair_mask", [P, 2])
        wo = sb("wo", [P, PAIRS, D])
        cos_t = sb("cos_t", [P, S])
        sin_t = sb("sin_t", [P, S])
        w_l1kv = sb("w_l1kv", [P, 2 * D])
        w_l1q = sb("w_l1q", [P, D])
        w_dense = sb("w_dense", [P, D])
        keep = sb("keep", [P, B, KB])
        cols = sb("cols", [P, 9])
        LAT_G, LAT_B, CTX_G, CTX_B, FFN_G, FFN_B, BO_COL, BS_COL, BI_COL = range(9)
        b_proj = sb("b_proj", [P, D])
        b_wo = sb("b_wo", [P, D])
        l1_g = sb("l1_g", [P, D])
        l1_b = sb("l1_b", [P, D])
        b_dense = sb("b_dense", [P, D])
        b_ffn = sb("b_ffn", [P, D])

        xb = sb("xb", [P, QT, D])
        cb = sb("cb", [P, KB, D])
        x_t = sb("x_t", [P, T])
        q0 = sb("q0", [P, T])
        k0 = sb("k0", [P, T])
        km = sb("km", [P, 2, G, T])
        vm = sb("vm", [P, QT, G, P])
        prob0 = sb("prob0", [P, H, P])
        prob1 = sb("prob1", [P, H, T])
        row_max = sb("row_max", [P, QT, G, G])
        neg_max = sb("neg_max", [P, QT, G, G])
        row_sum = sb("row_sum", [P, QT, G, G])
        row_rec = sb("row_rec", [P, QT, H, HD])
        rec_t = sb("rec_t", [P, T])
        xbp = sb("xbp", [P, QT, D])
        x1 = sb("x1", [P, QT, D])
        pt = sb("pt", [P, 4, 512])
        o0 = sb("o0", [P, T])
        ctx_t = sb("ctx_t", [P, S])
        cn = sb("cn", [P, KB, D])
        cn_raw = ctx_t
        cn_s = sb("cn_s", [P, 2, S], F32R)
        kv1 = sb("kv1", [P, 2 * KB, D])
        k1 = sb("k1", [P, KB, D])
        v1 = sb("v1", [P, KB, D + 1])
        stats = sb("stats", [P, 8, 6])
        mv = sb("mv", [P, 8, 2])
        var_eps = sb("var_eps", [P, 8])
        rstd = sb("rstd", [P, 8])
        act_scale = sb("act_scale", [P, 3, 4])
        act_bias = sb("act_bias", [P, 3, 4])
        y = sb("y", [P, QT, D])
        lat = sb("lat", [P, QT, D])
        lat_raw = x_t
        lat_s = sb("lat_s", [P, 2, T], F32R)
        k_raw = sb("k_raw", [P, S])
        k_sin = sb("k_sin", [P, S])
        kr_s = sb("kr_s", [P, 2, 2, S], F32R)
        q_raw = sb("q_raw", [P, T])
        qm_s = sb("qm_s", [P, 2, 2, 2, T], F32R)
        v = sb("v", [P, 2, KB, 2 * P])
        prob = sb("prob", [P, 2, KB, 512])
        psum = sb("psum", [P, 2, 512])
        o_rec = sb("o_rec", [P, T])
        on = sb("on", [P, PAIRS, T])

        x2 = sb("x2", [P, NT, D])
        kv_sums = sb("kv_sums", [P, B, D + 1])

        mats = km[:, :, :, :].rearrange("p j g t -> p (j g t)").rearrange("p (k d) -> p k d", d=D)
        M_WI, M_WS, M_WO, M_A, M_B, M_C, M_FFN0, M_FFN1 = range(8)
        f_t = prob[:, 0, :, :].rearrange("p k c -> p (k c)")
        x3_t = prob[:, 1, :, :].rearrange("p k c -> p (k c)")
        hid = prob1[:, 0:8, :].rearrange("p k c -> p (k c)")
        x5 = prob1[:, 8:16, :].rearrange("p k (t d) -> p (k t) d", d=D)
        tail = pt[:, :, :].rearrange("p k (t d) -> p (k t) d", d=D)
        a_t, b_t, wo_t, bwi_t, aws_t, g_t, gws_t, w_round = (tail[:, k, :] for k in range(8))
        kvm = mats[:, B:2 * B, :]
        ksm = kv1[:, :, :]
        pre_t, x4_t, q1_t = (psum[:, 0, k * P:(k + 1) * P] for k in range(3))
        att_t = cn_raw[:, :]
        den = o_rec[:, :]
        att = on[:, :, :].rearrange("p k (i d) -> p (k i) d", d=D)
        mixed = prob0[:, :, :]
        f_all = v[:, :, :, :].rearrange("p g k c -> p (g k c)").rearrange("p (t d) -> p t d", d=D)
        x4_all = f_all
        x4_by_batch = x4_all.rearrange("p (b q) d -> p b q d", q=QT)
        att_by_batch = att.rearrange("p (b q) d -> p b q d", q=QT)
        x4 = x1
        q1 = lat
        one_row = sin_t[0:1, :]
        c_rows = rec_t[0:1, 0:2 * D]
        t4 = cn[:, :, :]
        t4b = cb[:, :, :]
        settled = sb("settled", [P, 32])
        small = sb("small", [P, 16])
        (F_MAX, F_SUM, F_ALL, BETA, INV_BETA, F_INV, F_SCALE, OUT_BIAS, Q_MAX, Q_SCALE, Q_INV) = (
            0, 4, 5, 6, 7, 8, 9, 10, 11, 13, 15)
        diag2 = sb("diag2", [2, 4])
        level = f_all
        q8 = prob[:, 0, 0:2, :].bitcast(BF16).rearrange("p k (t d) -> p (k t) d", d=D)
        w8 = sb("w8", [P, 2, D], BF16)
        q8_t = sb("q8_t", [P, 512], BF16)
        ident16 = sb("ident16", [P, P], BF16)

        mats_in = sem("mats_in")
        ta_full = sem("ta_full")
        ta_free = sem("ta_free")
        td_full = sem("td_full")
        td_free = sem("td_free")
        f_quantized = sem("f_quantized")
        x3_ready = sem("x3_ready")
        prep_ready = sem("prep_ready")
        c_ready = sem("c_ready")
        z_ready = sem("z_ready")
        h_ready = sem("h_ready")
        q1_ready = sem("q1_ready")
        kvm_ready = sem("kvm_ready")
        att_ready = sem("att_ready")
        att_out = sem("att_out")
        mixed_in = [sem(f"mixed_in{k}") for k in range(LATE_GROUPS)]
        red_ready = sem("red_ready")
        ident16_ready = sem("ident16_ready")
        q8_ready = sem("q8_ready")
        x5b_ready = sem("x5b_ready")
        out_ready = sem("out_ready")
        consts_made = sem("consts_made")
        mask_ready = sem("mask_ready")
        first_in = sem("first_in")
        weights_in = sem("weights_in")
        scratch_out = sem("scratch_out")
        bias_in = sem("bias_in")
        x_in = sem("x_in")
        ctx_in = sem("ctx_in")
        a_full = sem("a_full")
        a_free = sem("a_free")
        d_full = sem("d_full")
        d_free = sem("d_free")
        var_ready = sem("var_ready")
        rstd_ready = sem("rstd_ready")
        dve_chain = sem("dve_chain")
        pool_chain = sem("pool_chain")
        trig_ready = sem("trig_ready")
        km_ready = sem("km_ready")
        cn_ready = sem("cn_ready")
        cn_split = sem("cn_split")
        lat_split = sem("lat_split")
        p_full = sem("p_full")
        y_full = sem("y_full")
        y_free = sem("y_free")
        p_free = sem("p_free")
        weights_high = sem("weights_high")
        weights_split = sem("weights_split")
        ksin_ready = sem("ksin_ready")
        ksum_ready = sem("ksum_ready")
        kr_high = sem("kr_high")
        kv_normed = sem("kv_normed")
        kv_ready = sem("kv_ready")
        q_split = sem("q_split")
        neg_ready = sem("neg_ready")
        exp0_done = sem("exp0_done")
        rec0_ready = sem("rec0_ready")
        o0_full = sem("o0_full")
        o0_ready = sem("o0_ready")
        lat_ready = sem("lat_ready")
        kr_ready = sem("kr_ready")
        unit_full = sem("unit_full")
        exp_done = sem("exp_done")
        clamped = sem("clamped")
        psum_ready = sem("psum_ready")
        o_full = sem("o_full")
        on_ready = sem("on_ready")
        xbp_ready = sem("xbp_ready")
        x1_ready = sem("x1_ready")
        x1p_ready = sem("x1p_ready")
        k1_ready = sem("k1_ready")
        x2_ready = sem("x2_ready")
        f_ready = sem("f_ready")
        out_done = sem("out_done")

        scratch = nc.dram_tensor("bias_scratch", [H, SCRATCH], F32).ap()

        att_dram = nc.dram_tensor("att_scratch", [B, H, T, HD], F32).ap()

        rel = prob0[0:WINDOW + 1, 0, 0:H]
        rel_row = prob1[0:H, 8:10, :].rearrange("p a b -> p (a b)")[:, 0:SCRATCH]
        w_nat = prob1[:, 2:4, :].rearrange("p a (b c) -> p (a b) c", c=P)
        trig_nat = prob1[:, 6, :].rearrange("p (t k d) -> p t k d", t=2, k=KB)
        trig_rep = km[:, :, 0:2, :].rearrange("p t a (b r d) -> p t (a b) r d", b=2, r=4)
        wkv_nat = prob[:, 0, :, :].rearrange("p k c -> p (k c)")
        wq_nat = prob[:, 1, 0:2, :].rearrange("p k c -> p (k c)")

        block = ctx.enter_context(nc.Block())

        FIRST_LOADS = 8
        SETUP_LOADS = 20

        @block.sync
        def _(sp):
            loads = {first_in: 0, weights_in: 0}

            def load(dst, src, slow=False, signal=weights_in):
                loads[signal] += 1
                sp.dma_start(dst, src, allow_slow_non_contiguous=slow).then_inc(signal, 16)

            def col(name, k):
                load(cols[:, k:k + 1], a[name].rearrange("(p o) -> p o", o=1), slow=True)

            def row(name, dst, signal=weights_in):
                load(dst[:, :], rows(a[name], (0, P), 0, [(1, D)]), signal=signal)

            load(rel, a["L0_attn_rel_bias"][MAX_REL:MAX_REL + WINDOW + 1, :], signal=first_in)
            load(w_nat[:, 0:3, :], a["L0_attn_w_qkv"].rearrange("(k p) c -> p k c", p=P), signal=first_in)
            load(w_nat[:, 3, :], a["L0_attn_w_proj"], signal=first_in)
            load(trig_nat[:, 0], a["L0_xattn_cos"].rearrange("(k p) d -> p k d", p=P), signal=first_in)
            load(trig_nat[:, 1], a["L0_xattn_sin"].rearrange("(k p) d -> p k d", p=P), signal=first_in)
            load(w_l1kv[:, 0:D], a["L1_xattn_wk"], signal=first_in)
            load(w_l1kv[:, D:2 * D], a["L1_xattn_wv"], signal=first_in)
            row("L0_attn_b_proj", b_proj, signal=first_in)
            sp.dma_start(xb[:, :, :], a["x"][0].rearrange("(k p) d -> p k d", p=P)).then_inc(x_in, 16)
            sp.dma_start(cb[:, :, :], a["ctx_1024"][0].rearrange("(k p) d -> p k d", p=P)).then_inc(ctx_in, 16)
            load(wkv_nat, a["L0_xattn_Wkv"])
            load(wq_nat, a["L0_xattn_Wq"])
            load(wo[:, :, :], a["L0_xattn_Wo"].rearrange("(k p) d -> p k d", p=P))
            sp.wait_ge(d_free, 2)
            sp.dma_start(scratch, rel_row).then_inc(scratch_out, 16)
            row("L1_xattn_ln_gamma", l1_g)
            row("L1_xattn_ln_beta", l1_b)
            col("L0_xattn_ln_ctx_g", CTX_G)
            col("L0_xattn_ln_ctx_b", CTX_B)
            sp.wait_ge(scratch_out, 16)
            sp.dma_start(bias_mask[:, :, :], rows(scratch, (1, P), 0, [(SCRATCH, H), (1, BAND)])).then_inc(bias_in, 16)
            load(keep[:, :, :], a["mask_BxS2_ff1"].rearrange("b (k p) -> p b k", p=P), slow=True)
            col("L0_xattn_ln_lat_g", LAT_G)
            col("L0_xattn_ln_lat_b", LAT_B)
            row("L0_xattn_bo", b_wo)
            load(w_l1q[:, :], a["L1_xattn_wq"])
            load(w_dense[:, :], a["L1_xattn_dense_w"])
            col("L0_ffn_ln_gamma", FFN_G)
            col("L0_ffn_ln_beta", FFN_B)
            col("L1_attn_bo", BO_COL)
            col("L1_attn_bs", BS_COL)
            col("L1_attn_bi", BI_COL)
            row("L1_xattn_dense_b", b_dense)
            row("L1_ffn_bias", b_ffn)
            assert loads == {first_in: FIRST_LOADS, weights_in: SETUP_LOADS}, loads

            def load_next(b, src):
                sp.wait_ge(a_free, n(b, ACT_JOBS, SETUP_A + A_X + 1))
                sp.wait_ge(xbp_ready, n(b, 1, 1))
                sp.dma_start(xb[:, :, :], a["x"][src].rearrange("(k p) d -> p k d", p=P)).then_inc(x_in, 16)
                sp.wait_ge(a_free, n(b, ACT_JOBS, SETUP_A + A_CTX + 1))
                sp.wait_ge(cn_ready, n(b, 1, 1))
                sp.dma_start(cb[:, :, :], a["ctx_1024"][src].rearrange("(k p) d -> p k d", p=P)).then_inc(ctx_in, 16)

            with sp.Fori(1, B) as b:
                load_next(b - 1, b)
            sp.wait_ge(y_full, B)
            for k, name in ((M_WI, "L1_attn_Wi"), (M_WS, "L1_attn_Ws"), (M_WO, "L1_attn_Wo"), (M_A, "L1_attn_A"),
                            (M_B, "L1_attn_B"), (M_C, "L1_attn_C"), (M_FFN0, "L0_ffn_weight"),
                            (M_FFN1, "L1_ffn_weight")):
                sp.dma_start(mats[:, k, :], a[name]).then_inc(mats_in, 16)
            def store_attended(b, q):
                sp.dma_start(att_dram[b, :, q * P:(q + 1) * P, :].rearrange("h t e -> t h e"),
                             att_by_batch[:, b, q, :].rearrange("p (h e) -> p h e", e=HD),
                             allow_slow_non_contiguous=True).then_inc(att_out, 16)

            for b in range(B):
                sp.wait_ge(att_ready, b + 1)
                store_attended(b, 0)
            att_rows = att_dram.rearrange("b h t e -> (b h t e)").rearrange("(k p d) -> p k d", p=P, d=D)
            per = B // LATE_GROUPS
            for k in range(LATE_GROUPS):
                sp.wait_ge(td_free, 9 + B * EARLY_D + 2 * LATE_GROUPS + k + 1)
                for b in range(per * k, per * (k + 1)):
                    store_attended(b, 1)
                sp.wait_ge(att_out, 16 * (B + per * (k + 1)))
                sp.dma_start(mixed[:, QT * per * k:QT * per * (k + 1), :],
                             att_rows[:, QT * per * k:QT * per * (k + 1), :]).then_inc(mixed_in[k], 16)
            out_v = out.rearrange("b (q p) d -> p (b q) d", p=P)
            for k in range(4):
                sp.wait_ge(out_ready, k + 1)
                sp.dma_start(out_v[:, 4 * k:4 * k + 4, :], f_all[:, 4 * k:4 * k + 4, :]).then_inc(out_done, 16)
            sp.wait_ge(out_done, 64)

        @block.gpsimd
        def _(pool):
            chain = Chain(pool, pool_chain)
            link = chain.link
            g = nc.gpsimd
            g.memset(ones[:, :], 1.0)
            g.memset(minus_half[:, :], -0.5)
            g.memset(minus_one[:, :], -1.0)
            for k, eps in enumerate(EPSILONS):
                g.memset(epsilons[:, k, :], eps)
            g.memset(ident[:, :], 0.0)
            g.memset(head_mask[:, :], 1.0)
            g.memset(quad_mask[:, :, :], 0.0)
            link(g.memset(v1[:, :, D:D + 1], 1.0))
            g.affine_select(out=ident[:, :], in_=ident[:, :], compare_op=ALU.not_equal, fill=1.0, base=0,
                            pattern=[[-1, P]], channel_multiplier=1)
            for j in range(G):
                g.memset(quad_mask[:, j, :].rearrange("p (g j d) -> p g j d", g=G, j=G)[:, :, j, :], 1.0)
            link(g.affine_select(out=head_mask[:, :], in_=head_mask[:, :], compare_op=ALU.is_ge, fill=0.0, base=0,
                                 pattern=[[-HD, H]], channel_multiplier=1))
            g.affine_select(out=head_mask[:, :], in_=head_mask[:, :], compare_op=ALU.is_ge, fill=0.0, base=HD - 1,
                            pattern=[[HD, H]], channel_multiplier=-1).then_inc(consts_made, 1)
            pool.wait_ge(consts_made, 1)
            g.tensor_copy(mask_jg[:, :].rearrange("p (j g) -> p g j", g=G),
                          head_mask[:, :].rearrange("p (g j) -> p g j", j=G)).then_inc(mask_ready, 1)
            pool.wait_ge(mask_ready, 1)
            def rstd_of(before, k, count, eps, half=0):
                tiles = slice(4 * half, 4 * half + count)
                pool.wait_ge(var_ready, before + k + 1)
                link(g.tensor_tensor(var_eps[:, tiles], mv[:, tiles, 1],
                                     epsilons[:, EPSILONS.index(eps), tiles], ALU.add))
                g.tensor_tensor(rstd[:, tiles], var_eps[:, tiles], minus_half[:, tiles],
                                ALU.pow).then_inc(rstd_ready, 1)

            def scale_and_bias(before, k, eps):
                scale, bias = act_scale[:, k, :], act_bias[:, k, :]
                pool.wait_ge(var_ready, before + k + 1)
                link(g.tensor_tensor(var_eps[:, 4:8], mv[:, 4:8, 1], epsilons[:, EPSILONS.index(eps), 4:8], ALU.add))
                link(g.tensor_tensor(scale, var_eps[:, 4:8], minus_half[:, 4:8], ALU.pow))
                link(g.tensor_tensor(bias, mv[:, 4:8, 0], scale, ALU.mult))
                g.tensor_tensor(bias, bias, minus_one[:, :], ALU.mult).then_inc(rstd_ready, 1)

            def self_attention(b, slot, norms, after=True):
                if slot == S_X:
                    pool.wait_ge(x_in, n(b, 16, 16))
                    if after:
                        pool.wait_ge(x1_ready, b)
                    g.tensor_tensor(xbp[:, :, :], xb[:, :, :], b_proj[:, :].unsqueeze(1).broadcast_to([P, QT, D]),
                                    ALU.add).then_inc(xbp_ready, 1)
                if slot == S_CTX:
                    scale_and_bias(norms, 0, EPS_LN)
                if slot in S_NORM:
                    scale_and_bias(norms, 1 + S_NORM.index(slot), 1e-6)
                if slot in S_AFFINE:
                    i = S_AFFINE.index(slot)
                    tiles = kv1[:, KB * (i % 2):KB * (i % 2 + 1), :]
                    row, op = (l1_g, ALU.mult) if i < 2 else (l1_b, ALU.add)
                    if i < 2:
                        pool.wait_ge(kv_normed, n(b, 2, i + 1))
                    last = g.tensor_tensor(tiles, tiles, row[:, :].unsqueeze(1).broadcast_to([P, KB, D]), op)
                    if i < 2:
                        link(last)
                    if i == 3:
                        last.then_inc(kv_ready, 1)
                if slot == S_PROJ:
                    rstd_of(norms, 3, QT, EPS_LN)
                    rstd_of(norms, 4, QT, EPS_LN)
                    pool.wait_ge(x1_ready, n(b, 1, 1))
                    x2_b = x2[:, bass.ds(b * QT, QT), :]
                    g.tensor_tensor(x2_b, x1[:, :, :], b_wo[:, :].unsqueeze(1).broadcast_to([P, QT, D]),
                                    ALU.add).then_inc(x1p_ready, 1)

            def rotate(prep):
                pool.wait_ge(ksin_ready, prep)
                link(g.tensor_tensor(k_raw[:, :], k_raw[:, :], cos_t[:, :], ALU.mult))
                g.tensor_tensor(k_raw[:, :], k_raw[:, :], k_sin[:, :], ALU.add).then_inc(ksum_ready, 1)

            pool.wait_ge(first_in, 16 * FIRST_LOADS)
            first = chain.k
            chain.start(first)
            for slot in range(SLOTS):
                if slot == S_AFFINE[0]:
                    pool.wait_ge(weights_in, 16 * SETUP_LOADS)
                self_attention(0, slot, 0, after=False)
            assert chain.k == SELF_POOL_LINKS, chain.k
            chain.start(first + SELF_POOL_LINKS)
            rotate(1)
            rotate(2)
            first += SELF_POOL_LINKS + 2
            def batch(b, last=False):
                chain.start(first + b * POOL_LINKS)
                norms = n(b, NORMS, SELF_NORMS)
                for p in range(PAIRS):
                    for i in range(4 if not last else 0):
                        self_attention(b + 1, PER_PAIR * p + i, norms)
                    pool.wait_ge(clamped, n(b, HALVES, 2 * p + 1))
                    if p >= 2:
                        pool.wait_ge(o_full, n(b, PAIRS, p - 1))
                    pp = prob[:, p % 2]
                    link(g.tensor_tensor(psum[:, p % 2, :], pp[:, 0, :], pp[:, 1, :], ALU.add))
                    pool.wait_ge(clamped, n(b, HALVES, 2 * p + 2))
                    link(g.tensor_tensor(psum[:, p % 2, :], psum[:, p % 2, :], pp[:, 2, :], ALU.add))
                    g.tensor_tensor(psum[:, p % 2, :], psum[:, p % 2, :], pp[:, 3, :],
                                    ALU.add).then_inc(psum_ready, 1)
                    if p + 2 < PAIRS or not last:
                        rotate(n(b, PAIRS, p + 3))
                    for i in range(4, PER_PAIR if not last else 4):
                        self_attention(b + 1, PER_PAIR * p + i, norms)
                rstd_of(norms, SELF_NORMS if not last else 0, QT, EPS_LN)
                assert chain.k == (LAST_POOL_LINKS if last else POOL_LINKS), chain.k

            with pool.Fori(0, B - 1) as b:
                batch(b)
            batch(B - 1, last=True)
            base = first + (B - 1) * POOL_LINKS + LAST_POOL_LINKS
            chain.start(base)
            g.tensor_copy(ident16[:, :], ident[:, :]).then_inc(ident16_ready, 1)
            pool.wait_ge(y_full, B)
            g.memset(one_row, 1.0).then_inc(ident16_ready, 1)
            norms = B * NORMS
            for k in range(4):
                rstd_of(norms, k, 4, 1e-3, half=k % 2)
            for k in range(4):
                rstd_of(norms + 4, k, 4, EPS_LN, half=k % 2)
            base += chain.k
            with pool.Fori(0, B) as b:
                chain.start(base + b * EARLY_POOL_LINKS)
                late = norms + 8
                for k, eps in enumerate((EPS_LN, 1e-6)):
                    rstd_of(n(b, EARLY_NORMS, late), k, 1, eps)
                assert chain.k == EARLY_POOL_LINKS, chain.k
            chain.start(base + B * EARLY_POOL_LINKS)
            late = B * NORMS + 8 + B * EARLY_NORMS
            for k, eps in enumerate((EPS_LN, 1e-6)):
                for group in range(LATE_GROUPS):
                    rstd_of(late, LATE_GROUPS * k + group, 4, eps, half=group)
            late += 2 * LATE_GROUPS
            for k in range(0, 8, 4):
                for i, eps in enumerate((1e-6, 1e-6, EPS_LN, EPS_LN)):
                    rstd_of(late, k + i, 4, eps, half=i % 2)
            late += 8
            pool.wait_ge(x2_ready, B + 4)
            g.tensor_tensor(x2[:, 0:NT, :], x5[:, :, :], b_ffn[:, :].unsqueeze(1).broadcast_to([P, NT, D]),
                            ALU.add).then_inc(x5b_ready, 1)
            for k in range(4):
                rstd_of(late, k, 4, EPS_LN, half=k % 2)

        @block.scalar
        def _(act):
            s = nc.scalar

            act.wait_ge(mask_ready, 1)
            act.wait_ge(a_full, 1)
            s.activation(sin_t[0:DH, :], bank_a[0:DH, :], ACT.Identity)
            s.activation(sin_t[DH:P, :], bank_a[DH:P, :], ACT.Identity, scale=-1.0).then_inc(a_free, 1)
            def evacuate(b, job, dst, src, free=True, **kw):
                act.wait_ge(a_full, n(b, ACT_JOBS, SETUP_A + job + 1))
                i = s.activation(dst, src, ACT.Identity, **kw)
                if free:
                    i.then_inc(a_free, 1)

            def apply_norm(norms, k, dst, src):
                act.wait_ge(rstd_ready, norms + k + 1)
                for i in range(4):
                    last = s.activation(dst[:, i, :], src[:, i, :], ACT.Identity, scale=act_scale[:, k, i:i + 1],
                                        bias=act_bias[:, k, i:i + 1])
                return last

            def self_attention(b, slot, norms):
                if slot == S_CTX_NORM:
                    apply_norm(norms, 0, cn, cb).then_inc(cn_ready, 1)
                if slot in S_KV_NORM:
                    k = S_KV_NORM.index(slot)
                    tiles = kv1[:, KB * k:KB * (k + 1), :]
                    apply_norm(norms, 1 + k, tiles, tiles).then_inc(kv_normed, 1)
                if slot == S_X:
                    evacuate(b, A_X, x_t[:, :], bank_a[:, 0:T])
                if slot == S_CTX:
                    evacuate(b, A_CTX, ctx_t[:, :], bank_a[:, :])
                if slot == S_K:
                    evacuate(b, A_K, k0[:, :], bank_a[:, 0:T])
                if slot in (S_KV_A, S_KV_B):
                    k = slot - S_KV_A
                    evacuate(b, A_KV + k, kv1[:, 4 * k:4 * k + 4, :].rearrange("p k d -> p (k d)"), bank_a[:, :])
                if slot in S_MASKED:
                    j = S_MASKED.index(slot)
                    if j == 0:
                        act.wait_ge(a_free, n(b, ACT_JOBS, SETUP_A + A_K + 1))
                    if j >= 2:
                        act.wait_ge(d_full, n(b, DVE_JOBS, SETUP_D + D_SCORE + 3 * (j - 1)))
                    for g in range(G):
                        last = s.activation(km[:, j % 2, g, :], k0[:, :], ACT.Identity,
                                            scale=mask_jg[:, G * j + g:G * j + g + 1])
                    last.then_inc(km_ready, 1)
                if slot in S_EXP:
                    half, i = divmod(S_EXP.index(slot), 6)
                    heads = [(qt, j, g) for qt in range(QT) for j in (2 * half, 2 * half + 1) for g in range(G)]
                    if i == 0:
                        act.wait_ge(neg_ready, n(b, 2, half + 1))
                    for qt, j, g in heads[i * 16 // 6:(i + 1) * 16 // 6]:
                        h = 4 * g + j
                        pr = prob0[:, h, :] if qt == 0 else prob1[:, h, WINDOW:T]
                        last = s.activation(pr, pr, ACT.Exp, bias=neg_max[:, qt, j, g:g + 1],
                                            accum_out=row_sum[:, qt, j, g:g + 1])
                    if i == 5:
                        last.then_inc(exp0_done, 1)
                at = slot - S_TURN
                if 0 <= at < TURNS:
                    evacuate(b, A_TURN + at, pt[:, at % 4, :], bank_a[:, :])
                if slot == S_REC:
                    evacuate(b, A_REC, rec_t[:, :], bank_a[:, 0:T])
                if slot == S_LAT:
                    by_feature = dict(scale=cols[:, LAT_G:LAT_G + 1], bias=cols[:, LAT_B:LAT_B + 1])
                    evacuate(b, A_LAT, lat_raw[:, :], bank_a[:, 0:T], free=False, **by_feature)
                    s.activation(lat_s[:, 0, :], bank_a[:, 0:T], ACT.Identity, **by_feature).then_inc(a_free, 1)
                if slot == S_CN:
                    by_feature = dict(scale=cols[:, CTX_G:CTX_G + 1], bias=cols[:, CTX_B:CTX_B + 1])
                    evacuate(b, A_CN, cn_raw[:, :], bank_a[:, :], free=False, **by_feature)
                    s.activation(cn_s[:, 0, :], bank_a[:, :], ACT.Identity, **by_feature).then_inc(a_free, 1)

            def keys(job, prep, after=True):
                act.wait_ge(p_full, job)
                if after:
                    act.wait_ge(kr_ready, prep - 1)
                s.activation(k_raw[:, :], bank_p, ACT.Identity).then_inc(p_free, 1)

            def keys_high(prep, buf):
                act.wait_ge(ksum_ready, prep)
                s.activation(kr_s[:, buf, 0, :], k_raw[:, :], ACT.Identity).then_inc(kr_high, 1)

            def values(job, group, half):
                act.wait_ge(p_full, job)
                s.activation(v[:, group % 2, 2 * half:2 * half + 2, :],
                             bank_p.rearrange("p (k c) -> p k c", k=2), ACT.Identity).then_inc(p_free, 1)

            def queries(job, prep, buf, after=True):
                act.wait_ge(p_full, job)
                if after:
                    act.wait_ge(q_split, prep - 1)
                s.activation(q_raw[:, :], bank_p[:, 0:T], ACT.Identity)
                for h in range(2):
                    last = s.activation(qm_s[:, buf, 0, h, :], bank_p[:, 0:T], ACT.Identity,
                                        scale=pair_mask[:, h:h + 1])
                last.then_inc(p_free, 1)

            def split_weights():
                act.wait_ge(weights_in, 16 * SETUP_LOADS)
                natural = "c (p h t d) -> c p t h d"
                for wide, nat in ((wk_s, wkv_nat[:, 0:INNER]), (wq_s, wq_nat)):
                    for t in range(2):
                        s.activation(wide[:, 0, :].rearrange("c (p t h d) -> c p t h d", t=2, h=2, d=HALF)[:, :, t],
                                     nat.rearrange(natural, h=2, t=2, d=HALF)[:, :, t], ACT.Identity)
                s.activation(wv_s[:, 0, :], wkv_nat[:, INNER:2 * INNER], ACT.Identity).then_inc(weights_high, 1)

            for slot in range(SLOTS):
                if slot == S_EXP[0]:
                    split_weights()
                self_attention(0, slot, 0)
            keys(1, 1, after=False)
            for half in range(2):
                values(2 + half, 0, half)
            queries(4, 1, 0, after=False)
            keys_high(1, 0)
            keys(5, 2)
            def batch(b, last=False):
                for p in range(PAIRS):
                    def exps(kb):
                        act.wait_ge(unit_full, n(b, UNITS, KB * p + kb + 1))
                        if p >= 2 and kb == 0:
                            act.wait_ge(o_full, n(b, PAIRS, p - 1))
                        s.activation(prob[:, p % 2, kb, :], sc[:, kb % 2, :], ACT.Exp,
                                     scale=DH ** -0.5).then_inc(exp_done, 1)

                    def slots(lo, hi):
                        for i in range(lo, hi if not last else lo):
                            self_attention(b + 1, PER_PAIR * p + i, n(b, NORMS, SELF_NORMS))

                    def prep(make, kind, *args):
                        make(n(b, PREP_JOBS, FIRST_PREP + PREP.index((p, kind)) + 1), *args)

                    def next_values(half):
                        if p % 2 == 1:
                            prep(values, f"values {half}", (p + 1) // 2, half)

                    last_pair = p == PAIRS - 1
                    exps(0)
                    slots(0, 1)
                    exps(1)
                    slots(1, 2)
                    if not last_pair:
                        next_values(0)
                    exps(2)
                    if not last_pair:
                        next_values(1)
                    slots(2, 3)
                    if not last_pair:
                        prep(queries, "queries", n(b, PAIRS, p + 2), (p + 1) % 2)
                    if not (last and last_pair):
                        keys_high(n(b, PAIRS, p + 2), (p + 1) % 2)
                    slots(3, 4)
                    exps(3)
                    if p + 2 < PAIRS or not last:
                        prep(keys, "keys", n(b, PAIRS, p + 3))
                    slots(4, 5)
                    slots(5, 6)
                if not last:
                    for half in range(2):
                        next_values(half)
                    prep(queries, "queries", n(b, PAIRS, PAIRS + 1), 0)

            with act.Fori(0, B - 1) as b:
                batch(b)
            batch(B - 1, last=True)

            def late(job, dst, src, **kw):
                act.wait_ge(ta_full, job)
                s.activation(dst, src, ACT.Identity, **kw).then_inc(ta_free, 1)

            late(1, tail[:, 0:3, :].rearrange("p k d -> p (k d)"), bank_a[:, 0:3 * D])
            for k in range(4):
                late(2 + k, f_t[:, 512 * k:512 * k + 512], bank_a[:, :], scale=cols[:, FFN_G:FFN_G + 1],
                     bias=cols[:, FFN_B:FFN_B + 1])
            for k in range(4):
                late(6 + k, x3_t.rearrange("p (t b) -> p b t", b=B)[:, 2 * k:2 * k + 2, :],
                     bank_a[:, :].rearrange("p (b t) -> p b t", b=2))
            act.wait_ge(c_ready, 1)
            s.activation(hid[:, 0:B], cf[:, 0:B], ACT.Tanh).then_inc(h_ready, 1)
            def step(t):
                act.wait_ge(z_ready, t)
                s.activation(hid[:, bass.ds(t * B, B)], cf[:, bass.ds(t * B, B)], ACT.Tanh).then_inc(h_ready, 1)

            for t in range(1, 1 + Z_STEPS):
                step(t)
            with act.Fori(0, (P - 1 - Z_STEPS) // STEPS) as part:
                for i in range(STEPS):
                    step(part * STEPS + 1 + Z_STEPS + i)
            with act.Fori(0, B) as b:
                job = 10 + b * EARLY_A
                for i in range(LATE_STEPS):
                    step(b * LATE_STEPS + P + i)
                    if i == 1:
                        late(job, pre_t, bank_a[:, 0:P], bias=small[:, OUT_BIAS:OUT_BIAS + 1])
                    if i == 7:
                        late(job + 1, x4_t, bank_a[:, 0:P])
                    if i == 14:
                        late(job + 2, q1_t, bank_a[:, 0:P])
            job = 10 + B * EARLY_A
            for k in range(3):
                for group in range(LATE_GROUPS):
                    late(job, psum[:, group, :], (bank_a, ob)[group][:, :],
                         **(dict(bias=small[:, OUT_BIAS:OUT_BIAS + 1]) if k == 0 else {}))
                    job += 1
            for k in range(4):
                late(job + k, att_t, bank_a[:, :])
            job += 4
            for k in range(4):
                act.wait_ge(ta_full, job + k)
                s.activation(q8_t[:, :], bank_a[:, 0:256].bitcast(BF16), ACT.Identity).then_inc(ta_free, 1)

        @block.vector
        def _(dve):
            chain = Chain(dve, dve_chain)
            link = chain.link
            w = nc.vector

            w.memset(settled[:, :], 0.0).then_inc(y_free, 1)
            for block_row in range(4):
                for h in range(2):
                    lo = HALF * block_row
                    w.memset(pair_mask[lo:lo + HALF, h:h + 1], 1.0 if block_row % 2 == h else 0.0)
            dve.wait_ge(first_in, 16 * FIRST_LOADS)
            for t in range(2):
                w.tensor_copy(trig_rep[:, t], trig_nat[:, t].unsqueeze(2).broadcast_to([P, KB, 4, HALF]))
            w.memset(rel_row, MASKED).then_inc(trig_ready, 1)
            dve.wait_ge(trig_ready, 1)
            dve.wait_ge(d_full, 1)
            w.tensor_copy(w_qkv_t[:, :], bank_d[:, 0:3 * D])
            w.tensor_copy(w_proj_t[:, :], bank_d[:, 3 * D:4 * D]).then_inc(d_free, 1)
            dve.wait_ge(d_full, 2)
            w.tensor_copy(rel_row[:, P - 1:P + WINDOW], bank_d[0:H, 0:WINDOW + 1]).then_inc(d_free, 1)
            dve.wait_ge(d_full, 3)
            w.tensor_copy(cos_t[:, :], bank_d[:, :]).then_inc(d_free, 1)
            first = chain.k
            def band_of(h, count):
                band = bias_mask[:, h, 0:count]
                return bass.AP(tensor=band.tensor, offset=band.offset + count - 1, ap=[list(band.ap[0]), [-1, count]])

            cells = [0]

            def settle():
                cells[0] = cells[0] % 31 + 1
                w.tensor_copy(settled[:, cells[0]:cells[0] + 1], settled[:, 0:1])

            def measure(tiles, half=0):
                settle()
                for i, tile in enumerate(tiles):
                    last = w.bn_stats(stats[:, 4 * half + i, :], tile)
                link(last)
                settle()
                for i in range(len(tiles)):
                    last = w.bn_aggr(mv[:, 4 * half + i, :], stats[:, 4 * half + i, :])
                last.then_inc(var_ready, 1)

            def statistics(before, k, tiles):
                measure(tiles)
                dve.wait_ge(rstd_ready, before + k + 1)

            def normalize(dsts, tiles, half=0):
                for i, (dst, tile) in enumerate(zip(dsts, tiles)):
                    at = 4 * half + i
                    last = w.tensor_scalar(dst, tile, mv[:, at, 0:1], rstd[:, at:at + 1], ALU.subtract, ALU.mult)
                return last

            def in_turns(count, first_part, second_part):
                for k in range(count + 1):
                    if k < count:
                        first_part(k)
                    if k >= 1:
                        second_part(k - 1)

            def bank_ready(b, job):
                dve.wait_ge(d_full, n(b, DVE_JOBS, SETUP_D + job + 1))

            def tiles_of(t, count):
                return [t[:, i, :] for i in range(count)]

            def self_attention(b, slot, norms):
                if slot == S_CTX:
                    dve.wait_ge(ctx_in, n(b, 16, 16))
                    measure(tiles_of(cb, KB), 1)
                if slot == S_Q:
                    bank_ready(b, 0)
                    w.tensor_scalar(q0[:, :], d_bank(0)[:, 0:T], HD ** -0.5, None, ALU.mult).then_inc(d_free, 1)
                if slot == S_V:
                    bank_ready(b, 1)
                    for t in range(QT):
                        last = w.tensor_tensor(vm[:, t],
                                               d_bank(1)[:, t * D:(t + 1) * D].unsqueeze(1).broadcast_to([P, G, D]),
                                               quad_mask[:, :, :], ALU.mult)
                    last.then_inc(d_free, 1)
                if slot in S_SCORE:
                    at = S_SCORE.index(slot)
                    j, i = divmod(at, 3)
                    bank_ready(b, D_SCORE + at)
                    settle()
                    if i == 0:
                        for g in range(G):
                            h = 4 * g + j
                            last = w.tensor_tensor_reduce(prob0[:, h, :], d_bank(D_SCORE + at)[:, g * P:(g + 1) * P],
                                                          band_of(h, P), 1.0, 0.0, ALU.add, ALU.max,
                                                          row_max[:, 0, j, g:g + 1])
                    else:
                        for k in range(2):
                            g = 2 * (i - 1) + k
                            h = 4 * g + j
                            last = w.tensor_tensor_reduce(prob1[:, h, WINDOW:T],
                                                          d_bank(D_SCORE + at)[:, k * BAND:(k + 1) * BAND],
                                                          band_of(h, BAND), 1.0, 0.0, ALU.add, ALU.max,
                                                          row_max[:, 1, j, g:g + 1])
                    last.then_inc(d_free, 1)
                    if at % 6 == 5:
                        half = at // 6
                        dve.wait_ge(d_free, n(b, DVE_JOBS, SETUP_D + D_SCORE + at + 1))
                        heads = slice(2 * half, 2 * half + 2)
                        w.tensor_scalar(neg_max[:, :, heads, :], row_max[:, :, heads, :], -1.0, None,
                                        ALU.mult).then_inc(neg_ready, 1)
                if slot in S_NORM:
                    k = S_NORM.index(slot)
                    tiles = tiles_of(kv1[:, KB * k:KB * (k + 1), :], KB)
                    dve.wait_ge(a_free, n(b, ACT_JOBS, SETUP_A + A_KV + k + 1))
                    dve.wait_ge(rstd_ready, norms + 1 + k)
                    measure(tiles, 1)
                if slot == S_RELU:
                    dve.wait_ge(kv_ready, n(b, 1, 1))
                    kv1_v = kv1[:, :, :].rearrange("p (k t) d -> p k t d", t=2)
                    keep_b = keep[:, b, :].unsqueeze(2).broadcast_to([P, KB, D])
                    link(w.tensor_scalar(k1[:, :, :], kv1_v[:, :, 0, :], 0.0, 1e-6, ALU.max, ALU.add))
                    w.tensor_tensor(v1[:, :, 0:D], kv1_v[:, :, 1, :], keep_b, ALU.mult)
                    w.tensor_tensor(k1[:, :, :], k1[:, :, :], keep_b, ALU.mult).then_inc(k1_ready, 1)
                if slot == S_SUMS:
                    dve.wait_ge(exp0_done, n(b, 2, 2))
                    for qt in range(QT):
                        last = w.reciprocal(row_rec[:, qt].rearrange("p (g j) d -> p j g d", j=G),
                                            row_sum[:, qt].unsqueeze(3).broadcast_to([P, G, G, HD]))
                    last.then_inc(rec0_ready, 1)
                if slot == S_DIVIDE:
                    dve.wait_ge(o0_full, n(b, 1, 1))
                    dve.wait_ge(a_free, n(b, ACT_JOBS, SETUP_A + A_REC + 1))
                    w.tensor_tensor(o0[:, :], o0_bank[:, 0:T], rec_t[:, :], ALU.mult).then_inc(o0_ready, 1)
                if slot == S_PROJ:
                    bank_ready(b, D_PROJ)
                    dve.wait_ge(xbp_ready, n(b, 1, 1))
                    w.tensor_tensor(y[:, :, :],
                                    d_bank(D_PROJ)[:, 0:QT * D].rearrange("p (q d) -> p q d", q=QT), xbp[:, :, :],
                                    ALU.add).then_inc(d_free, 1)
                    dve.wait_ge(d_free, n(b, DVE_JOBS, SETUP_D + D_PROJ + 1))
                    statistics(norms, 3, tiles_of(y, QT))
                    normalize(tiles_of(x1, QT), tiles_of(y, QT)).then_inc(x1_ready, 1)
                    dve.wait_ge(x1_ready, n(b, 1, 1))
                    statistics(norms, 4, tiles_of(x1, QT))
                    normalize(tiles_of(lat, QT), tiles_of(x1, QT)).then_inc(lat_ready, 1)
                if slot == S_KV:
                    bank_ready(b, D_KV)
                    settle()
                    w.tensor_copy(kv_sums[:, b, :], d_bank(D_KV)[:, 0:D + 1]).then_inc(d_free, 1)
                if slot == S_LAT:
                    dve.wait_ge(a_free, n(b, ACT_JOBS, SETUP_A + A_LAT + 1))
                    w.tensor_tensor(lat_s[:, 1, :], lat_raw[:, :], lat_s[:, 0, :].bitcast(F32),
                                    ALU.subtract).then_inc(lat_split, 1)
                if slot == S_CN:
                    dve.wait_ge(a_free, n(b, ACT_JOBS, SETUP_A + A_CN + 1))
                    w.tensor_tensor(cn_s[:, 1, :], cn_raw[:, :], cn_s[:, 0, :].bitcast(F32),
                                    ALU.subtract).then_inc(cn_split, 1)

            def keys_sin(job, prep):
                dve.wait_ge(p_free, job)
                w.tensor_tensor(k_sin[0:DH, :], k_raw[DH:P, :], sin_t[DH:P, :], ALU.mult)
                w.tensor_tensor(k_sin[DH:P, :], k_raw[0:DH, :], sin_t[0:DH, :], ALU.mult).then_inc(ksin_ready, 1)

            def keys_low(prep, buf):
                dve.wait_ge(kr_high, prep)
                w.tensor_tensor(kr_s[:, buf, 1, :], k_raw[:, :], kr_s[:, buf, 0, :].bitcast(F32),
                                ALU.subtract).then_inc(kr_ready, 1)

            def queries_low(job, buf):
                dve.wait_ge(p_free, job)
                for h in range(2):
                    last = w.scalar_tensor_tensor(out=qm_s[:, buf, 1, h, :], in0=q_raw[:, :],
                                                  scalar=pair_mask[:, h:h + 1],
                                                  in1=qm_s[:, buf, 0, h, :].bitcast(F32), op0=ALU.mult,
                                                  op1=ALU.subtract)
                last.then_inc(q_split, 1)

            def split_weights():
                dve.wait_ge(weights_high, 1)
                natural = "c (p h t d) -> c p t h d"
                for wide, nat in ((wk_s, wkv_nat[:, 0:INNER]), (wq_s, wq_nat)):
                    for t in range(2):
                        view = [wide[:, k, :].rearrange("c (p t h d) -> c p t h d", t=2, h=2, d=HALF)[:, :, t]
                                for k in range(2)]
                        w.tensor_tensor(view[1], nat.rearrange(natural, h=2, t=2, d=HALF)[:, :, t],
                                        view[0].bitcast(F32), ALU.subtract)
                w.tensor_tensor(wv_s[:, 1, :], wkv_nat[:, INNER:2 * INNER], wv_s[:, 0, :].bitcast(F32),
                                ALU.subtract).then_inc(weights_split, 1)

            for slot in range(SLOTS):
                if slot == S_SCORE[0]:
                    dve.wait_ge(bias_in, 16)
                    w.memset(prob1[:, :, 0:WINDOW], 0.0)
                if slot == S_RELU:
                    dve.wait_ge(weights_in, 16 * SETUP_LOADS)
                if slot == S_SUMS:
                    split_weights()
                self_attention(0, slot, 0)
            assert chain.k - first == SELF_DVE_LINKS, chain.k - first
            keys_sin(1, 1)
            queries_low(4, 0)
            keys_low(1, 0)
            keys_sin(5, 2)
            first = chain.k
            def batch(b, last=False):
                chain.start(first + b * DVE_LINKS)
                norms = n(b, NORMS, SELF_NORMS)

                def attended(p):
                    bank = pair_bank(p)
                    dve.wait_ge(o_full, n(b, PAIRS, p + 1))
                    if p >= 1:
                        dve.wait_ge(on_ready, n(b, PAIRS, p))
                    link(w.reciprocal(o_rec[:, :], bank[:, T:2 * T]))
                    w.tensor_tensor(on[:, p, :], bank[:, 0:T], o_rec[:, :], ALU.mult).then_inc(on_ready, 1)

                for p in range(PAIRS):
                    def clamp(hf):
                        dve.wait_ge(exp_done, n(b, UNITS, KB * p + 2 * hf + 2))
                        pr = prob[:, p % 2, 2 * hf:2 * hf + 2, :]
                        w.tensor_scalar(pr, pr, float(np.exp(-CLIP)), float(np.exp(CLIP)), ALU.max,
                                        ALU.min).then_inc(clamped, 1)

                    def slots(lo, hi):
                        for i in range(lo, hi if not last else lo):
                            self_attention(b + 1, PER_PAIR * p + i, norms)

                    def prep(make, kind, *args):
                        make(n(b, PREP_JOBS, FIRST_PREP + PREP.index((p, kind)) + 1), *args)

                    slots(0, 1)
                    clamp(0)
                    slots(1, 2)
                    slots(2, 3)
                    slots(3, 4)
                    if p < PAIRS - 1:
                        prep(queries_low, "queries", (p + 1) % 2)
                    if p < PAIRS - 1 or not last:
                        keys_low(n(b, PAIRS, p + 2), (p + 1) % 2)
                    clamp(1)
                    if p + 2 < PAIRS or not last:
                        prep(keys_sin, "keys", n(b, PAIRS, p + 3))
                    slots(4, 5)
                    slots(5, 6)
                    if p >= 1:
                        attended(p - 1)
                attended(PAIRS - 1)
                if not last:
                    prep(queries_low, "queries", 0)
                x2_b = x2[:, bass.ds(b * QT, QT), :]
                dve.wait_ge(x1p_ready, n(b, 1, 1))
                dve.wait_ge(y_full, n(b, 1, 1))
                w.tensor_tensor(y[:, :, :], ob[:, 0:QT * D].rearrange("p (q d) -> p q d", q=QT), x2_b,
                                ALU.add).then_inc(y_free, 1)
                dve.wait_ge(y_free, n(b, 1, 2))
                statistics(norms, SELF_NORMS if not last else 0, tiles_of(y, QT))
                if not last:
                    dve.wait_ge(x1p_ready, n(b, 1, 2))
                link(normalize(tiles_of(x1, QT), tiles_of(y, QT)))
                settle()
                w.tensor_copy(x2_b, x1[:, :, :]).then_inc(x2_ready, 1)
                assert chain.k == (LAST_DVE_LINKS if last else DVE_LINKS), chain.k

            with dve.Fori(0, B - 1) as b:
                batch(b)
            batch(B - 1, last=True)
            base = first + (B - 1) * DVE_LINKS + LAST_DVE_LINKS
            chain.start(base)

            def cell(k, m=1):
                return small[:, k:k + m]

            dve.wait_ge(y_full, B)
            dve.wait_ge(x2_ready, B)
            base_norms = B * NORMS

            def f_tiles(t, k):
                return tiles_of(t[:, 4 * k:4 * k + 4, :], 4)

            def normalize_f(k):
                dve.wait_ge(rstd_ready, base_norms + k + 1)
                normalize(f_tiles(f_all, k), f_tiles(x2, k), k % 2).then_inc(f_ready, 1)
                dve.wait_ge(f_ready, k + 1)

            in_turns(4, lambda k: measure(f_tiles(x2, k), k % 2), normalize_f)
            dve.wait_ge(mats_in, 16 * 8)
            w.tensor_reduce(cell(F_SUM), mats[:, M_FFN0, :], AX_X, ALU.add,
                            apply_absolute_value=True).then_inc(red_ready, 1)
            dve.wait_ge(td_full, 1)
            w.tensor_scalar(cell(BETA), bank_d[:, 0:1], 1.0 / (D * D), None, ALU.mult).then_inc(td_free, 1)
            dve.wait_ge(td_free, 1)
            link(w.tensor_scalar(cell(INV_BETA), cell(BETA), 1e-5, None, ALU.add))
            link(w.reciprocal(cell(INV_BETA), cell(INV_BETA)))
            link(w.tensor_scalar(w_round, mats[:, M_FFN0, :], cell(INV_BETA), ROUND, ALU.mult, ALU.add))
            link(w.tensor_scalar(w_round, w_round, ROUND, None, ALU.subtract))
            w.tensor_scalar(w_round, w_round, -1.0, 1.0, ALU.max, ALU.min).then_inc(prep_ready, 1)
            dve.wait_ge(td_full, 2)
            w.tensor_copy(tail[:, 3:6, :].rearrange("p k d -> p (k d)"), bank_d[:, 0:3 * D])
            w.tensor_copy(c_rows[:, 0:D], bank_d[0:1, 3 * D:4 * D]).then_inc(td_free, 1)
            dve.wait_ge(td_full, 3)
            w.tensor_tensor(gws_t, bank_d[:, 0:D], ident[:, :], ALU.add)
            w.tensor_copy(c_rows[:, D:2 * D], bank_d[0:1, D:2 * D])
            w.tensor_tensor(cell(OUT_BIAS), bank_d[:, 2 * D:2 * D + 1], cols[:, BO_COL:BO_COL + 1],
                            ALU.add).then_inc(td_free, 1)
            for k in range(4):
                dve.wait_ge(ta_free, 2 + k)
                last = w.tensor_reduce(cell(F_MAX + k), f_t[:, 512 * k:512 * k + 512], AX_X, ALU.max,
                                       apply_absolute_value=True)
            link(last)
            w.tensor_reduce(cell(Q_MAX), cell(F_MAX, 4), AX_X, ALU.max).then_inc(red_ready, 1)
            dve.wait_ge(td_full, 4)
            w.tensor_reduce(diag2[0:1, 0:1], bank_d[0:1, 0:P], AX_X, ALU.max).then_inc(td_free, 1)
            dve.wait_ge(td_full, 5)
            w.tensor_copy(cell(F_ALL), bank_d[:, 0:1]).then_inc(td_free, 1)
            dve.wait_ge(td_free, 5)
            w.tensor_scalar(cell(F_SCALE), cell(F_ALL), cell(BETA), 1.0 / QB, ALU.mult, ALU.mult)
            link(w.reciprocal(cell(F_INV), cell(F_ALL)))
            for k in range(4):
                part = f_t[:, 512 * k:512 * k + 512]
                link(w.tensor_scalar(part, part, QB, cell(F_INV), ALU.mult, ALU.mult))
                limit = float(np.float32(QB - 1e-5))
                w.tensor_scalar(part, part, -limit, limit, ALU.max, ALU.min).then_inc(f_quantized, 1)
            pre3 = (t4, k_raw[:, :].rearrange("p (t d) -> p t d", d=D))

            def add_product(k):
                dve.wait_ge(td_full, 6 + k)
                w.scalar_tensor_tensor(out=pre3[k % 2], in0=bank_d[:, :].rearrange("p (t d) -> p t d", d=D),
                                       scalar=cell(F_SCALE), in1=x2[:, 4 * k:4 * k + 4, :], op0=ALU.mult,
                                       op1=ALU.add).then_inc(td_free, 1)
                dve.wait_ge(td_free, 6 + k)
                measure(tiles_of(pre3[k % 2], 4), k % 2)

            def normalize_x3(k):
                if k >= 1:
                    dve.wait_ge(ta_full, 5 + k)
                dve.wait_ge(rstd_ready, base_norms + 4 + k + 1)
                normalize(tiles_of(t4b, 4), tiles_of(pre3[k % 2], 4), k % 2).then_inc(x3_ready, 1)
                dve.wait_ge(x3_ready, k + 1)

            in_turns(4, add_product, normalize_x3)
            base += chain.k

            def affine(t, count):
                for row, op in ((l1_g, ALU.mult), (l1_b, ALU.add)):
                    link(w.tensor_tensor(t, t, row[:, :].unsqueeze(1).broadcast_to([P, count, D]), op))

            hm = head_mask[:, :].unsqueeze(1).unsqueeze(3).broadcast_to([P, B, H, HD])
            w.tensor_tensor(ksm.rearrange("p b (h d) -> p b h d", d=HD),
                            kv_sums[:, 0:B, D].unsqueeze(2).unsqueeze(3).broadcast_to([P, B, H, HD]), hm, ALU.mult)
            w.tensor_tensor(kvm.rearrange("p b (h d) -> p b h d", d=HD),
                            kv_sums[:, 0:B, 0:D].rearrange("p b (h d) -> p b h d", d=HD), hm,
                            ALU.mult).then_inc(kvm_ready, 1)
            with dve.Fori(0, B) as b:
                chain.start(base + b * EARLY_DVE_LINKS)
                late = n(b, EARLY_NORMS, B * NORMS + 8)
                job = 10 + b * EARLY_D
                dve.wait_ge(td_full, job)
                pre = [bank_d[:, 0:P]]
                statistics(late, 0, pre)
                normalize(tiles_of(x4, 1), pre).then_inc(td_free, 1)
                dve.wait_ge(td_full, job + 1)
                statistics(late, 1, pre)
                normalize(tiles_of(q1, 1), pre).then_inc(td_free, 1)
                dve.wait_ge(td_free, job + 1)
                affine(q1[:, 0:1, :], 1)
                w.tensor_scalar(q1[:, 0, :], q1[:, 0, :], 0.0, 1e-6, ALU.max, ALU.add).then_inc(q1_ready, 1)
                dve.wait_ge(td_full, job + 2)
                link(w.tensor_scalar(den[:, 0:P], bank_d[:, P:2 * P], 1e-6, None, ALU.add))
                link(w.reciprocal(den[:, 0:P], den[:, 0:P]))
                w.tensor_tensor(att[:, bass.ds(b * QT, 1), :].rearrange("p q d -> p (q d)"), bank_d[:, 0:P],
                                den[:, 0:P], ALU.mult).then_inc(att_ready, 1)
                dve.wait_ge(att_ready, b + 1)
                w.tensor_copy(x4_all[:, bass.ds(b * QT, 1), :], x4[:, 0:1, :]).then_inc(td_free, 1)
                assert chain.k == EARLY_DVE_LINKS, chain.k
            chain.start(base + B * EARLY_DVE_LINKS)
            job = 10 + B * EARLY_D
            late = B * NORMS + 8 + B * EARLY_NORMS
            groups = [(g, slice(g * B // LATE_GROUPS, (g + 1) * B // LATE_GROUPS),
                       (bank_d, bank_d2)[g][:, :].rearrange("p (t d) -> p t d", d=D), (t4, t4b)[g])
                      for g in range(LATE_GROUPS)]
            for g, of_group, bank, _ in groups:
                dve.wait_ge(td_full, job + g)
                measure(tiles_of(bank, 4), g)
            for g, of_group, bank, _ in groups:
                dve.wait_ge(rstd_ready, late + g + 1)
                normalize(tiles_of(x4_by_batch[:, of_group, 1, :], 4), tiles_of(bank, 4), g).then_inc(td_free, 1)
                dve.wait_ge(td_free, job + g)
            for g, _, bank, q in groups:
                dve.wait_ge(td_full, job + 2 + g)
                measure(tiles_of(bank, 4), g)
            for g, _, bank, q in groups:
                dve.wait_ge(rstd_ready, late + LATE_GROUPS + g + 1)
                normalize(tiles_of(q, 4), tiles_of(bank, 4), g).then_inc(td_free, 1)
                dve.wait_ge(td_free, job + 2 + g)
                affine(q, 4)
                w.tensor_scalar(q, q, 0.0, 1e-6, ALU.max, ALU.add).then_inc(q1_ready, 1)
            for g, of_group, _, _ in groups:
                dve.wait_ge(td_full, job + 4 + g)
                by_sum = (k_raw, k_sin)[g][:, :]
                link(w.tensor_scalar(by_sum, sc[:, 2 * g + 1, :], 1e-6, None, ALU.add))
                link(w.reciprocal(by_sum, by_sum))
                w.tensor_tensor(att_by_batch[:, of_group, 1, :], sc[:, 2 * g, :].rearrange("p (t d) -> p t d", d=D),
                                by_sum.rearrange("p (t d) -> p t d", d=D), ALU.mult).then_inc(td_free, 1)
            job += 3 * LATE_GROUPS
            late += 2 * LATE_GROUPS
            def dense(k):
                t = (t4, t4b)[k % 2]
                dve.wait_ge(td_full, job + k)
                w.tensor_tensor(t, bank_d[:, :].rearrange("p (t d) -> p t d", d=D),
                                b_dense[:, :].unsqueeze(1).broadcast_to([P, 4, D]), ALU.add).then_inc(td_free, 1)
                dve.wait_ge(td_free, job + k)
                measure(tiles_of(t, 4), k % 2)

            def residual(k):
                t = (t4, t4b)[k % 2]
                dve.wait_ge(rstd_ready, late + 4 * (k // 2) + k % 2 + 1)
                link(normalize(tiles_of(t, 4), tiles_of(t, 4), k % 2))
                affine(t, 4)
                link(w.tensor_tensor(t, t, x4_all[:, 4 * k:4 * k + 4, :], ALU.add))
                measure(tiles_of(t, 4), k % 2)

            def normalize_x5(k):
                t = (t4, t4b)[k % 2]
                dve.wait_ge(rstd_ready, late + 4 * (k // 2) + 2 + k % 2 + 1)
                normalize([x5[:, 4 * k + i, :] for i in range(4)], tiles_of(t, 4), k % 2).then_inc(x2_ready, 1)
                dve.wait_ge(x2_ready, B + k + 1)

            for step, k in ((dense, 0), (dense, 1), (residual, 0), (residual, 1), (normalize_x5, 0), (dense, 2),
                            (normalize_x5, 1), (dense, 3), (residual, 2), (residual, 3), (normalize_x5, 2),
                            (normalize_x5, 3)):
                step(k)
            job += 4
            late += 8
            w.tensor_reduce(cell(Q_MAX + 1), mats[:, M_FFN1, :], AX_X, ALU.max, apply_absolute_value=True)
            w.tensor_reduce(cell(Q_MAX), x5[:, :, :], mybir.AxisListType.XY, ALU.max,
                            apply_absolute_value=True).then_inc(red_ready, 1)
            dve.wait_ge(td_full, job)
            w.tensor_reduce(diag2[0:2, 2:3], bank_d[0:2, 0:P], AX_X, ALU.max).then_inc(td_free, 1)
            dve.wait_ge(td_free, job)
            w.tensor_scalar(diag2[0:2, 0:2], ident[0:2, 0:2], diag2[0:2, 2:3], None, ALU.mult).then_inc(red_ready, 1)
            dve.wait_ge(td_full, job + 1)
            w.tensor_scalar(cell(Q_SCALE, 2), bank_d[:, 0:2], 1e-12, None, ALU.max).then_inc(td_free, 1)
            dve.wait_ge(td_free, job + 1)
            link(w.reciprocal(cell(Q_SCALE, 2), cell(Q_SCALE, 2)))
            link(w.tensor_scalar(cell(Q_SCALE, 2), cell(Q_SCALE, 2), FP8_MAX, None, ALU.mult))
            link(w.tensor_tensor(cell(Q_INV), cell(Q_SCALE), cell(Q_SCALE + 1), ALU.mult))
            link(w.reciprocal(cell(Q_INV), cell(Q_INV)))

            def round8(dst, src, lev, scale):
                link(w.tensor_scalar(src, src, scale, None, ALU.mult))
                link(w.tensor_scalar(lev.bitcast(U32), src.bitcast(U32), 0x7F800000, None, ALU.bitwise_and))
                link(w.tensor_scalar(lev, lev, FP8_MIN_NORMAL, FP8_ROUND, ALU.max, ALU.mult))
                link(w.tensor_tensor(src, src, lev, ALU.add))
                return w.tensor_tensor(dst, src, lev, ALU.subtract)

            round8(w8[:, 0, :], mats[:, M_FFN1, :], w_round, cell(Q_SCALE + 1)).then_inc(q8_ready, 1)
            dve.wait_ge(x5b_ready, 1)
            for k in range(4):
                part = x5[:, 4 * k:4 * k + 4, :]
                round8(q8[:, 4 * k:4 * k + 4, :], part, level[:, 4 * k:4 * k + 4, :],
                       cell(Q_SCALE)).then_inc(q8_ready, 1)
            dve.wait_ge(td_full, job + 2)
            w.tensor_copy(w8[:, 1, :], bank_d[:, 0:64].bitcast(BF16)).then_inc(td_free, 1)
            dve.wait_ge(q8_ready, 5)
            def residual_tiles(k):
                return x2[:, 4 * k:4 * k + 4, :]

            def add_last(k):
                dve.wait_ge(td_full, job + 3 + k)
                res = residual_tiles(k)
                w.scalar_tensor_tensor(out=res, in0=bank_d[:, :].rearrange("p (t d) -> p t d", d=D),
                                       scalar=cell(Q_INV), in1=res, op0=ALU.mult, op1=ALU.add).then_inc(td_free, 1)
                dve.wait_ge(td_free, job + 3 + k)
                measure(tiles_of(res, 4), k % 2)

            def normalize_last(k):
                dve.wait_ge(rstd_ready, late + k + 1)
                normalize(f_tiles(f_all, k), tiles_of(residual_tiles(k), 4), k % 2).then_inc(out_ready, 1)
                dve.wait_ge(out_ready, k + 1)

            in_turns(4, add_last, normalize_last)

        @block.tensor
        def _(pe):
            mm = nc.tensor.matmul

            def turn(out_ap, in_ap):
                return nc.tensor.transpose(out_ap, in_ap, ident[0:in_ap.shape[0], 0:in_ap.shape[0]])

            pe.wait_ge(first_in, 16 * FIRST_LOADS)
            pe.wait_ge(consts_made, 1)
            for k in range(4):
                last = turn(bank_d[:, k * P:(k + 1) * P], w_nat[:, k, :])
            last.then_inc(d_full, 1)
            pe.wait_ge(d_free, 1)
            pe.wait_ge(trig_ready, 1)
            turn(bank_d[0:H, 0:WINDOW + 1], rel).then_inc(d_full, 1)
            pe.wait_ge(d_free, 2)
            for t, bank in ((0, bank_d), (1, bank_a)):
                for k in range(KB):
                    last = turn(bank[:, k * P:(k + 1) * P], trig_rep[:, t, k].rearrange("p r d -> p (r d)"))
                last.then_inc(d_full if t == 0 else a_full, 1)

            def split_mm(out_ap, a_high, a_low, b_high, b_low, **kw):
                mm(out_ap, a_high, b_low, start=True, stop=False, **kw)
                mm(out_ap, a_low, b_high, start=False, stop=False, **kw)
                return mm(out_ap, a_high, b_high, start=False, stop=True, **kw)

            jobs = []
            for half in range(2):
                two = (2 * half, 2 * half + 1)
                jobs += [[(0, j, 0, g) for g in range(G)] for j in two]
                jobs += [[(1, j, kt, 2 * m + g) for kt in range(QT) for g in range(2)] for j in two for m in range(2)]

            def self_attention(b, slot):
                def a_job(job):
                    pe.wait_ge(a_free, n(b, ACT_JOBS, SETUP_A + job))

                def d_job(job):
                    pe.wait_ge(d_free, n(b, DVE_JOBS, SETUP_D + job - 1))
                    return d_bank(job)

                def weigh_values(t):
                    a_job(A_TURN + t + 1)
                    for i, (qt, j, kt, g) in enumerate(jobs[t]):
                        last = mm(o0_bank[32 * g:32 * g + 32, qt * P:(qt + 1) * P], vm[:, kt, j, 32 * g:32 * g + 32],
                                  pt[:, t % 4, i * P:(i + 1) * P], start=(j == 0 and kt == 0 and qt == 0),
                                  stop=(j == G - 1 and (qt == 0 or kt == QT - 1)), skip_group_check=True)
                    return last

                if slot == S_X:
                    pe.wait_ge(x_in, n(b, 16, 16))
                    a_job(0)
                    for t in range(QT):
                        last = turn(bank_a[:, t * P:(t + 1) * P], xb[:, t, :])
                    last.then_inc(a_full, 1)
                if slot == S_CTX:
                    pe.wait_ge(ctx_in, n(b, 16, 16))
                    a_job(A_CTX)
                    for k in range(KB):
                        last = turn(bank_a[:, k * P:(k + 1) * P], cb[:, k, :])
                    last.then_inc(a_full, 1)
                if slot == S_K:
                    a_job(A_K)
                    mm(bank_a[:, 0:T], w_qkv_t[:, D:2 * D], x_t[:, :], start=True, stop=True).then_inc(a_full, 1)
                if slot == S_Q:
                    bank = d_job(0)
                    mm(bank[:, 0:T], w_qkv_t[:, 0:D], x_t[:, :], start=True, stop=True).then_inc(d_full, 1)
                if slot == S_V:
                    bank = d_job(1)
                    for t in range(QT):
                        last = mm(bank[:, t * D:(t + 1) * D], x_t[:, t * P:(t + 1) * P], w_qkv_t[:, 2 * D:3 * D],
                                  start=True, stop=True, skip_group_check=True)
                    last.then_inc(d_full, 1)
                if slot in (S_KV_A, S_KV_B):
                    j = slot - S_KV_A
                    a_job(A_KV + j)
                    for k in range(2):
                        kb = 2 * j + k
                        last = mm(bank_a[:, 2 * k * D:2 * (k + 1) * D], ctx_t[:, kb * P:(kb + 1) * P], w_l1kv[:, :],
                                  start=True, stop=True, skip_group_check=True)
                    last.then_inc(a_full, 1)
                if slot in S_SCORE:
                    at = S_SCORE.index(slot)
                    j, i = divmod(at, 3)
                    if i == 0:
                        pe.wait_ge(km_ready, n(b, G, j + 1))
                    bank = d_job(D_SCORE + at)
                    if i == 0:
                        last = mm(bank[:, 0:4 * P], q0[:, 0:P], km[:, j % 2, :, 0:P], start=True, stop=True)
                    else:
                        g = 2 * (i - 1)
                        last = mm(bank[:, 0:2 * BAND], q0[:, P:T], km[:, j % 2, g:g + 2, T - BAND:T],
                                  start=True, stop=True)
                    last.then_inc(d_full, 1)
                at = slot - S_TURN
                if 0 <= at < TURNS:
                    if at % 6 == 0:
                        pe.wait_ge(exp0_done, n(b, 2, at // 6 + 1))
                    a_job(A_TURN + at)
                    for i, (qt, j, kt, g) in enumerate(jobs[at]):
                        h = 4 * g + j
                        src = prob0[:, h, :] if qt == 0 else prob1[:, h, kt * P:(kt + 1) * P]
                        last = turn(bank_a[:, i * P:(i + 1) * P], src)
                    last.then_inc(a_full, 1)
                if 1 <= at <= TURNS:
                    last = weigh_values(at - 1)
                    if at == TURNS:
                        last.then_inc(o0_full, 1)
                if slot == S_REC:
                    pe.wait_ge(rec0_ready, n(b, 1, 1))
                    a_job(A_REC)
                    for qt in range(QT):
                        last = turn(bank_a[:, qt * P:(qt + 1) * P], row_rec[:, qt].rearrange("p h d -> p (h d)"))
                    last.then_inc(a_full, 1)
                if slot == S_PROJ:
                    pe.wait_ge(o0_ready, n(b, 1, 1))
                    bank = d_job(D_PROJ)
                    for qt in range(QT):
                        last = mm(bank[:, qt * D:(qt + 1) * D], o0[:, qt * P:(qt + 1) * P], w_proj_t[:, :],
                                  start=True, stop=True, skip_group_check=True)
                    last.then_inc(d_full, 1)
                if slot == S_KV:
                    bank = d_job(D_KV)
                    pe.wait_ge(k1_ready, n(b, 1, 1))
                    for kb in range(KB):
                        last = mm(bank[:, 0:D + 1], k1[:, kb, :], v1[:, kb, :], start=(kb == 0), stop=(kb == KB - 1))
                    last.then_inc(d_full, 1)
                if slot == S_LAT:
                    a_job(A_LAT)
                    pe.wait_ge(lat_ready, n(b, 1, 1))
                    for qt in range(QT):
                        last = turn(bank_a[:, qt * P:(qt + 1) * P], lat[:, qt, :])
                    last.then_inc(a_full, 1)
                if slot == S_CN:
                    a_job(A_CN)
                    pe.wait_ge(cn_ready, n(b, 1, 1))
                    for k in range(KB):
                        last = turn(bank_a[:, k * P:(k + 1) * P], cn[:, k, :])
                    last.then_inc(a_full, 1)

            def prep_keys(done, p, after=True):
                if after:
                    pe.wait_ge(p_free, done)
                c = slice(p * P, (p + 1) * P)
                split_mm(bank_p, wk_s[:, 0, c], wk_s[:, 1, c], cn_s[:, 0, :], cn_s[:, 1, :]).then_inc(p_full, 1)

            def prep_values(done, group, half):
                pe.wait_ge(p_free, done)
                c = slice(group * 2 * P, (group + 1) * 2 * P)
                for k in range(2):
                    kb = slice((2 * half + k) * P, (2 * half + k + 1) * P)
                    last = split_mm(bank_p[:, k * 2 * P:(k + 1) * 2 * P], cn_s[:, 0, kb], cn_s[:, 1, kb],
                                    wv_s[:, 0, c], wv_s[:, 1, c], skip_group_check=True)
                last.then_inc(p_full, 1)

            def prep_queries(done, p):
                pe.wait_ge(p_free, done)
                c = slice(p * P, (p + 1) * P)
                split_mm(bank_p[:, 0:T], wq_s[:, 0, c], wq_s[:, 1, c], lat_s[:, 0, :],
                         lat_s[:, 1, :]).then_inc(p_full, 1)

            for slot in range(SLOTS):
                self_attention(0, slot)
            pe.wait_ge(weights_in, 16 * SETUP_LOADS)
            pe.wait_ge(weights_split, 1)
            pe.wait_ge(cn_split, 1)
            prep_keys(0, 0, after=False)
            for half in range(2):
                prep_values(1 + half, 0, half)
            pe.wait_ge(lat_split, 1)
            prep_queries(3, 0)
            prep_keys(4, 1)
            def batch(b, last=False):
                for p in range(PAIRS):
                    def unit(kb):
                        i = KB * p + kb
                        if kb == 0:
                            pe.wait_ge(kr_ready, n(b, PAIRS, p + 1))
                            pe.wait_ge(q_split, n(b, PAIRS, p + 1))
                        if i >= 2:
                            pe.wait_ge(exp_done, n(b, UNITS, i - 1))
                        c = slice(kb * P, (kb + 1) * P)
                        split_mm(sc[:, kb % 2, :], kr_s[:, p % 2, 0, c], kr_s[:, p % 2, 1, c], qm_s[:, p % 2, 0],
                                 qm_s[:, p % 2, 1]).then_inc(unit_full, 1)

                    def values_of(q, kbs):
                        o = pair_bank(q)
                        if kbs[0] == 0:
                            if q == 0:
                                pe.wait_ge(y_free, n(b, 1, 1))
                            elif q < PAIRS - 1:
                                pe.wait_ge(on_ready, n(b, PAIRS, q))
                        pe.wait_ge(clamped, n(b, HALVES, 2 * q + kbs[-1] // 2 + 1))
                        for kb in kbs:
                            for h in range(2):
                                lo = P * (q % 2) + DH * h
                                mm(o[DH * h:DH * (h + 1), 0:T], v[:, (q // 2) % 2, kb, lo:lo + DH],
                                   prob[:, q % 2, kb, T * h:T * (h + 1)], start=(kb == 0), stop=(kb == KB - 1),
                                   skip_group_check=True)

                    def sum_of(q):
                        pe.wait_ge(psum_ready, n(b, PAIRS, q + 1))
                        for h in range(2):
                            last = mm(pair_bank(q)[DH * h:DH * (h + 1), T:2 * T], ones[:, 0:DH],
                                      psum[:, q % 2, T * h:T * (h + 1)], start=True, stop=True, skip_group_check=True)
                        last.then_inc(o_full, 1)

                    def slots(lo, hi):
                        for i in range(lo, hi if not last else lo):
                            self_attention(b + 1, PER_PAIR * p + i)

                    def prep(make, kind, *args):
                        make(n(b, PREP_JOBS, FIRST_PREP + PREP.index((p, kind))), *args)

                    def next_values(half):
                        if p % 2 == 1:
                            prep(prep_values, f"values {half}", (p + 1) % PAIRS // 2, half)

                    last_pair = p == PAIRS - 1
                    unit(0)
                    slots(0, 1)
                    unit(1)
                    slots(1, 2)
                    if not last_pair:
                        next_values(0)
                    unit(2)
                    if not last_pair:
                        next_values(1)
                    slots(2, 3)
                    if not last_pair:
                        prep(prep_queries, "queries", p + 1)
                    slots(3, 4)
                    unit(3)
                    if p == PAIRS - 2 and not last:
                        pe.wait_ge(cn_split, n(b, 1, 2))
                    if p + 2 < PAIRS or not last:
                        prep(prep_keys, "keys", (p + 2) % PAIRS)
                    if p >= 1:
                        values_of(p - 1, (0, 1))
                    slots(4, 5)
                    if p >= 1:
                        values_of(p - 1, (2, 3))
                        sum_of(p - 1)
                    slots(5, 6)
                values_of(PAIRS - 1, (0, 1))
                if not last:
                    next_values(0)
                values_of(PAIRS - 1, (2, 3))
                if not last:
                    next_values(1)
                sum_of(PAIRS - 1)
                if not last:
                    pe.wait_ge(lat_split, n(b, 1, 2))
                    prep(prep_queries, "queries", 0)
                pe.wait_ge(on_ready, n(b, PAIRS, PAIRS - 1))
                for p in range(PAIRS):
                    if p == PAIRS - 1:
                        pe.wait_ge(on_ready, n(b, PAIRS, PAIRS))
                    for qt in range(QT):
                        product = mm(ob[:, qt * D:(qt + 1) * D], on[:, p, qt * P:(qt + 1) * P], wo[:, p, :],
                                  start=(p == 0 and qt == 0), stop=(p == PAIRS - 1), skip_group_check=True)
                product.then_inc(y_full, 1)

            with pe.Fori(0, B - 1) as b:
                batch(b)
            batch(B - 1, last=True)

            pe.wait_ge(a_free, SETUP_A + B * ACT_JOBS)
            pe.wait_ge(mats_in, 16 * 8)
            for k, m in enumerate((M_A, M_B, M_WO)):
                last = turn(bank_a[:, k * P:(k + 1) * P], mats[:, m, :])
            last.then_inc(ta_full, 1)
            pe.wait_ge(d_free, SETUP_D + B * DVE_JOBS)
            pe.wait_ge(p_free, FIRST_PREP + (B - 1) * PREP_JOBS + LAST_PREPS)
            for k in range(4):
                pe.wait_ge(f_ready, k + 1)
                pe.wait_ge(ta_free, 1 + k)
                for i in range(4):
                    last = turn(bank_a[:, i * P:(i + 1) * P], f_all[:, 4 * k + i, :])
                last.then_inc(ta_full, 1)
            pe.wait_ge(red_ready, 1)
            mm(bank_d[:, 0:1], ones[:, :], small[:, F_SUM:F_SUM + 1], start=True, stop=True).then_inc(td_full, 1)
            pe.wait_ge(td_free, 1)
            mm(bank_d[:, 0:D], mats[:, M_WI, :], b_t, start=True, stop=True, skip_group_check=True)
            mm(bank_d[:, D:2 * D], mats[:, M_WS, :], a_t, start=True, stop=True, skip_group_check=True)
            mm(bank_d[:, 2 * D:3 * D], mats[:, M_C, :], wo_t, start=True, stop=True, skip_group_check=True)
            mm(bank_d[0:1, 3 * D:4 * D], cols[:, BI_COL:BI_COL + 1], b_t, start=True, stop=True,
               skip_group_check=True).then_inc(td_full, 1)
            pe.wait_ge(td_free, 2)
            mm(bank_d[:, 0:D], mats[:, M_WS, :], g_t, start=True, stop=True, skip_group_check=True)
            mm(bank_d[0:1, D:2 * D], cols[:, BI_COL:BI_COL + 1], b_t, start=True, stop=False, skip_group_check=True)
            mm(bank_d[0:1, D:2 * D], cols[:, BS_COL:BS_COL + 1], a_t, start=False, stop=True, skip_group_check=True)
            mm(bank_d[:, 2 * D:2 * D + 1], g_t, cols[:, BS_COL:BS_COL + 1], start=True, stop=True,
               skip_group_check=True).then_inc(td_full, 1)
            pe.wait_ge(td_free, 3)
            pe.wait_ge(red_ready, 2)
            turn(bank_d[0:1, 0:P], small[:, Q_MAX:Q_MAX + 1]).then_inc(td_full, 1)
            pe.wait_ge(td_free, 4)
            mm(bank_d[:, 0:1], ones[0:1, :], diag2[0:1, 0:1], start=True, stop=True).then_inc(td_full, 1)

            def keep_clock():
                mm(bank_d2[:, 0:2 * P], ident[:, :], w_qkv_t[:, 0:2 * P], start=True, stop=True,
                   skip_group_check=True)

            def turn_x3(k):
                pe.wait_ge(x3_ready, k + 1)
                pe.wait_ge(ta_free, 5 + k)
                for i in range(4):
                    last = turn(bank_a[:, i * P:(i + 1) * P], t4b[:, i, :])
                last.then_inc(ta_full, 1)

            pe.wait_ge(prep_ready, 1)
            for k in range(4):
                pe.wait_ge(td_free, 5 + k)
                pe.wait_ge(f_quantized, k + 1)
                for i in range(4):
                    t = 4 * k + i
                    last = mm(bank_d[:, i * D:(i + 1) * D], f_t[:, t * P:(t + 1) * P], w_round, start=True, stop=True,
                              skip_group_check=True)
                last.then_inc(td_full, 1)
                if k >= 1:
                    turn_x3(k - 1)
            for _ in range(8):
                keep_clock()
            turn_x3(3)
            pe.wait_ge(ta_free, 9)
            pe.wait_ge(ident16_ready, 2)
            def z_of(lo, hi, start):
                bank = cf[:, lo:hi]
                mm(bank, bwi_t, x3_t[:, lo:hi], start=start, stop=False, skip_group_check=True)
                skip = B if lo == 0 else 0
                mm(bank[:, skip:], aws_t, x3_t[:, lo + skip - B:hi - B], start=False, stop=False,
                   skip_group_check=True)
                last = mm(bank[:, skip:], c_rows[:, D:2 * D], one_row[:, skip:hi - lo], start=False, stop=True,
                          skip_group_check=True)
                if skip:
                    last = mm(bank[:, 0:B], c_rows[:, 0:D], one_row[:, 0:B], start=False, stop=True,
                              skip_group_check=True)
                return last

            z_of(0, 512, True).then_inc(c_ready, 1)
            z_of(512, 1024, True)
            hid_b = hid.rearrange("p (t b) -> p b t", b=B)
            x3_b = x3_t.rearrange("p (t b) -> p b t", b=B)

            def step(t):
                pe.wait_ge(h_ready, t)
                mm(cf[:, bass.ds(t * B, B)], a_t, hid[:, bass.ds((t - 1) * B, B)], start=False, stop=True,
                   skip_group_check=True).then_inc(z_ready, 1)

            for t in range(1, 1 + Z_STEPS):
                step(t)
                lo = 1024 + P * (t - 1)
                z_of(lo, lo + P, lo % 512 == 0)
            with pe.Fori(0, (P - 1 - Z_STEPS) // STEPS) as part:
                for i in range(STEPS):
                    step(part * STEPS + 1 + Z_STEPS + i)
                    keep_clock()
            with pe.Fori(0, B) as b:
                ja = 9 + b * EARLY_A
                jd = 9 + b * EARLY_D
                for i in range(LATE_STEPS):
                    step(b * LATE_STEPS + P + i)
                    keep_clock()
                    if i == 0:
                        pe.wait_ge(ta_free, ja)
                        mm(bank_a[:, 0:P], g_t, hid_b[:, b, 0:P], start=True, stop=False)
                        mm(bank_a[:, 0:P], gws_t, x3_b[:, b, 0:P], start=False, stop=True).then_inc(ta_full, 1)
                    if i == 2:
                        pe.wait_ge(ta_free, ja + 1)
                        pe.wait_ge(td_free, jd)
                        turn(bank_d[:, 0:P], pre_t).then_inc(td_full, 1)
                    if i == 6:
                        pe.wait_ge(td_free, jd + 1)
                        turn(bank_a[:, 0:P], x4[:, 0, :]).then_inc(ta_full, 1)
                    if i == 8:
                        pe.wait_ge(ta_free, ja + 2)
                        mm(bank_d[:, 0:P], x4_t, w_l1q[:, :], start=True, stop=True).then_inc(td_full, 1)
                    if i == 13:
                        pe.wait_ge(q1_ready, b + 1)
                        turn(bank_a[:, 0:P], q1[:, 0, :]).then_inc(ta_full, 1)
                    if i == 15:
                        pe.wait_ge(ta_free, ja + 3)
                        pe.wait_ge(td_free, jd + 2)
                        pe.wait_ge(kvm_ready, 1)
                        mm(bank_d[:, 0:P], q1_t, kvm[:, b, :], start=True, stop=True, skip_group_check=True)
                        mm(bank_d[:, P:2 * P], q1_t, ksm[:, b, :], start=True, stop=True,
                           skip_group_check=True).then_inc(td_full, 1)
            ja = 9 + B * EARLY_A
            jd = 9 + B * EARLY_D
            pe.wait_ge(h_ready, T)
            groups = [(g, range(g * B // LATE_GROUPS, (g + 1) * B // LATE_GROUPS), (bank_a, ob)[g],
                       (bank_d, bank_d2)[g], (t4, t4b)[g]) for g in range(LATE_GROUPS)]

            def turn_four(bank, tiles):
                for i, tile in enumerate(tiles):
                    last = turn(bank[:, i * P:(i + 1) * P], tile)
                return last

            pe.wait_ge(ta_free, ja)
            for g, of_group, bank, _, _ in groups:
                b4 = slice(of_group[0], of_group[-1] + 1)
                mm(bank[:, :], g_t, hid_b[:, b4, P:T], start=True, stop=False)
                mm(bank[:, :], gws_t, x3_b[:, b4, P:T], start=False, stop=True).then_inc(ta_full, 1)
            pe.wait_ge(td_free, jd)
            for g, _, _, bank, _ in groups:
                pe.wait_ge(ta_free, ja + 1 + g)
                turn_four(bank, [psum[:, g, i * P:(i + 1) * P] for i in range(4)]).then_inc(td_full, 1)
            for g, of_group, bank, _, _ in groups:
                pe.wait_ge(td_free, jd + 1 + g)
                turn_four(bank, [x4_by_batch[:, b, 1, :] for b in of_group]).then_inc(ta_full, 1)
            for g, _, _, bank, _ in groups:
                pe.wait_ge(ta_free, ja + 3 + g)
                for i in range(4):
                    last = mm(bank[:, i * P:(i + 1) * P], psum[:, g, i * P:(i + 1) * P], w_l1q[:, :], start=True,
                              stop=True, skip_group_check=True)
                last.then_inc(td_full, 1)
            for g, _, bank, _, q in groups:
                pe.wait_ge(q1_ready, B + 1 + g)
                turn_four(bank, [q[:, i, :] for i in range(4)]).then_inc(ta_full, 1)
            for g, of_group, _, _, _ in groups:
                pe.wait_ge(ta_free, ja + 5 + g)
                for i, b in enumerate(of_group):
                    tok = psum[:, g, i * P:(i + 1) * P]
                    mm(sc[:, 2 * g, i * P:(i + 1) * P], tok, kvm[:, b, :], start=True, stop=True,
                       skip_group_check=True)
                    last = mm(sc[:, 2 * g + 1, i * P:(i + 1) * P], tok, ksm[:, b, :], start=True, stop=True,
                              skip_group_check=True)
                last.then_inc(td_full, 1)
            ja += 3 * LATE_GROUPS
            jd += 3 * LATE_GROUPS
            for k in range(4):
                pe.wait_ge(mixed_in[k // 2], 16)
                pe.wait_ge(ta_free, ja + k)
                for i in range(4):
                    last = turn(bank_a[:, i * P:(i + 1) * P], mixed[:, 4 * k + i, :])
                last.then_inc(ta_full, 1)
                pe.wait_ge(ta_free, ja + k + 1)
                pe.wait_ge(td_free, jd + k)
                for i in range(4):
                    last = mm(bank_d[:, i * P:(i + 1) * P], att_t[:, i * P:(i + 1) * P], w_dense[:, :], start=True,
                              stop=True, skip_group_check=True)
                last.then_inc(td_full, 1)
            ja += 4
            jd += 4
            pe.wait_ge(td_free, jd)
            pe.wait_ge(red_ready, 3)
            turn(bank_d[0:2, 0:P], small[:, Q_MAX:Q_MAX + 2]).then_inc(td_full, 1)
            pe.wait_ge(td_free, jd + 1)
            pe.wait_ge(red_ready, 4)
            mm(bank_d[:, 0:2], ones[0:2, :], diag2[0:2, 0:2], start=True, stop=True).then_inc(td_full, 1)
            pe.wait_ge(q8_ready, 1)
            pe.wait_ge(td_free, jd + 2)
            nc.tensor.transpose(bank_d[:, 0:64].bitcast(BF16), w8[:, 0, :], ident16[:, :]).then_inc(td_full, 1)
            for k in range(4):
                pe.wait_ge(q8_ready, 2 + k)
                pe.wait_ge(ta_free, ja + k)
                for i in range(4):
                    last = nc.tensor.transpose(bank_a[:, 64 * i:64 * i + 64].bitcast(BF16), q8[:, 4 * k + i, :],
                                               ident16[:, :])
                last.then_inc(ta_full, 1)
                pe.wait_ge(ta_free, ja + k + 1)
                pe.wait_ge(td_free, jd + 3 + k)
                for i in range(4):
                    last = mm(bank_d[:, i * P:(i + 1) * P], q8_t[:, i * P:(i + 1) * P], w8[:, 1, :], start=True,
                              stop=True, skip_group_check=True)
                last.then_inc(td_full, 1)


_INS = [
    "x", "ctx_1024", "mask_BxS2_ff1", "L0_attn_w_qkv", "L0_attn_w_proj", "L0_attn_b_proj", "L0_attn_rel_bias",
    "L0_xattn_cos", "L0_xattn_sin", "L0_xattn_ln_lat_g", "L0_xattn_ln_lat_b", "L0_xattn_ln_ctx_g",
    "L0_xattn_ln_ctx_b", "L0_xattn_Wq", "L0_xattn_Wkv", "L0_xattn_Wo", "L0_xattn_bo", "L0_ffn_weight",
    "L0_ffn_ln_gamma", "L0_ffn_ln_beta", "L1_attn_Wi", "L1_attn_bi", "L1_attn_Ws", "L1_attn_bs", "L1_attn_Wo",
    "L1_attn_bo", "L1_attn_A", "L1_attn_B", "L1_attn_C", "L1_xattn_wq", "L1_xattn_wk", "L1_xattn_wv",
    "L1_xattn_ln_gamma", "L1_xattn_ln_beta", "L1_xattn_dense_w", "L1_xattn_dense_b", "L1_ffn_weight", "L1_ffn_bias",
]


def kernel(**inputs):
    import numpy as _np
    import concourse.bacc as _bacc
    from concourse import mybir as _mybir
    from concourse.bass_utils import run_bass_kernel_spmd as _run

    nc = _bacc.Bacc("TRN2", target_bir_lowering=False, num_devices=1)
    arrays, args = {}, {}
    for name in _INS:
        arr = _np.ascontiguousarray(inputs[name])
        arrays[f"in_{name}_dram"] = arr
        args[name] = nc.dram_tensor(f"in_{name}_dram", arr.shape, _mybir.dt.from_np(arr.dtype),
                                    kind="ExternalInput").ap()
    out = nc.dram_tensor("out_0_dram", (B, T, D), F32, kind="ExternalOutput").ap()
    decoder(nc, args, out)
    r = _run(nc, [arrays], core_ids=[0])
    return r.results[0]["out_0_dram"]
```
